# Optimizing a Trainium2 kernel written in Bass

```python
import numpy as np
import jax
import jax.numpy as jnp

def _softmax(x, axis=-1):
    return jax.nn.softmax(x, axis=axis)

def _gelu(x):
    return jax.nn.gelu(x, approximate=True)

def _silu(x):
    return jax.nn.silu(x)

def _sigmoid(x):
    return jax.nn.sigmoid(x)

def _layernorm(x, axis=-1, eps=1e-05):
    m = jnp.mean(x, axis=axis, keepdims=True)
    v = jnp.var(x, axis=axis, keepdims=True)
    return (x - m) / jnp.sqrt(v + eps)

def _scatter_add(tgt, idx, src, axis=0):
    return tgt.at[idx].add(src)

def _segment_sum(src, seg, n):
    return jax.ops.segment_sum(src, seg, n)
kernel_name = 'mk_seq_preln_d1_jaxref_r8_760494'

def setup_inputs(seed: int=0):
    np.random.seed(seed)
    _w = jnp.asarray

    def _L0_attn_setup():
        import jax, jax.numpy as jnp
        import numpy as np
        from jax import lax
        DIM = 256
        NK = 8
        NV = 16
        DK = 64
        DV = 64
        KCONV = 4
        KEY_DIM = NK * DK
        VAL_DIM = NV * DV
        CONV_DIM = 2 * KEY_DIM + VAL_DIM
        B = 1
        T = 256
        EPS = 1e-06

        def _l2norm(x, eps=1e-06):
            return x * lax.rsqrt(jnp.sum(x * x, -1, keepdims=True) + eps)

        def _gated_delta_rule(q, k, v, g, beta):

            def step(S, inp):
                q_t, k_t, v_t, g_t, b_t = inp
                S = S * jnp.exp(g_t)[..., None, None]
                pred = jnp.einsum('bhk,bhkv->bhv', k_t, S)
                delta = (v_t - pred) * b_t[..., None]
                S = S + k_t[..., None] * delta[..., None, :]
                o = jnp.einsum('bhk,bhkv->bhv', q_t, S)
                return (S, o)
            Bn, H, Tn, dk = q.shape
            dv = v.shape[-1]
            S0 = jnp.zeros((Bn, H, dk, dv), q.dtype)
            xs = (jnp.moveaxis(q, 2, 0), jnp.moveaxis(k, 2, 0), jnp.moveaxis(v, 2, 0), jnp.moveaxis(g, 2, 0), jnp.moveaxis(beta, 2, 0))
            _, out = lax.scan(step, S0, xs)
            return jnp.moveaxis(out, 0, 2)
        key = jax.random.key(seed)
        ks = jax.random.split(key, 8)
        s = 0.02
        return {'x': jax.random.normal(ks[0], (B, T, DIM), jnp.float32), 'W_qkv': jax.random.normal(ks[1], (CONV_DIM, DIM), jnp.float32) * s, 'W_z': jax.random.normal(ks[2], (VAL_DIM, DIM), jnp.float32) * s, 'W_b': jax.random.normal(ks[3], (NV, DIM), jnp.float32) * s, 'W_a': jax.random.normal(ks[4], (NV, DIM), jnp.float32) * s, 'W_out': jax.random.normal(ks[5], (DIM, VAL_DIM), jnp.float32) * s, 'conv_w': jax.random.normal(ks[6], (CONV_DIM, 1, KCONV), jnp.float32) * 0.5, 'dt_bias': jnp.ones((NV,), jnp.float32), 'A_log': jnp.log(jax.random.uniform(ks[7], (NV,), jnp.float32, 0.001, 16.0)), 'norm_weight': jnp.ones((DV,), jnp.float32)}
    _L0_attn_in = _L0_attn_setup()

    def _L0_ffn_setup():
        import jax, jax.numpy as jnp
        import numpy as np
        from jax import lax
        H = 256
        I = 128
        E = 32
        K = 4
        SH_I = 256
        EPS = 1e-06

        def _rmsnorm(x, w, eps=EPS):
            var = jnp.mean(jnp.square(x.astype(jnp.float32)), axis=-1, keepdims=True)
            return (x * lax.rsqrt(var + eps)).astype(x.dtype) * w
        key = jax.random.key(seed)
        ks = jax.random.split(key, 8)
        s = lambda d: 1.0 / np.sqrt(d)
        return {'x': jax.random.normal(ks[0], (2, 256, H), jnp.float32), 'norm_w': jnp.ones((H,), jnp.float32), 'router_w': jax.random.normal(ks[1], (E, H), jnp.float32) * s(H), 'w1': jax.random.normal(ks[2], (E, H, 2 * I), jnp.float32) * s(H), 'w2': jax.random.normal(ks[3], (E, I, H), jnp.float32) * s(I), 'sg': jax.random.normal(ks[4], (H, SH_I), jnp.float32) * s(H), 'su': jax.random.normal(ks[5], (H, SH_I), jnp.float32) * s(H), 'sd': jax.random.normal(ks[6], (SH_I, H), jnp.float32) * s(SH_I)}
    _L0_ffn_in = _L0_ffn_setup()
    _d = {'L0_attn_x': _L0_attn_in['x'], 'L0_attn_W_qkv': _L0_attn_in['W_qkv'], 'L0_attn_W_z': _L0_attn_in['W_z'], 'L0_attn_W_b': _L0_attn_in['W_b'], 'L0_attn_W_a': _L0_attn_in['W_a'], 'L0_attn_W_out': _L0_attn_in['W_out'], 'L0_attn_conv_w': _L0_attn_in['conv_w'], 'L0_attn_dt_bias': _L0_attn_in['dt_bias'], 'L0_attn_A_log': _L0_attn_in['A_log'], 'L0_attn_norm_weight': _L0_attn_in['norm_weight'], 'L0_ffn_norm_w': _L0_ffn_in['norm_w'], 'L0_ffn_router_w': _L0_ffn_in['router_w'], 'L0_ffn_w1': _L0_ffn_in['w1'], 'L0_ffn_w2': _L0_ffn_in['w2'], 'L0_ffn_sg': _L0_ffn_in['sg'], 'L0_ffn_su': _L0_ffn_in['su'], 'L0_ffn_sd': _L0_ffn_in['sd']}
    _x0 = _d['L0_attn_x']
    _d['L0_attn_x'] = jax.random.normal(jax.random.fold_in(jax.random.key(seed), 1), (1, 2048, 256), dtype=_x0.dtype)
    del _x0
    return _d

def reference(L0_attn_x, L0_attn_W_qkv, L0_attn_W_z, L0_attn_W_b, L0_attn_W_a, L0_attn_W_out, L0_attn_conv_w, L0_attn_dt_bias, L0_attn_A_log, L0_attn_norm_weight, L0_ffn_norm_w, L0_ffn_router_w, L0_ffn_w1, L0_ffn_w2, L0_ffn_sg, L0_ffn_su, L0_ffn_sd):

    def _L0_attn_ref(x, W_qkv, W_z, W_b, W_a, W_out, conv_w, dt_bias, A_log, norm_weight):
        import jax, jax.numpy as jnp
        import numpy as np
        from jax import lax
        DIM = 256
        NK = 8
        NV = 16
        DK = 64
        DV = 64
        KCONV = 4
        KEY_DIM = NK * DK
        VAL_DIM = NV * DV
        CONV_DIM = 2 * KEY_DIM + VAL_DIM
        B = 1
        T = 256
        EPS = 1e-06

        def _l2norm(x, eps=1e-06):
            return x * lax.rsqrt(jnp.sum(x * x, -1, keepdims=True) + eps)

        def _gated_delta_rule(q, k, v, g, beta):

            def step(S, inp):
                q_t, k_t, v_t, g_t, b_t = inp
                S = S * jnp.exp(g_t)[..., None, None]
                pred = jnp.einsum('bhk,bhkv->bhv', k_t, S)
                delta = (v_t - pred) * b_t[..., None]
                S = S + k_t[..., None] * delta[..., None, :]
                o = jnp.einsum('bhk,bhkv->bhv', q_t, S)
                return (S, o)
            Bn, H, Tn, dk = q.shape
            dv = v.shape[-1]
            S0 = jnp.zeros((Bn, H, dk, dv), q.dtype)
            xs = (jnp.moveaxis(q, 2, 0), jnp.moveaxis(k, 2, 0), jnp.moveaxis(v, 2, 0), jnp.moveaxis(g, 2, 0), jnp.moveaxis(beta, 2, 0))
            _, out = lax.scan(step, S0, xs)
            return jnp.moveaxis(out, 0, 2)
        Bx, Tx, _ = x.shape
        qkv = x @ W_qkv.T
        h = jnp.pad(qkv.transpose(0, 2, 1), ((0, 0), (0, 0), (KCONV - 1, 0)))
        h = lax.conv_general_dilated(h, conv_w, (1,), 'VALID', dimension_numbers=('NCH', 'OIH', 'NCH'), feature_group_count=CONV_DIM)
        qkv = jax.nn.silu(h).transpose(0, 2, 1)
        z = (x @ W_z.T).reshape(Bx, Tx, NV, DV)
        beta = jax.nn.sigmoid(x @ W_b.T)
        g = -jnp.exp(A_log) * jax.nn.softplus(x @ W_a.T + dt_bias)
        q, k, v = jnp.split(qkv, [KEY_DIM, 2 * KEY_DIM], axis=-1)
        q = q.reshape(Bx, Tx, NK, DK)
        k = k.reshape(Bx, Tx, NK, DK)
        v = v.reshape(Bx, Tx, NV, DV)
        r = NV // NK
        q = jnp.repeat(q, r, axis=2)
        k = jnp.repeat(k, r, axis=2)
        q = _l2norm(q.transpose(0, 2, 1, 3)) * DK ** (-0.5)
        k = _l2norm(k.transpose(0, 2, 1, 3))
        v = v.transpose(0, 2, 1, 3)
        y = _gated_delta_rule(q, k, v, g.transpose(0, 2, 1), beta.transpose(0, 2, 1))
        y = y.transpose(0, 2, 1, 3)
        yn = y * lax.rsqrt(jnp.mean(y * y, -1, keepdims=True) + EPS)
        yn = norm_weight * yn * jax.nn.silu(z)
        return yn.reshape(Bx, Tx, VAL_DIM) @ W_out.T

    def _L0_ffn_ref(x, norm_w, router_w, w1, w2, sg, su, sd):
        import jax, jax.numpy as jnp
        import numpy as np
        from jax import lax
        H = 256
        I = 128
        E = 32
        K = 4
        SH_I = 256
        EPS = 1e-06

        def _rmsnorm(x, w, eps=EPS):
            var = jnp.mean(jnp.square(x.astype(jnp.float32)), axis=-1, keepdims=True)
            return (x * lax.rsqrt(var + eps)).astype(x.dtype) * w
        B, S, _ = x.shape
        residual = x
        h = _rmsnorm(x, norm_w)
        flat = h.reshape(-1, H)
        T = flat.shape[0]
        logits = flat.astype(jnp.float32) @ router_w.T
        scores = jax.nn.softmax(logits, axis=-1)
        topk_w, topk_ids = lax.top_k(scores, K)
        topk_w = topk_w / jnp.sum(topk_w, axis=-1, keepdims=True)
        ids = topk_ids.reshape(-1)
        sort_idx = jnp.argsort(ids)
        tok_idx = sort_idx // K
        xs = jnp.take(flat, tok_idx, axis=0)
        group_sizes = jnp.bincount(ids, length=E).astype(jnp.int32)
        gu = lax.ragged_dot(xs, w1, group_sizes)
        g, u = jnp.split(gu, 2, axis=-1)
        act = jax.nn.silu(g) * u
        ys = lax.ragged_dot(act, w2, group_sizes)
        y = jnp.zeros((T * K, H), ys.dtype).at[sort_idx].set(ys)
        routed = jnp.sum(y.reshape(T, K, H) * topk_w[..., None].astype(ys.dtype), axis=1)
        shared = jax.nn.silu(flat @ sg) * (flat @ su) @ sd
        out = residual + (routed + shared).reshape(B, S, H)
        return out
    x = L0_attn_x
    x = x + _L0_attn_ref(_layernorm(x, axis=-1), L0_attn_W_qkv, L0_attn_W_z, L0_attn_W_b, L0_attn_W_a, L0_attn_W_out, L0_attn_conv_w, L0_attn_dt_bias, L0_attn_A_log, L0_attn_norm_weight)
    x = x + _L0_ffn_ref(_layernorm(x, axis=-1), L0_ffn_norm_w, L0_ffn_router_w, L0_ffn_w1, L0_ffn_w2, L0_ffn_sg, L0_ffn_su, L0_ffn_sd)
    return x

_drawn_inputs = setup_inputs


def setup_inputs(seed=0):
    import zlib

    import numpy as np

    out = dict(_drawn_inputs(seed))
    spreads = {'L0_attn_dt_bias': (1.0, 0.6),
     'L0_attn_norm_weight': (1.0, 0.6),
     'L0_ffn_norm_w': (1.0, 0.2)}
    factors = {'L0_attn_W_b': 5.438, 'L0_attn_W_a': 8.0}
    for name, (base, spread) in spreads.items():
        noise = np.random.default_rng([zlib.crc32(name.encode()), seed]).standard_normal(out[name].shape)
        drawn = base * np.exp(spread * noise) if base else spread * noise
        out[name] = jnp.asarray(drawn.astype(out[name].dtype))
    for name, factor in factors.items():
        out[name] = (out[name] * factor).astype(out[name].dtype)
    return out
```

```python
from contextlib import ExitStack

import concourse.bass as bass
from concourse import mybir

F32 = mybir.dt.float32
I32 = mybir.dt.int32
U32 = mybir.dt.uint32
ACT = mybir.ActivationFunctionType
ALU = mybir.AluOpType
X = mybir.AxisListType.X

P = 128
T, DIM = 2048, 256
KD = DIM // P
NB = T // P
NK, NV, DH = 8, 16, 64
C = 32
NC = P // C
G = NV // 4
UT = NV // 2
TAPS = 4
CT = (2 * NK * DH + NV * DH) // P
CH = 2 * NK * DH + 2 * NV * DH
PG = CH // P // 4
LV = 5
E, I, TOPK = 32, 128, 4
EV = E + 2
PAIRS = EV // 2
LN_EPS, EPS = 1e-5, 1e-6
MAGIC = 0x5F3759DF
STAGES = ("keys", "read", "first", ("p", 1), "solve", ("t", 1), ("p", 2), "write", ("t", 2), ("p", 3), ("t", 3),
          ("p", 4), ("t", 4))


class Chain:

    def __init__(self, engine, sem):
        self.engine, self.sem, self.base, self.count, self.per, self.pre = engine, sem, 0, 0, 0, 0

    def block(self, b):
        if isinstance(b, int):
            self.pre, self.base, self.count = self.base + self.count, self.base + self.count, 0
        else:
            self.per = self.per or self.count
            self.base, self.count = self.pre + b * self.per, 0

    def leave(self, blocks):
        self.base, self.count, self.per = self.pre + blocks * self.per, 0, 0

    def done(self, instruction):
        self.count += 1
        instruction.then_inc(self.sem, 1)
        self.engine.wait_ge(self.sem, self.base + self.count)


def gated_delta_moe(nc, x, w_qkvz, w_ab, w_out, conv_w, dt_bias, a_log, head_w, ffn_w, w_router, w1, w2, out):
    ctx = ExitStack()
    with ctx:
        def sem(name):
            return ctx.enter_context(nc.semaphore(name))

        def sb(name, *dims, dt=F32):
            t = ctx.enter_context(nc.sbuf_tensor(name, [P] + list(dims), dt))
            return t[(slice(None),) * (len(dims) + 1)]

        res = sb("res", NB, DIM)
        xt = sb("xt", KD, T)
        wc = sb("wc", NB, EV)
        ident = sb("ident", P)
        small = sb("small", 24, 32)

        W1N, W2N = KD * EV * 2 * I, EV * DIM
        arena = sb("arena", W1N + W2N)
        used = [0]

        def carve(*dims):
            n = 1
            for d in dims:
                n *= d
            a = arena[:, used[0]:used[0] + n]
            used[0] += n
            assert used[0] <= W1N + W2N
            names = "abcd"[:len(dims)]
            return a.rearrange(f"p ({' '.join(names)}) -> p {' '.join(names)}", **dict(zip(names, dims))) if len(dims) > 1 else a

        wqz = carve(KD, CH)
        wo = carve(UT, DIM)
        kbd = carve(G, NC, P)
        qbd = carve(G, NC, P)
        vbd = carve(G, NC, P)
        hist = carve(CT, TAPS - 1 + P)
        conv = carve(2, 4, P)
        ctmp = carve(2, 4, P)
        qk = carve(2, G, P)
        vt = carve(UT, P)
        zg = carve(UT, P)
        am = carve(LV, G, P)
        tt = carve(2, G, P)
        sqb = ctmp.rearrange("p n t i -> p (n t i)")
        osel = sqb.rearrange("p (n i) -> p n i", n=NC * G)
        yt = conv.rearrange("p n t i -> p (n t) i")

        tn = sb("tn", G, P)
        pp = sb("pp", G, P)
        aq = sb("aq", 2, G, P)
        kh = sb("kh", 2, G, P)
        vx = sb("vx", 2, G, P)
        state = sb("state", G, P)
        rhs = sb("rhs", G, P)
        uu = sb("uu", G, P)
        up = sb("up", G, P)
        oo = sb("oo", NC, G, P)
        osq = sb("osq", G, P)
        dmat = sb("dmat", NC * G, C)
        dc = sb("dc", NC * G, C)
        gm = sb("gm", NC * G, C)
        kqc = sb("kqc", 2, 2, G, C)
        prm = sb("prm", NB, 6, NC * G)
        bp = sb("bp", 6, NC * G)
        hp = sb("hp", 2, NC * G, 2)
        wab = sb("wab", KD, 2 * NV)
        cw = sb("cw", CT, TAPS)
        fw = sb("fw", DIM)
        wr = sb("wr", KD, E)
        hw = sb("hw", 1)
        dtb = sb("dtb", NV)
        alg = sb("alg", NV)
        row = sb("row", 3, DIM)
        htb = sb("htb", KD, P)
        rt = sb("rt", 6, E)
        idx = sb("idx", 8, dt=U32)
        iota = sb("iota", E)
        wcb = sb("wcb", EV)

        blk1 = sb("blk1", P)
        gt = sb("gt", P)
        le = sb("le", P)
        lvm = sb("lvm", LV, P)
        ind4 = sb("ind4", 4)
        rsel = sb("rsel", 2, 2, DH)
        parind = sb("parind", 2)
        le32 = sb("le32", C)
        eq32 = sb("eq32", C)
        sel = sb("sel", 2, C)
        rmask = sb("rmask", 2)

        th = aq
        ea = kh
        eat = vx

        pre = arena[:, KD * CH + UT * DIM:KD * CH + UT * DIM + 3 * G * NC * P]
        NBV = NB * NV
        xc = pre[:, 0:NB * DIM].rearrange("p (b d) -> p b d", b=NB)
        xsq = arena[:, used[0] - 2 * NB * DIM // 2:used[0]]
        beta_tok = pre[:, 4096:4096 + 2 * NBV].rearrange("p (k b h) -> p k b h", k=2, b=NB)
        pt = pre[:, 4096 + 2 * NBV:4096 + 6 * NBV].rearrange("p (k b h) -> p k b h", k=4, b=NB)
        ghi = prm

        ps = [ctx.enter_context(nc.psum_tensor(f"ps{n}", [P, 512], F32)) for n in range(8)]
        BA, BB, BQ, BP, BT, BTT, BS, BO = (t[:, :] for t in ps)
        banks = [BA, BB, BQ, BP, BT, BTT, BS, BO]

        def tiles(bank):
            return bank.rearrange("p (g j) -> p g j", g=4)

        s_in, s_w, s_ew, s_cst, s_pool, s_vch, s_ach = (sem(n) for n in (
            "inputs_loaded", "weights_loaded", "experts_loaded", "constants_ready", "pool_steps", "vector_steps", "scalar_steps"))
        S = {n: sem(n) for n in (
            "xc_out", "xsq_out", "xn_out", "xt_t", "xt_out", "ab_mm", "beta_tanh", "sp_in", "sp_exp", "sp_ln", "alog_exp",
            "gate_out", "ghi_mm", "ghi_out", "sum_mm", "sum_exp", "pre_done",
            "proj_mm", "hist_in", "conv_out", "tanh_out", "silu_out", "z_tanh", "z_out", "hist_moved",
            "bd_ready", "sq_out", "ss_mm", "ss_out", "hi_mm", "hi_used", "decay_rhs", "decay_mm", "decay_exp",
            "beta_rhs", "beta_mm", "params_out", "bp_in",
            "kh_t", "kh_out", "vx_t", "vx_out", "kq_mm", "kq_out", "mask_out", "qmask_out",
            "first_out", "first_t", "first_in", "p_mm", "p_out", "t_mm", "t_out", "tt_mm", "tt_out",
            "ks_mm", "qs_mm", "qs_used", "rhs_out", "sdec_out", "u_mm", "u_out", "up_out", "au_mm", "o_out",
            "osq_out", "osq_used", "ku_mm", "s_out", "osel_out", "y_mm", "y_out", "op_mm", "x2_out", "h_out", "h_t",
            "htb_in", "ht_out", "rt_mm", "rt_in", "rt_exp", "wc_out",
            "hb_in", "wcb_in", "h1_mm", "h1_tanh", "act_out", "act_t", "act_in", "moe_mm", "fin_out", "stored")}

        block = ctx.enter_context(nc.Block())

        @block.sync
        def _(sp):
            sp.dma_start(res, x.rearrange("(b p) d -> p b d", p=P)).then_inc(s_in, 16)
            for dst, src in ((wab, w_ab), (dtb, dt_bias), (alg, a_log)):
                sp.dma_start(dst, src).then_inc(s_in, 16)
            for dst, src in ((wqz, w_qkvz), (cw, conv_w), (wo, w_out), (hw, head_w), (fw, ffn_w), (wr, w_router)):
                sp.dma_start(dst, src).then_inc(s_w, 16)
            for name in ("rt_mm", "rt_exp", "wc_out", "hist_moved"):
                sp.wait_ge(S[name], NB)
            sp.wait_ge(S["ht_out"], NB)
            sp.wait_ge(S["osq_out"], NB * NC)
            sp.dma_start(arena[:, 0:W1N], w1).then_inc(s_ew, 16)
            sp.dma_start(arena[:, W1N:W1N + W2N], w2).then_inc(s_ew, 16)
            with sp.Fori(0, NB) as b:
                sp.wait_ge(S["fin_out"], b + 1)
                sp.dma_start(out[bass.ts(b, P), :], res[:, b, :]).then_inc(S["stored"], 16)
            sp.wait_ge(S["stored"], 16 * NB)

        @block.gpsimd
        def _(pool):
            g = nc.gpsimd
            steps = [0]

            def step(ins):
                steps[0] += 1
                ins.then_inc(s_pool, 1)
                pool.wait_ge(s_pool, steps[0])

            def keep(ap, pattern, base, mult):
                step(g.affine_select(out=ap, in_=ap, pattern=pattern, compare_op=ALU.is_ge, fill=0.0,
                                     base=base, channel_multiplier=mult))

            step(g.memset(ident, 0.0))
            step(g.affine_select(out=ident, in_=ident, pattern=[[-1, P]], compare_op=ALU.not_equal,
                                 fill=1.0, base=0, channel_multiplier=1))
            step(g.memset(blk1, 1.0))
            keep(blk1, [[-C, 4], [0, C]], 0, 1)
            keep(blk1, [[C, 4], [0, C]], C - 1, -1)
            for m, base, mult in ((gt, -1, 1), (le, 0, -1)):
                step(g.tensor_copy(m, blk1))
                keep(m, [[-mult, P]], base, mult)
            step(g.memset(lvm, 0.0))
            for l in range(LV):
                b = 1 << l
                half = lvm[:, l, :].rearrange("p (n two b) -> p n two b", two=2, b=b)[:, :, 1, :]
                step(g.memset(half, 1.0))
                keep(half, [[-2 * b, P // (2 * b)], [0, b]], 0, 1)
                keep(half, [[2 * b, P // (2 * b)], [0, b]], b - 1, -1)
            step(g.memset(parind, 1.0))
            keep(parind, [[-DH, 2]], 0, 1)
            keep(parind, [[DH, 2]], DH - 1, -1)
            step(g.iota(iota, pattern=[[1, E]], base=0, channel_multiplier=0, allow_small_or_imprecise_dtypes=True))
            for z in (hist[:, :, 0:TAPS - 1], state):
                step(g.memset(z, 0.0))
            g.memset(wc[:, :, E:EV], 0.5).then_inc(s_cst, 1)
            pool.wait_ge(S["pre_done"], 1)
            for z in (kbd, qbd):
                step(g.memset(z, 0.0))
            g.memset(vbd, 0.0).then_inc(s_cst, 1)

            def masks(n, later, c, levels):
                pool.wait_ge(S["kq_out"], n + 1)
                for l in levels:
                    if later or c > 0:
                        if l == 0:
                            pool.wait_ge(S["first_out"], n)
                        else:
                            pool.wait_ge(S["p_mm"], n * (LV - 1) - (LV - 1) + l)
                    g.tensor_tensor(am[:, l, :, :].rearrange("p g (h i) -> p g h i", i=C),
                                    kqc[:, c % 2, 1, :, :].unsqueeze(2).broadcast_to([P, G, 4, C]),
                                    lvm[:, l, :].rearrange("p (h i) -> p h i", i=C).unsqueeze(1).broadcast_to([P, G, 4, C]),
                                    ALU.mult).then_inc(S["mask_out"], 1)

            def query_mask(n, later, c):
                if later or c > 1:
                    pool.wait_ge(S["au_mm"], n - 1)
                g.tensor_tensor(aq[:, c % 2, :, :].rearrange("p g (h i) -> p g h i", i=C),
                                kqc[:, c % 2, 0, :, :].unsqueeze(2).broadcast_to([P, G, 4, C]),
                                le.rearrange("p (h i) -> p h i", i=C).unsqueeze(1).broadcast_to([P, G, 4, C]),
                                ALU.mult).then_inc(S["qmask_out"], 1)

            def state_decay(n, c):
                pool.wait_ge(S["ks_mm"], n + 1)
                pool.wait_ge(S["qs_mm"], n + 1)
                s4 = state.rearrange("p g (r d) -> p g r d", r=2)
                for r in range(2):
                    g.tensor_tensor(s4[:, :, r, :], s4[:, :, r, :],
                                    bp[:, 4 + r, c * G:(c + 1) * G].unsqueeze(2).broadcast_to([P, G, DH]),
                                    ALU.mult).then_inc(S["sdec_out"], 1)

            def u_decay(n, later, c):
                pool.wait_ge(S["u_out"], n + 1)
                if later or c > 0:
                    pool.wait_ge(S["ku_mm"], n)
                g.tensor_tensor(up, uu, bp[:, 3, c * G:(c + 1) * G].unsqueeze(2).broadcast_to([P, G, P]),
                                ALU.mult).then_inc(S["up_out"], 1)

            def o_square(n, later, c):
                pool.wait_ge(S["o_out"], n + 1)
                if later or c > 0:
                    pool.wait_ge(S["osq_used"], n)
                g.tensor_tensor(osq, oo[:, c, :, :], oo[:, c, :, :], ALU.mult).then_inc(S["osq_out"], 1)

            def attention(b, later):
                pool.wait_ge(S["params_out"], b + 1)
                for c in range(NC + 1):
                    n = b * NC + c
                    for stage in STAGES:
                        if c < NC:
                            if stage == "keys":
                                masks(n, later, c, (0, 1))
                            if stage == "first":
                                masks(n, later, c, (2, 3))
                            if stage == ("t", 1):
                                masks(n, later, c, (4,))
                                query_mask(n, later, c)
                        if c > 0:
                            if stage == "read":
                                state_decay(n - 1, c - 1)
                            if stage == "solve":
                                u_decay(n - 1, later, c - 1)
                            if stage == "write":
                                o_square(n - 1, later, c - 1)

            attention(0, False)
            with pool.Fori(1, NB) as b:
                attention(b, True)

        @block.scalar
        def _(act):
            a = nc.scalar
            act.wait_ge(s_in, 64)
            a.activation(alg, alg, ACT.Exp).then_inc(S["alog_exp"], 1)
            act.wait_ge(S["xc_out"], 1)
            a.activation(xsq, xc.rearrange("p b d -> p (b d)"), ACT.Square).then_inc(S["xsq_out"], 1)
            for n in range(NB // 2):
                act.wait_ge(S["xt_t"], n + 1)
                a.activation(xt[:, :, 2 * P * n:2 * P * (n + 1)], banks[n].rearrange("p (k t) -> p k t", k=KD),
                             ACT.Copy).then_inc(S["xt_out"], 1)
            act.wait_ge(S["ab_mm"], 1)
            ab = BA.rearrange("p (b kh) -> p b kh", b=NB)
            a.activation(beta_tok[:, 1, :, :], ab[:, :, 0:NV], ACT.Tanh, scale=0.5).then_inc(S["beta_tanh"], 1)
            act.wait_ge(S["sp_in"], 1)
            a.activation(pt[:, 1, :, :], pt[:, 0, :, :], ACT.Exp).then_inc(S["sp_exp"], 1)
            act.wait_ge(S["sp_exp"], 1)
            a.activation(pt[:, 2, :, :], pt[:, 1, :, :], ACT.Ln, bias=1.0).then_inc(S["sp_ln"], 1)
            act.wait_ge(S["sum_mm"], 1)
            for k in range(4):
                a.activation(prm[:, :, 2 + k, :].rearrange("p b (c g) -> p c b g", c=NC),
                             banks[4 + k][:, 0:NBV].rearrange("p (c b g) -> p c b g", c=NC, b=NB),
                             ACT.Exp).then_inc(S["sum_exp"], 1)

            def tanh(b, later, n):
                act.wait_ge(S["conv_out"], b * 4 + n + 1)
                if n >= 2:
                    act.wait_ge(S["silu_out"], b * 4 + n - 1)
                if later and n < 2:
                    act.wait_ge(S["y_mm"], b * 2)
                a.activation(ctmp[:, n % 2, :, :], conv[:, n % 2, :, :], ACT.Tanh, scale=0.5).then_inc(S["tanh_out"], 1)

            def projections(b, later):
                for n in range(PG):
                    act.wait_ge(S["proj_mm"], b * PG + n + 1)
                    bank = tiles((BA, BB)[n % 2])
                    if n < 4:
                        if later and n == 0:
                            act.wait_ge(S["hist_moved"], b)
                        a.activation(hist[:, 4 * n:4 * n + 4, TAPS - 1:TAPS - 1 + P], bank, ACT.Copy).then_inc(S["hist_in"], 1)
                    else:
                        if later and n == 4:
                            act.wait_ge(S["y_out"], b * 2)
                        a.activation(zg[:, 4 * (n - 4):4 * (n - 3), :], bank, ACT.Tanh, scale=0.5).then_inc(S["z_tanh"], 1)
                    if 1 <= n < 5:
                        tanh(b, later, n - 1)

            def spread(b, later):
                act.wait_ge(S["silu_out"], b * 4 + 2)
                if later:
                    for name in ("kq_mm", "ks_mm", "qs_mm", "kh_t", "vx_t"):
                        act.wait_ge(S[name], b * NC)
                act.wait_ge(s_cst, 2)
                for kind, dst in ((1, kbd), (0, qbd)):
                    for par in range(2):
                        rows = slice(DH * par, DH * par + DH)
                        a.activation(dst[rows, :, :, :].rearrange("p g c (h i) -> p (g c) h i", i=C)[:, :, 2 * par:2 * par + 2, :],
                                     qk[rows, kind, :, :].rearrange("p g (c i) -> p (g c) i", i=C).unsqueeze(2)
                                     .broadcast_to([DH, G * NC, 2, C]), ACT.Copy).then_inc(S["bd_ready"], 1)
                act.wait_ge(S["silu_out"], b * 4 + 4)
                act.wait_ge(S["conv_out"], b * 4 + 4)
                a.activation(sqb, qk.rearrange("p k g t -> p (k g t)"), ACT.Square).then_inc(S["sq_out"], 1)
                for r in range(2):
                    rows = slice(DH * r, DH * r + DH)
                    for par in range(2):
                        h = 2 * par + r
                        a.activation(vbd[rows, :, :, C * h:C * (h + 1)],
                                     vt[rows, :, :].rearrange("p (g par) (c i) -> p g par c i", par=2, i=C)[:, :, par, :, :],
                                     ACT.Copy).then_inc(S["bd_ready"], 1)
                a.activation(hist[:, :, 0:TAPS - 1], hist[:, :, P:P + TAPS - 1], ACT.Copy).then_inc(S["hist_moved"], 1)
                act.wait_ge(S["decay_mm"], b + 1)
                if later:
                    act.wait_ge(S["kq_out"], b * NC)
                a.activation(dmat, BP.rearrange("p (n i) -> p n i", i=C), ACT.Exp).then_inc(S["decay_exp"], 1)

            def inverse(n, later, c, stage):
                if stage == "keys":
                    act.wait_ge(S["kh_t"], n + 1)
                    if later or c > 1:
                        act.wait_ge(S["ku_mm"], n - 1)
                    a.activation(kh[:, c % 2, :, :], tiles(BP), ACT.Copy).then_inc(S["kh_out"], 1)
                if stage == "first":
                    act.wait_ge(S["first_t"], n + 1)
                    a.activation(tn, tiles(BT), ACT.Copy).then_inc(S["first_in"], 1)
                if stage[0] == "p":
                    m = n * (LV - 1) + stage[1]
                    act.wait_ge(S["p_mm"], m)
                    if later or c > 0 or stage[1] > 1:
                        act.wait_ge(S["tt_mm"], m - 1)
                    a.activation(pp, tiles(BP), ACT.Copy).then_inc(S["p_out"], 1)

            def step(n, later, c, stage):
                if stage == "solve":
                    act.wait_ge(S["u_mm"], n + 1)
                    if later or c > 0:
                        act.wait_ge(S["au_mm"], n)
                        act.wait_ge(S["up_out"], n)
                    a.activation(uu, tiles(BS), ACT.Copy).then_inc(S["u_out"], 1)

            def attention(b, later):
                projections(b, later)
                spread(b, later)
                for c in range(NC + 1):
                    for stage in STAGES:
                        if c < NC:
                            inverse(b * NC + c, later, c, stage)
                        if c > 0:
                            step(b * NC + c - 1, later, c - 1, stage)
                act.wait_ge(S["h_t"], b + 1)
                if later:
                    act.wait_ge(S["rt_mm"], b)
                a.activation(htb, BA[:, 0:DIM].rearrange("p (k t) -> p k t", k=KD), ACT.Copy).then_inc(S["htb_in"], 1)
                act.wait_ge(S["htb_in"], b + 1)
                act.wait_ge(s_cst, 2)
                a.activation(xt[:, :, bass.ts(b, P)], htb, ACT.Copy).then_inc(S["ht_out"], 1)
                act.wait_ge(S["rt_in"], b + 1)
                a.activation(rt[:, 1, :], rt[:, 0, :], ACT.Exp, bias=small[:, 14, 0:1],
                             accum_out=small[:, 15, 0:1]).then_inc(S["rt_exp"], 1)

            attention(0, False)
            with act.Fori(1, NB) as b:
                attention(b, True)

            def gate(n, p, later):
                act.wait_ge(S["h1_mm"], n + 1)
                if later or p > 1:
                    act.wait_ge(S["act_out"], n if p == 0 else n - 1)
                a.activation(th[:, p % 2, 0:2, :], (BA, BB)[p % 2].rearrange("p (e k i) -> p e k i", e=2, k=2)[:, :, 0, :],
                             ACT.Tanh, scale=0.5).then_inc(S["h1_tanh"], 1)

            def turned(n, p, later):
                act.wait_ge(S["act_t"], n + 1)
                if later or p > 1:
                    act.wait_ge(S["moe_mm"], n if p == 0 else n - 1)
                a.activation(eat[:, p % 2, 0:2, :], (BQ, BP)[p % 2][:, 0:2 * P].rearrange("p (e t) -> p e t", e=2),
                             ACT.Copy).then_inc(S["act_in"], 1)

            def experts(b, later):
                if later:
                    act.wait_ge(S["h1_mm"], b * PAIRS)
                act.wait_ge(s_cst, 2)
                a.activation(htb, xt[:, :, bass.ts(b, P)], ACT.Copy).then_inc(S["hb_in"], 1)
                gate(b * PAIRS, 0, later)
                for p in range(PAIRS):
                    if p + 1 < PAIRS:
                        gate(b * PAIRS + p + 1, p + 1, later)
                    turned(b * PAIRS + p, p, later)

            act.wait_ge(S["rt_mm"], NB)
            act.wait_ge(S["wc_out"], NB)
            experts(0, False)
            with act.Fori(1, NB) as b:
                experts(b, True)

        @block.vector
        def _(dve):
            v = nc.vector
            ch = Chain(dve, s_vch)
            done = ch.done

            def hold():
                v.tensor_copy(small[:, 23, 0:1], iota[:, 0:1])

            def rsqrt(y, value, tmp, half):
                done(v.tensor_scalar(tmp.bitcast(I32), value.bitcast(I32), 1, None, ALU.logical_shift_right))
                done(v.tensor_scalar(y.bitcast(I32), tmp.bitcast(I32), -1.0, float(MAGIC), ALU.mult, ALU.add))
                done(v.tensor_scalar(half, value, -0.5, None, ALU.mult))
                for _ in range(3):
                    done(v.tensor_tensor(tmp, y, y, ALU.mult))
                    done(v.tensor_tensor(tmp, tmp, half, ALU.mult))
                    done(v.scalar_tensor_tensor(out=y, in0=tmp, scalar=1.5, in1=y, op0=ALU.add, op1=ALU.mult))

            dve.wait_ge(s_cst, 1)
            v.tensor_reduce(eq32, ident.rearrange("p (h i) -> p i h", i=C), X, ALU.add)
            v.tensor_reduce(le32, le.rearrange("p (h i) -> p i h", i=C), X, ALU.add)
            idv = ident.rearrange("p (a r i) -> p a r i", a=2, r=2)
            v.tensor_tensor(sel, idv[:, :, 0, :], idv[:, :, 1, :], ALU.add)
            done(v.tensor_reduce(ind4, blk1.rearrange("p (h i) -> p h i", i=C), X, ALU.add))
            done(v.tensor_scalar(ind4, ind4, 1.0 / C, None, ALU.mult))
            v.tensor_tensor(rmask, ind4[:, 0:2], ind4[:, 2:4], ALU.add)
            for r in range(2):
                done(v.tensor_copy(rsel[:, r, :, :], ind4.rearrange("p (a r) -> p a r", r=2)[:, :, r].unsqueeze(2).broadcast_to([P, 2, DH])))
            dve.wait_ge(s_in, 64)
            mean, var, rstd, t0, t1 = (small[:, k, 0:NB] for k in range(5))
            done(v.tensor_reduce(mean, res, X, ALU.add))
            done(v.tensor_scalar(mean, mean, 1.0 / DIM, None, ALU.mult))
            v.tensor_tensor(xc, res, mean.unsqueeze(2).broadcast_to([P, NB, DIM]), ALU.subtract).then_inc(S["xc_out"], 1)
            dve.wait_ge(S["xsq_out"], 1)
            done(v.tensor_reduce(var, xsq.rearrange("p (b d) -> p b d", b=NB), X, ALU.add))
            done(v.tensor_scalar(var, var, 1.0 / DIM, LN_EPS, ALU.mult, ALU.add))
            rsqrt(rstd, var, t0, t1)
            v.tensor_tensor(xc, xc, rstd.unsqueeze(2).broadcast_to([P, NB, DIM]), ALU.mult).then_inc(S["xn_out"], 1)
            dve.wait_ge(S["ab_mm"], 1)
            dve.wait_ge(S["beta_tanh"], 1)
            ab = BA.rearrange("p (b kh) -> p b kh", b=NB)
            za, zn = pt[:, 3, :, :], pt[:, 0, :, :]
            done(v.tensor_tensor(za, ab[:, :, NV:2 * NV], dtb.unsqueeze(1).broadcast_to([P, NB, NV]), ALU.add))
            done(v.tensor_scalar(zn, za, -1.0, None, ALU.mult))
            v.tensor_tensor(zn, zn, za, ALU.min).then_inc(S["sp_in"], 1)
            done(v.tensor_scalar(beta_tok[:, 1, :, :], beta_tok[:, 1, :, :], 0.5, 0.5, ALU.mult, ALU.add))
            dve.wait_ge(S["sp_ln"], 1)
            done(v.scalar_tensor_tensor(out=za, in0=za, scalar=0.0, in1=pt[:, 2, :, :], op0=ALU.max, op1=ALU.add))
            dve.wait_ge(S["alog_exp"], 1)
            done(v.tensor_scalar(alg, alg, -1.0, None, ALU.mult))
            v.tensor_tensor(beta_tok[:, 0, :, :], za, alg.unsqueeze(1).broadcast_to([P, NB, NV]), ALU.mult).then_inc(S["gate_out"], 1)
            dve.wait_ge(S["ghi_mm"], 1)
            for k in range(2):
                v.tensor_copy(prm[:, :, k, :].rearrange("p b (c g) -> p c b g", c=NC),
                              BB.rearrange("p (c k b g) -> p c k b g", c=NC, k=2, b=NB)[:, :, k, :, :]).then_inc(S["ghi_out"], 1)
            dve.wait_ge(s_w, 96)
            done(v.tensor_scalar(hw, hw, 0.5, None, ALU.mult))
            v.tensor_scalar(wo, wo, hw, None, ALU.mult)
            dve.wait_ge(S["sum_exp"], 4)
            dve.wait_ge(S["ghi_out"], 2)
            dve.wait_ge(S["sum_mm"], 1)
            v.tensor_scalar(alg, alg, 1.0, None, ALU.mult).then_inc(S["pre_done"], 1)

            def convolve(b, later, n):
                dve.wait_ge(S["hist_in"], b * 4 + n + 1)
                if n >= 2:
                    dve.wait_ge(S["silu_out"], b * 4 + n - 1)
                if later and n < 2:
                    dve.wait_ge(S["op_mm"], b)
                for tap in reversed(range(TAPS)):
                    for k in range(4):
                        t = 4 * n + k
                        src, w, acc = hist[:, t, tap:tap + P], cw[:, t, tap:tap + 1], conv[:, n % 2, k, :]
                        if tap == TAPS - 1:
                            ins = v.tensor_scalar(acc, src, w, None, ALU.mult)
                        else:
                            ins = v.scalar_tensor_tensor(out=acc, in0=src, scalar=w, in1=acc, op0=ALU.mult, op1=ALU.add)
                    if tap:
                        done(ins)
                ins.then_inc(S["conv_out"], 1)

            def silu2(b, later, n):
                dve.wait_ge(S["conv_out"], b * 4 + n + 1)
                dve.wait_ge(S["tanh_out"], b * 4 + n + 1)
                if later:
                    if n < 2:
                        dve.wait_ge(S["kq_mm"], b * NC)
                    dve.wait_ge(S["bd_ready"], b * 8)
                dst = qk[:, n, :, :] if n < 2 else vt[:, 4 * (n - 2):4 * (n - 1), :]
                v.scalar_tensor_tensor(out=dst, in0=ctmp[:, n % 2, :, :], scalar=1.0, in1=conv[:, n % 2, :, :],
                                       op0=ALU.add, op1=ALU.mult).then_inc(S["silu_out"], 1)

            def front(b, later):
                dve.wait_ge(s_cst, 2)
                if later:
                    dve.wait_ge(S["up_out"], b * NC)
                    dve.wait_ge(S["sdec_out"], b * 2 * NC)
                    dve.wait_ge(s_cst, 2)
                done(v.tensor_copy(bp, prm[:, b, :, :]))
                if later:
                    dve.wait_ge(S["beta_mm"], b)
                v.tensor_tensor(gm, le32.unsqueeze(1).broadcast_to([P, NC * G, C]),
                                bp[:, 0, :].unsqueeze(2).broadcast_to([P, NC * G, C]), ALU.mult).then_inc(S["decay_rhs"], 1)
                convolve(b, later, 0)
                for n in range(1, 4):
                    convolve(b, later, n)
                    silu2(b, later, n - 1)
                silu2(b, later, 3)
                for n in range(2):
                    dve.wait_ge(S["z_tanh"], b * 2 + n + 1)
                    zz = zg[:, 4 * n:4 * n + 4, :]
                    v.scalar_tensor_tensor(out=zz, in0=zz, scalar=1.0, in1=tiles((BA, BB)[n]), op0=ALU.add,
                                           op1=ALU.mult).then_inc(S["z_out"], 1)
                dve.wait_ge(S["ss_mm"], b + 1)
                sst = small[:, 5, 0:16]
                v.tensor_copy(sst, BQ[:, 0:16]).then_inc(S["ss_out"], 1)
                dve.wait_ge(S["hi_mm"], b + 1)
                x2, rr, ta, tb = (small[:, k, :] for k in (6, 7, 8, 9))
                v.tensor_scalar(x2, BTT[:, 0:32], 4 * EPS, None, ALU.add).then_inc(S["hi_used"], 1)
                dve.wait_ge(S["hi_used"], b + 1)
                rsqrt(rr, x2, ta, tb)
                rq, rk = rr[:, 0:16], rr[:, 16:32]
                bk, ck, rqs = small[:, 10, 0:16], small[:, 11, 0:16], small[:, 12, 0:16]
                v.tensor_scalar(rqs, rq, DH ** -0.5, None, ALU.mult)
                done(v.tensor_tensor(bk, bp[:, 1, :], rk, ALU.mult))
                done(v.tensor_tensor(ck, bk, rk, ALU.mult))
                done(v.tensor_scalar(bk, bk, 0.5, None, ALU.mult))
                dve.wait_ge(S["decay_mm"], b + 1)
                v.tensor_tensor(gm, eq32.unsqueeze(1).broadcast_to([P, NC * G, C]),
                                ck.unsqueeze(2).broadcast_to([P, NC * G, C]), ALU.mult).then_inc(S["beta_rhs"], 1)
                for r in range(2):
                    v.tensor_scalar(hp[:, 1, :, r], bp[:, 2, :], rmask[:, r:r + 1], None, ALU.mult)
                    done(v.tensor_scalar(hp[:, 0, :, r], bp[:, 2, :], rmask[:, r:r + 1], -1.0, ALU.mult, ALU.mult))
                    done(v.tensor_tensor(hp[:, 0, :, r], hp[:, 0, :, r], ck, ALU.mult))
                dve.wait_ge(S["beta_mm"], b + 1)
                dve.wait_ge(S["decay_exp"], b + 1)
                v.tensor_tensor(dc, dmat, BT.rearrange("p (n i) -> p n i", i=C), ALU.mult).then_inc(S["params_out"], 1)
                dve.wait_ge(S["params_out"], b + 1)

            def inverse(b, n, later, c, stage):
                if stage == "keys":
                    cg = slice(c * G, (c + 1) * G)
                    kq = BQ[:, 0:2 * G * C].rearrange("p (g k i) -> p g k i", g=G, k=2)
                    dve.wait_ge(S["kq_mm"], n + 1)
                    if later or c > 1:
                        dve.wait_ge(S["qmask_out"], n - 1)
                        dve.wait_ge(S["mask_out"], (n - 1) * LV)
                    v.tensor_tensor(kqc[:, c % 2, 0, :, :], kq[:, :, 0, :], dmat[:, cg, :], ALU.mult)
                    v.tensor_tensor(kqc[:, c % 2, 1, :, :], kq[:, :, 1, :], dc[:, cg, :], ALU.mult).then_inc(S["kq_out"], 1)
                    dve.wait_ge(S["vx_t"], n + 1)
                    v.tensor_tensor(vx[:, c % 2, :, :], tiles(BTT), small[:, 10, 0:16][:, cg].unsqueeze(2).broadcast_to([P, G, P]),
                                    ALU.mult).then_inc(S["vx_out"], 1)
                if stage == "first":
                    dve.wait_ge(S["mask_out"], n * LV + 1)
                    if later or c > 1:
                        dve.wait_ge(S["u_mm"], n - 1)
                    v.tensor_tensor(tt[:, c % 2, :, :], ident.unsqueeze(1).broadcast_to([P, G, P]), am[:, 0, :, :],
                                    ALU.subtract).then_inc(S["first_out"], 1)
                if stage[0] == "t":
                    l = stage[1]
                    if l < LV - 1:
                        dve.wait_ge(S["t_mm"], n * (LV - 2) + l)
                        dve.wait_ge(S["first_in"], n + 1)
                        if l > 1:
                            dve.wait_ge(S["t_out"], n * (LV - 2) + l - 1)
                        v.tensor_tensor(tn, tn, tiles(BT), ALU.subtract).then_inc(S["t_out"], 1)
                    dve.wait_ge(S["tt_mm"], n * (LV - 1) + l)
                    if l == 1:
                        dve.wait_ge(S["first_out"], n + 1)
                    else:
                        dve.wait_ge(S["tt_out"], n * (LV - 1) + l - 1)
                    v.tensor_tensor(tt[:, c % 2, :, :], tt[:, c % 2, :, :], tiles(BTT), ALU.subtract).then_inc(S["tt_out"], 1)

            def step(b, n, later, c, stage):
                cg = slice(c * G, (c + 1) * G)

                def scale(k):
                    return hp[:, k, cg, :].unsqueeze(3).broadcast_to([P, G, 2, DH])

                def heads(t):
                    return t.rearrange("p g (r d) -> p g r d", r=2)

                if stage == "read":
                    dve.wait_ge(S["ks_mm"], n + 1)
                    if later or c > 0:
                        dve.wait_ge(S["u_mm"], n)
                    done(v.tensor_tensor(heads(rhs), heads(tiles(BS)), scale(0), ALU.mult))
                    dve.wait_ge(S["vx_out"], n + 1)
                    v.tensor_tensor(rhs, rhs, vx[:, c % 2, :, :], ALU.add).then_inc(S["rhs_out"], 1)
                    dve.wait_ge(S["qs_mm"], n + 1)
                    if later:
                        dve.wait_ge(S["y_mm"], b * 2)
                    v.tensor_tensor(heads(oo[:, c, :, :]), heads(tiles(BO)), scale(1), ALU.mult).then_inc(S["qs_used"], 1)
                if stage == "write":
                    dve.wait_ge(S["au_mm"], n + 1)
                    dve.wait_ge(S["qs_used"], n + 1)
                    v.tensor_tensor(oo[:, c, :, :], oo[:, c, :, :], tiles(BO), ALU.add).then_inc(S["o_out"], 1)
                    dve.wait_ge(S["ku_mm"], n + 1)
                    dve.wait_ge(S["sdec_out"], 2 * n + 2)
                    v.tensor_tensor(state, state, tiles(BS), ALU.add).then_inc(S["s_out"], 1)
                if stage == ("p", 3):
                    dve.wait_ge(S["osq_out"], n + 1)
                    v.tensor_reduce(small[:, 13, 0:16][:, cg], osq, X, ALU.add).then_inc(S["osq_used"], 1)

            def tail(b, later):
                rqs, ss = small[:, 12, 0:16], small[:, 13, 0:16]
                q2, rn, ta, tb = (small[:, k, 0:16] for k in (6, 7, 8, 9))
                dve.wait_ge(S["osq_used"], b * NC + NC)
                done(v.tensor_tensor(q2, rqs, rqs, ALU.mult))
                done(v.tensor_tensor(q2, q2, ss, ALU.mult))
                done(v.tensor_scalar(q2, q2, 1.0 / DH, EPS, ALU.mult, ALU.add))
                rsqrt(rn, q2, ta, tb)
                done(v.tensor_tensor(rn, rn, rqs, ALU.mult))
                dve.wait_ge(S["ss_mm"], b + 1)
                v.tensor_tensor(osel, sel.rearrange("p a i -> p (a i)").unsqueeze(1).broadcast_to([P, NC * G, 2 * C]),
                                rn.unsqueeze(2).broadcast_to([P, NC * G, 2 * C]), ALU.mult).then_inc(S["osel_out"], 1)
                for n in range(2):
                    dve.wait_ge(S["y_mm"], b * 2 + n + 1)
                    dve.wait_ge(S["z_out"], b * 2 + n + 1)
                    v.tensor_tensor(yt[:, 4 * n:4 * n + 4, :], zg[:, 4 * n:4 * n + 4, :], tiles((BA, BB)[n]),
                                    ALU.mult).then_inc(S["y_out"], 1)
                x2, xn, hh = (row[:, k, :] for k in range(3))
                dve.wait_ge(S["op_mm"], b + 1)
                v.tensor_tensor(x2, res[:, b, :], BQ[:, 0:DIM], ALU.add).then_inc(S["x2_out"], 1)
                dve.wait_ge(S["x2_out"], b + 1)
                done(v.bn_stats(small[:, 16, 0:6], x2))
                hold()
                done(v.bn_aggr(small[:, 17, 0:2], small[:, 16, 0:6]))
                mean, var = small[:, 17, 0:1], small[:, 17, 1:2]
                r1, v1, r2, v2, ta, tb = (small[:, k, 0:1] for k in (18, 19, 20, 21, 8, 9))
                done(v.tensor_scalar(v1, var, LN_EPS, None, ALU.add))
                rsqrt(r1, v1, ta, tb)
                v.tensor_scalar(xn, x2, mean, r1, ALU.subtract, ALU.mult)
                done(v.tensor_tensor(v2, r1, r1, ALU.mult))
                done(v.tensor_scalar(v2, v2, var, EPS, ALU.mult, ALU.add))
                rsqrt(r2, v2, ta, tb)
                if later:
                    dve.wait_ge(S["h_t"], b)
                v.scalar_tensor_tensor(out=hh, in0=xn, scalar=r2, in1=fw, op0=ALU.mult, op1=ALU.mult).then_inc(S["h_out"], 1)
                done(v.tensor_tensor(res[:, b, :], x2, xn, ALU.add))
                lg, pr, sc, acc = rt[:, 0, :], rt[:, 1, :], rt[:, 2, :], rt[:, 3, :]
                mx, top, val, idf = small[:, 14, 0:1], small[:, 22, 0:8], small[:, 22, 8:16], small[:, 22, 16:24]
                dve.wait_ge(S["rt_mm"], b + 1)
                done(v.tensor_copy(lg, BB[:, 0:E]))
                done(v.tensor_reduce(mx, lg, X, ALU.max))
                v.tensor_scalar(mx, mx, -1.0, None, ALU.mult).then_inc(S["rt_in"], 1)
                dve.wait_ge(S["rt_exp"], b + 1)
                done(v.reciprocal(small[:, 15, 1:2], small[:, 15, 0:1]))
                done(v.tensor_scalar(sc, pr, small[:, 15, 1:2], None, ALU.mult))
                hold()
                done(v.max(top, sc))
                hold()
                done(v.max_index(idx, top, sc))
                v.tensor_copy(idf, idx)
                done(v.tensor_reduce(small[:, 15, 2:3], top[:, 0:TOPK], X, ALU.add))
                done(v.reciprocal(small[:, 15, 3:4], small[:, 15, 2:3]))
                done(v.tensor_scalar(val, top, small[:, 15, 3:4], 0.5, ALU.mult, ALU.mult))
                done(v.tensor_scalar(acc, iota, idf[:, 0:1], val[:, 0:1], ALU.is_equal, ALU.mult))
                for k in range(1, TOPK):
                    done(v.tensor_scalar(rt[:, 4, :], iota, idf[:, k:k + 1], val[:, k:k + 1], ALU.is_equal, ALU.mult))
                    to = acc if k < TOPK - 1 else wc[:, b, 0:E]
                    ins = v.tensor_tensor(to, acc, rt[:, 4, :], ALU.add)
                    if k < TOPK - 1:
                        done(ins)
                ins.then_inc(S["wc_out"], 1)

            def attention(b, later):
                ch.block(b)
                front(b, later)
                for c in range(NC + 1):
                    for stage in STAGES:
                        if c < NC:
                            inverse(b, b * NC + c, later, c, stage)
                        if c > 0:
                            step(b, b * NC + c - 1, later, c - 1, stage)
                tail(b, later)

            attention(0, False)
            with dve.Fori(1, NB) as b:
                attention(b, True)
            ch.leave(NB)

            def experts(b, later):
                ch.block(b)
                if later:
                    dve.wait_ge(s_cst, 2)
                done(v.tensor_copy(wcb, wc[:, b, :]))
                for p in range(PAIRS):
                    n = b * PAIRS + p
                    h1 = (BA, BB)[p % 2].rearrange("p (e k i) -> p e k i", e=2, k=2)
                    act_ = ea[:, p % 2, :, :]
                    dve.wait_ge(S["h1_tanh"], n + 1)
                    if later or p > 1:
                        dve.wait_ge(S["act_t"], n if p == 0 else n - 1)
                    done(v.scalar_tensor_tensor(out=act_[:, 2:4, :], in0=th[:, p % 2, 0:2, :], scalar=1.0, in1=h1[:, :, 0, :],
                                                op0=ALU.add, op1=ALU.mult))
                    for k in range(2):
                        ins = v.scalar_tensor_tensor(out=act_[:, k, :], in0=act_[:, 2 + k, :], scalar=wcb[:, 2 * p + k:2 * p + k + 1],
                                                     in1=h1[:, k, 1, :], op0=ALU.mult, op1=ALU.mult)
                    ins.then_inc(S["act_out"], 1)
                dve.wait_ge(S["moe_mm"], (b + 1) * PAIRS)
                v.tensor_tensor(res[:, b, :], res[:, b, :], BT[:, 0:DIM], ALU.add).then_inc(S["fin_out"], 1)

            experts(0, False)
            with dve.Fori(1, NB) as b:
                experts(b, True)

        @block.tensor
        def _(pe):
            mm, tr = nc.tensor.matmul, nc.tensor.transpose

            pe.wait_ge(s_cst, 1)
            pe.wait_ge(S["xn_out"], 1)
            for n in range(NB // 2):
                for k in range(KD):
                    for j in range(2):
                        ins = tr(banks[n][:, (2 * k + j) * P:(2 * k + j + 1) * P], xc[:, 2 * n + j, k * P:(k + 1) * P], ident)
                ins.then_inc(S["xt_t"], 1)
            pe.wait_ge(S["xt_out"], NB // 2)
            for b in range(NB):
                for k in range(KD):
                    ins = mm(BA[:, 2 * NV * b:2 * NV * (b + 1)], xt[:, k, b * P:(b + 1) * P], wab[:, k, :],
                             start=k == 0, stop=k == KD - 1)
            ins.then_inc(S["ab_mm"], 1)
            pe.wait_ge(S["gate_out"], 1)
            gb = beta_tok.rearrange("p k b (g h) -> p k b g h", h=4)
            for c in range(NC):
                for h in range(4):
                    ins = mm(BB[C * h:C * (h + 1), c * P:(c + 1) * P].rearrange("p (k b g) -> p (k b) g", k=2, b=NB),
                             ident[:, C * c:C * (c + 1)], gb[:, :, :, :, h].rearrange("p k b g -> p (k b) g"), start=True, stop=True)
            ins.then_inc(S["ghi_mm"], 1)
            pe.wait_ge(S["ghi_out"], 2)
            gsrc = prm[:, :, 0, :].rearrange("p b (c g) -> p c b g", c=NC)
            for k, w in enumerate((le, gt, rsel[:, 0, :, :].rearrange("p a d -> p (a d)"), rsel[:, 1, :, :].rearrange("p a d -> p (a d)"))):
                for c in range(NC):
                    ins = mm(banks[4 + k][:, c * NB * G:(c + 1) * NB * G].rearrange("p (b g) -> p b g", b=NB), w, gsrc[:, c, :, :],
                             start=True, stop=True)
            ins.then_inc(S["sum_mm"], 1)

            def front(b, later):
                if later:
                    pe.wait_ge(S["htb_in"], b)
                    pe.wait_ge(S["rt_in"], b)
                for n in range(PG):
                    if n >= 2:
                        pe.wait_ge(S["hist_in"], b * 4 + n - 1)
                    for t in range(4):
                        for k in range(KD):
                            m = (4 * n + t) * P
                            ins = mm((BA, BB)[n % 2][:, t * P:(t + 1) * P], wqz[:, k, m:m + P], xcur(b, k),
                                     start=k == 0, stop=k == KD - 1)
                    ins.then_inc(S["proj_mm"], 1)
                pe.wait_ge(S["decay_rhs"], b + 1)
                if later:
                    pe.wait_ge(S["p_out"], b * NC * (LV - 1))
                mm(BP, gt, gm.rearrange("p n i -> p (n i)"), start=True, stop=True).then_inc(S["decay_mm"], 1)
                pe.wait_ge(S["sq_out"], b + 1)
                if later:
                    pe.wait_ge(S["x2_out"], b)
                for k in range(2 * G):
                    ins = mm(BQ[:, 2 * k:2 * k + 2], sqb[:, k * P:(k + 1) * P], parind, start=True, stop=True)
                ins.then_inc(S["ss_mm"], 1)
                pe.wait_ge(S["ss_out"], b + 1)
                if later:
                    pe.wait_ge(S["tt_out"], b * NC * (LV - 1))
                sst = small[:, 5, 0:16].rearrange("p (k g a) -> p k g a", k=2, g=G)
                for c in range(NC):
                    for h in range(4):
                        ins = mm(BTT[C * h:C * (h + 1), 0:32].rearrange("p (k c g) -> p k c g", k=2, c=NC)[:, :, c, :],
                                 ident[:, C * c:C * (c + 1)], sst[:, :, :, h // 2], start=True, stop=True)
                ins.then_inc(S["hi_mm"], 1)
                pe.wait_ge(S["beta_rhs"], b + 1)
                if later:
                    pe.wait_ge(S["t_out"], b * NC * (LV - 2))
                mm(BT, blk1, gm.rearrange("p n i -> p (n i)"), start=True, stop=True).then_inc(S["beta_mm"], 1)

            def xcur(b, k):
                return xt[:, k, bass.ts(b, P)]

            def inverse(b, n, later, c, stage):
                if stage == "keys":
                    pe.wait_ge(S["bd_ready"], b * 8 + 8)
                    if later or c > 0:
                        pe.wait_ge(S["p_out"], n * (LV - 1))
                    if c == 0:
                        pe.wait_ge(S["decay_exp"], b + 1)
                        pe.wait_ge(S["params_out"], b + 1)
                    for g_ in range(G):
                        ins = tr(tiles(BP)[:, g_, :], kbd[:, g_, c, :], ident)
                    ins.then_inc(S["kh_t"], 1)
                    if later or c > 0:
                        pe.wait_ge(S["tt_out"], n * (LV - 1))
                    for g_ in range(G):
                        ins = tr(tiles(BTT)[:, g_, :], vbd[:, g_, c, :], ident)
                    ins.then_inc(S["vx_t"], 1)
                    if later or c > 0:
                        pe.wait_ge(S["kq_out"], n)
                    for g_ in range(G):
                        ins = mm(BQ[:, g_ * 2 * C:(g_ + 1) * 2 * C].rearrange("p (k i) -> p k i", k=2), kbd[:, g_, c, :],
                                 qk[:, :, g_, c * C:(c + 1) * C], start=True, stop=True)
                    ins.then_inc(S["kq_mm"], 1)
                if stage == "first":
                    pe.wait_ge(S["first_out"], n + 1)
                    if later or c > 0:
                        pe.wait_ge(S["t_out"], n * (LV - 2))
                    for g_ in range(G):
                        ins = tr(tiles(BT)[:, g_, :], tt[:, c % 2, g_, :], ident)
                    ins.then_inc(S["first_t"], 1)
                if stage[0] == "p":
                    l = stage[1]
                    pe.wait_ge(S["mask_out"], n * LV + l + 1)
                    if l == 1:
                        pe.wait_ge(S["first_in"], n + 1)
                        pe.wait_ge(S["kh_out"], n + 1)
                    else:
                        pe.wait_ge(S["t_out"], n * (LV - 2) + l - 1)
                        pe.wait_ge(S["p_out"], n * (LV - 1) + l - 1)
                    for g_ in range(G):
                        ins = mm(tiles(BP)[:, g_, :], am[:, l, g_, :], tn[:, g_, :], start=True, stop=True)
                    ins.then_inc(S["p_mm"], 1)
                if stage[0] == "t":
                    l = stage[1]
                    pe.wait_ge(S["p_out"], n * (LV - 1) + l)
                    if l == 1:
                        pe.wait_ge(S["vx_out"], n + 1)
                    else:
                        pe.wait_ge(S["tt_out"], n * (LV - 1) + l - 1)
                    if l < LV - 1:
                        for g_ in range(G):
                            ins = mm(tiles(BT)[:, g_, :], tt[:, c % 2, g_, :], pp[:, g_, :], start=True, stop=True)
                        ins.then_inc(S["t_mm"], 1)
                    for g_ in range(G):
                        ins = mm(tiles(BTT)[:, g_, :], pp[:, g_, :], tt[:, c % 2, g_, :], start=True, stop=True)
                    ins.then_inc(S["tt_mm"], 1)

            def step(b, n, later, c, stage):
                if stage == "read":
                    if later or c > 0:
                        pe.wait_ge(S["s_out"], n)
                    for g_ in range(G):
                        ins = mm(tiles(BS)[:, g_, :], kbd[:, g_, c, :], state[:, g_, :], start=True, stop=True)
                    ins.then_inc(S["ks_mm"], 1)
                    if later or c > 0:
                        pe.wait_ge(S["o_out"], n)
                    for g_ in range(G):
                        ins = mm(tiles(BO)[:, g_, :], qbd[:, g_, c, :], state[:, g_, :], start=True, stop=True)
                    ins.then_inc(S["qs_mm"], 1)
                if stage == "solve":
                    pe.wait_ge(S["rhs_out"], n + 1)
                    pe.wait_ge(S["tt_out"], (n + 1) * (LV - 1))
                    for g_ in range(G):
                        ins = mm(tiles(BS)[:, g_, :], tt[:, c % 2, g_, :], rhs[:, g_, :], start=True, stop=True)
                    ins.then_inc(S["u_mm"], 1)
                if stage == "write":
                    pe.wait_ge(S["u_out"], n + 1)
                    pe.wait_ge(S["qmask_out"], n + 1)
                    pe.wait_ge(S["qs_used"], n + 1)
                    for g_ in range(G):
                        ins = mm(tiles(BO)[:, g_, :], aq[:, c % 2, g_, :], uu[:, g_, :], start=True, stop=True)
                    ins.then_inc(S["au_mm"], 1)
                    pe.wait_ge(S["up_out"], n + 1)
                    pe.wait_ge(S["kh_out"], n + 1)
                    for g_ in range(G):
                        ins = mm(tiles(BS)[:, g_, :], kh[:, c % 2, g_, :], up[:, g_, :], start=True, stop=True)
                    ins.then_inc(S["ku_mm"], 1)

            def tail(b, later):
                pe.wait_ge(S["osel_out"], b + 1)
                pe.wait_ge(S["z_out"], 2 * b + 2)
                for n in range(2):
                    for g_ in (2 * n, 2 * n + 1):
                        for c in range(NC):
                            dst = (BA, BB)[n].rearrange("p (g a c i) -> p g a c i", g=2, a=2, c=NC)[:, g_ % 2, :, c, :]
                            ins = mm(dst, oo[:, c, g_, :], osel[:, c * G + g_, :].rearrange("p (a i) -> p a i", a=2), start=True, stop=True)
                    ins.then_inc(S["y_mm"], 1)
                pe.wait_ge(S["y_out"], 2 * b + 2)
                pe.wait_ge(S["kq_out"], b * NC + NC)
                for u in range(UT):
                    ins = mm(BQ[:, 0:DIM], yt[:, u, :], wo[:, u, :], start=u == 0, stop=u == UT - 1)
                ins.then_inc(S["op_mm"], 1)
                pe.wait_ge(S["h_out"], b + 1)
                for k in range(KD):
                    ins = tr(BA[:, k * P:(k + 1) * P], row[:, 2, k * P:(k + 1) * P], ident)
                ins.then_inc(S["h_t"], 1)
                pe.wait_ge(S["htb_in"], b + 1)
                for k in range(KD):
                    ins = mm(BB[:, 0:E], htb[:, k, :], wr[:, k, :], start=k == 0, stop=k == KD - 1)
                ins.then_inc(S["rt_mm"], 1)

            def attention(b, later):
                front(b, later)
                for c in range(NC + 1):
                    for stage in STAGES:
                        if c < NC:
                            inverse(b, b * NC + c, later, c, stage)
                        if c > 0:
                            step(b, b * NC + c - 1, later, c - 1, stage)
                tail(b, later)

            pe.wait_ge(s_w, 96)
            pe.wait_ge(S["sum_exp"], 4)
            attention(0, False)
            with pe.Fori(1, NB) as b:
                attention(b, True)

            w1v = arena[:, 0:W1N].rearrange("p (k e j) -> p k e j", k=KD, e=EV)
            w2v = arena[:, W1N:W1N + W2N].rearrange("p (e d) -> p e d", e=EV)
            pe.wait_ge(s_ew, 32)
            pe.wait_ge(S["wc_out"], NB)

            def up_products(b, p, later):
                n = b * PAIRS + p
                if later or p > 1:
                    pe.wait_ge(S["act_out"], n if p == 0 else n - 1)
                for k in range(2):
                    for d in range(KD):
                        ins = mm((BA, BB)[p % 2][:, k * 2 * I:(k + 1) * 2 * I], htb[:, d, :], w1v[:, d, 2 * p + k, :],
                                 start=d == 0, stop=d == KD - 1)
                ins.then_inc(S["h1_mm"], 1)

            def down_products(b, p, later):
                n = b * PAIRS + p
                pe.wait_ge(S["act_out"], n + 1)
                if later or p > 1:
                    pe.wait_ge(S["act_in"], n if p == 0 else n - 1)
                for k in range(2):
                    ins = tr((BQ, BP)[p % 2][:, k * P:(k + 1) * P], ea[:, p % 2, k, :], ident)
                ins.then_inc(S["act_t"], 1)

            def sum_products(b, p, later):
                n = b * PAIRS + p
                pe.wait_ge(S["act_in"], n + 1)
                if later and p == 0:
                    pe.wait_ge(S["fin_out"], b)
                for k in range(2):
                    ins = mm(BT[:, 0:DIM], eat[:, p % 2, k, :], w2v[:, 2 * p + k, :], start=p == 0 and k == 0,
                             stop=p == PAIRS - 1 and k == 1)
                ins.then_inc(S["moe_mm"], 1)

            def experts(b, later):
                pe.wait_ge(S["hb_in"], b + 1)
                up_products(b, 0, later)
                for p in range(PAIRS):
                    if p + 1 < PAIRS:
                        up_products(b, p + 1, later)
                    down_products(b, p, later)
                    if p > 0:
                        sum_products(b, p - 1, later)
                sum_products(b, PAIRS - 1, later)

            experts(0, False)
            with pe.Fori(1, NB) as b:
                experts(b, True)


def kernel(L0_attn_x, L0_attn_W_qkv, L0_attn_W_z, L0_attn_W_b, L0_attn_W_a, L0_attn_W_out, L0_attn_conv_w, L0_attn_dt_bias,
           L0_attn_A_log, L0_attn_norm_weight, L0_ffn_norm_w, L0_ffn_router_w, L0_ffn_w1, L0_ffn_w2, L0_ffn_sg, L0_ffn_su, L0_ffn_sd):
    import numpy as np
    import concourse.bacc as bacc
    from concourse.bass_utils import run_bass_kernel_spmd

    def ktiles(w):
        w = np.asarray(w)
        return np.ascontiguousarray(w.reshape(w.shape[0] // P, P, w.shape[1]).transpose(1, 0, 2))

    def rows(w):
        w = np.asarray(w).reshape(-1)
        return np.ascontiguousarray(np.broadcast_to(w, (P, w.shape[0])))

    sg, su, sd = (np.asarray(w) for w in (L0_ffn_sg, L0_ffn_su, L0_ffn_sd))
    shared_in = np.stack([np.concatenate([sg[:, j * I:(j + 1) * I], su[:, j * I:(j + 1) * I]], 1) for j in range(EV - E)])
    w1 = np.concatenate([np.asarray(L0_ffn_w1), shared_in])
    w2 = np.concatenate([np.asarray(L0_ffn_w2), sd.reshape(EV - E, I, DIM)])
    arrays = {
        "x": np.asarray(L0_attn_x).reshape(T, DIM),
        "w_qkvz": ktiles(np.concatenate([np.asarray(L0_attn_W_qkv), np.asarray(L0_attn_W_z)]).T),
        "w_ab": ktiles(np.concatenate([np.asarray(L0_attn_W_b), np.asarray(L0_attn_W_a)]).T),
        "w_out": ktiles(np.asarray(L0_attn_W_out).T),
        "conv_w": ktiles(np.asarray(L0_attn_conv_w).reshape(CT * P, TAPS)),
        "dt_bias": rows(L0_attn_dt_bias),
        "a_log": rows(L0_attn_A_log),
        "head_w": np.ascontiguousarray(np.tile(np.asarray(L0_attn_norm_weight), 2).reshape(P, 1)),
        "ffn_w": rows(L0_ffn_norm_w),
        "w_router": ktiles(np.asarray(L0_ffn_router_w).T),
        "w1": np.ascontiguousarray(w1.reshape(EV, KD, P, 2 * I).transpose(2, 1, 0, 3).reshape(P, -1)),
        "w2": np.ascontiguousarray(w2.transpose(1, 0, 2).reshape(P, -1)),
    }
    nc = bacc.Bacc("TRN2", target_bir_lowering=False, num_devices=1)
    aps = [nc.dram_tensor(f"in_{n}", a.shape, F32, kind="ExternalInput").ap() for n, a in arrays.items()]
    out = nc.dram_tensor("out", (T, DIM), F32, kind="ExternalOutput").ap()
    gated_delta_moe(nc, *aps, out)
    r = run_bass_kernel_spmd(nc, [{f"in_{n}": a for n, a in arrays.items()}], core_ids=[0])
    return r.results[0]["out"].reshape(1, T, DIM)
```

```python
from contextlib import ExitStack

import concourse.bass as bass
from concourse import mybir

F32 = mybir.dt.float32
I32 = mybir.dt.int32
U32 = mybir.dt.uint32
ACT = mybir.ActivationFunctionType
ALU = mybir.AluOpType
X = mybir.AxisListType.X

P = 128
T, DIM = 2048, 256
KD = DIM // P
NB = T // P
NK, NV, DH = 8, 16, 64
C = 32
NC = P // C
G = NV // 4
UT = NV // 2
TAPS = 4
CT = (2 * NK * DH + NV * DH) // P
CH = 2 * NK * DH + 2 * NV * DH
PG = CH // P // 4
LV = 5
E, I, TOPK = 32, 128, 4
EV = E + 2
PAIRS = EV // 2
LN_EPS, EPS = 1e-5, 1e-6
MAGIC = 0x5F3759DF
DVE_STEPS = 49
STAGES = ("p1", "query", "t1", "solve", "p2", "write", "t2", "keys", "grow", "p3", "turn", "t3", "p4", "first", "t4",
          "read", "out")
TAP_AT = [[(0, "t1"), (0, "solve"), (0, "p2"), (0, "write")],
          [(0, "t2"), (0, "keys"), (0, "grow"), (0, "turn")],
          [(1, "p1"), (1, "query"), (1, "t1"), (1, "solve")],
          [(1, "p2"), (1, "write"), (1, "t2"), (1, "keys")]]
PROJECT_AT = [(0, "p1"), (0, "t1"), (0, "t3"), (1, "p1")]
TANH_AT = [(0, "t2"), (0, "t3"), (1, "p2"), (1, "grow")]
SILU_AT = [(0, "t3"), (0, "first"), (1, "write"), (1, "turn")]
SPREAD_AT = {(2, "grow"): (1, 0), (3, "p2"): (1, 1), (0, "query"): (0, 2), (0, "write"): (0, 3)}
COMMIT_AT = {(2, "turn"): (1, 0), (3, "keys"): (1, 1), (0, "solve"): (0, 2), (1, "p1"): (0, 3)}


class Chain:

    def __init__(self, engine, sem):
        self.engine, self.sem, self.base, self.count, self.pre = engine, sem, 0, 0, 0

    def enter(self, iteration, per):
        self.pre = self.base + self.count
        self.base, self.count = self.pre + iteration * per, 0

    def leave(self, iterations, per):
        assert self.count == per, self.count
        self.base, self.count = self.pre + iterations * per, 0

    def done(self, instruction):
        self.count += 1
        instruction.then_inc(self.sem, 1)
        self.engine.wait_ge(self.sem, self.base + self.count)


def wait(engine, sem, value):
    if not (isinstance(value, int) and value <= 0):
        engine.wait_ge(sem, value)


def gated_delta_moe(nc, x, w_qkvz, w_ab, w_out, conv_w, dt_bias, a_log, head_w, ffn_w, w_router, w1, w2, out):
    ctx = ExitStack()
    with ctx:
        def sem(name):
            return ctx.enter_context(nc.semaphore(name))

        def sb(name, *dims, dt=F32):
            t = ctx.enter_context(nc.sbuf_tensor(name, [P] + list(dims), dt))
            return t[(slice(None),) * (len(dims) + 1)]

        base = nc.dram_tensor("base", (T, DIM), F32).ap()

        xt = sb("xt", KD, T)
        wc = sb("wc", NB, EV)
        ident = sb("ident", P)
        small = sb("small", 24, 32)

        W1N, W2N = KD * EV * 2 * I, EV * DIM
        arena = sb("arena", W1N + W2N)
        used = [0]

        def carve(*dims):
            n = 1
            for d in dims:
                n *= d
            a = arena[:, used[0]:used[0] + n]
            used[0] += n
            assert used[0] <= W1N + W2N
            names = "abcd"[:len(dims)]
            return a.rearrange(f"p ({' '.join(names)}) -> p {' '.join(names)}", **dict(zip(names, dims))) if len(dims) > 1 else a

        wqz = carve(KD, CH)
        wo = carve(UT, DIM)
        kbd = carve(G, NC, P)
        qbd = carve(G, NC, P)
        vbd = carve(G, NC, P)
        hist = carve(CT, TAPS - 1 + P)
        conv = carve(2, 4, P)
        ctmp = carve(2, 4, P)
        qk = carve(2, G, P)
        vt = carve(UT, P)
        zg = carve(UT, P)
        am = carve(LV, G, P)
        tt = carve(2, G, P)

        tn = sb("tn", G, P)
        pp = sb("pp", G, P)
        aq = sb("aq", 2, G, P)
        kh = sb("kh", 2, G, P)
        vx = sb("vx", 2, G, P)
        state = sb("state", G, P)
        rhs = sb("rhs", G, P)
        uu = sb("uu", G, P)
        up = sb("up", G, P)
        oo = sb("oo", 2, G, P)
        osq = sb("osq", G, P)
        osel = sb("osel", G, 2 * C)
        yraw = sb("yraw", UT, P)
        yt = sb("yt", UT, P)
        sqb = sb("sqb", 2 * G, P)
        gm = sb("gm", NC * G, C)
        kqc = sb("kqc", 2, 2, G, C)
        qks = sb("qks", NC, 2, G, C)
        prm = sb("prm", NB, 6, NC * G)
        F_HP, F_SV, F_RQ, F_RQ2, F_D, F_DC, F_END = 24, 40, 44, 48, 52, 180, 308
        nxt = sb("nxt", NC, F_END)
        cur = sb("cur", NC, F_END)
        wab = sb("wab", KD, 2 * NV)
        cw = sb("cw", CT, TAPS)
        fw = sb("fw", DIM)
        wr = sb("wr", KD, E)
        hw = sb("hw", 1)
        dtb = sb("dtb", NV)
        alg = sb("alg", NV)
        xin = sb("xin", DIM)
        row = sb("row", 4, DIM)
        htb = sb("htb", KD, P)
        rt = sb("rt", 5, E)
        idx = sb("idx", 8, dt=U32)
        iota = sb("iota", E)
        wcb = sb("wcb", EV)

        blk1 = sb("blk1", P)
        gt = sb("gt", P)
        le = sb("le", P)
        lvm = sb("lvm", LV, P)
        ind4 = sb("ind4", 4)
        rsel = sb("rsel", 2, 2, DH)
        parind = sb("parind", 2)
        le32 = sb("le32", C)
        eq32 = sb("eq32", C)
        sel = sb("sel", 2, C)
        rmask = sb("rmask", 2)
        mhalf = sb("mhalf", 32)

        th, ea, eat = aq, kh, vx

        NBV = NB * NV
        scratch = KD * CH + UT * DIM
        xc = arena[:, scratch:scratch + NB * DIM].rearrange("p (b d) -> p b d", b=NB)
        beta_tok = arena[:, scratch + NB * DIM:scratch + NB * DIM + 2 * NBV].rearrange("p (k b h) -> p k b h", k=2, b=NB)
        pt = arena[:, scratch + NB * DIM + 2 * NBV:scratch + NB * DIM + 6 * NBV].rearrange("p (k b h) -> p k b h", k=4, b=NB)
        xsq = arena[:, used[0] - NB * DIM:used[0]]
        xall = arena[:, used[0] - 2 * NB * DIM:used[0] - NB * DIM].rearrange("p (b d) -> p b d", b=NB)
        assert scratch + NB * DIM + 6 * NBV <= scratch + 3 * G * NC * P

        ps = [ctx.enter_context(nc.psum_tensor(f"ps{n}", [P, 512], F32)) for n in range(8)]
        BA, BB, BQ, BP, BT, BTT, BS, BO = (t[:, :] for t in ps)
        banks = [BA, BB, BQ, BP, BT, BTT, BS, BO]

        def tiles(bank):
            return bank.rearrange("p (g j) -> p g j", g=4)

        s_in, s_w, s_ew, s_cst, s_pool, s_vch, s_ech = (sem(n) for n in (
            "inputs_loaded", "weights_loaded", "experts_loaded", "constants_ready", "pool_steps", "vector_steps", "expert_steps"))
        S = {n: sem(n) for n in (
            "xc_out", "xsq_out", "xn_out", "xt_t", "xt_out", "ab_mm", "beta_tanh", "sp_in", "sp_exp", "sp_ln", "alog_exp",
            "gate_out", "ghi_mm", "ghi_out", "sum_mm", "sum_exp", "pre_done",
            "proj_mm", "hist_in", "conv_out", "tanh_out", "silu_out", "hist_moved", "spread_in", "cur_in",
            "sq_out", "ss_mm", "ss_out", "hi_mm", "qk_in", "qk_pow", "decay_rhs", "decay_mm", "decay_exp",
            "beta_rhs", "beta_mm", "params_out",
            "kh_t", "kh_out", "vx_t", "vx_out", "kq_mm", "kq_out", "mask_out", "qmask_out",
            "first_out", "first_t", "first_in", "p_mm", "p_out", "t_mm", "t_out", "tt_mm", "tt_out",
            "ks_mm", "qs_mm", "qs_used", "rhs_out", "sdec_out", "u_mm", "u_out", "up_out", "au_mm", "o_out",
            "osq_out", "osq_used", "ku_mm", "s_out", "norm_in", "norm_pow", "osel_out", "y_mm", "y_out",
            "z_mm", "z_tanh", "z_out", "yt_out", "op_mm", "x_in", "x2_out", "ln_in", "ln_pow", "rms_in", "rms_pow",
            "h_out", "base_out", "base_stored", "h_t", "htb_in", "ht_out", "rt_mm", "rt_in", "rt_exp", "wc_out",
            "base_in", "hb_in", "h1_mm", "h1_tanh", "act_out", "act_t", "act_in", "moe_mm", "fin_out", "stored")}

        def run(b, inverse, prepare, step, spread, front, tail, first=False, last=False, end=False):
            for c in range(NC):
                n = b * NC + c
                for stage in STAGES:
                    if not end:
                        inverse(n, c, stage)
                    if not end and not (last and c == NC - 1):
                        prepare(n + 1, (c + 1) % NC, stage)
                    if not (first and c == 0) and not (end and c > 0):
                        step(b, n - 1, (c - 1) % NC, stage)
                    for at, what in ((SPREAD_AT, "spread"), (COMMIT_AT, "commit")):
                        ahead, k = at.get((c, stage), (None, None))
                        if (ahead == 0 and not end) or (ahead == 1 and not last and not end):
                            spread(b + ahead, k, what)
                    if not last and not end:
                        front(b + 1, (c, stage))
                    if not first:
                        tail(b - 1, (c, stage))

        def run_all(engine, *parts):
            prepare, spread, front = parts[1], parts[3], parts[4]
            for c in range(NC):
                for stage in STAGES:
                    front(0, (c, stage))
            for k in range(2):
                spread(0, k, "spread")
                spread(0, k, "commit")
            for stage in STAGES:
                prepare(0, 0, stage)
            run(0, *parts, first=True)
            run(1, *parts)
            with engine.Fori(2, NB - 1) as b:
                run(b, *parts)
            run(NB - 1, *parts, last=True)
            run(NB, *parts, end=True)

        def nothing(*_):
            pass

        block = ctx.enter_context(nc.Block())

        @block.sync
        def _(sp):
            sp.dma_start(xall, x.rearrange("(b p) d -> p b d", p=P)).then_inc(s_in, 16)
            for dst, src in ((wab, w_ab), (dtb, dt_bias), (alg, a_log)):
                sp.dma_start(dst, src).then_inc(s_in, 16)
            for dst, src in ((wqz, w_qkvz), (cw, conv_w), (wo, w_out), (hw, head_w), (fw, ffn_w), (wr, w_router)):
                sp.dma_start(dst, src).then_inc(s_w, 16)
            sp.dma_start(xin, x[0:P, :]).then_inc(S["x_in"], 16)

            def store_base(b):
                sp.wait_ge(S["base_out"], b + 1)
                sp.dma_start(base[bass.ts(b, P), :], row[:, 3, :]).then_inc(S["base_stored"], 16)

            with sp.Fori(0, NB - 1) as b:
                sp.wait_ge(S["x2_out"], b + 1)
                sp.dma_start(xin, x[bass.ts(b + 1, P), :]).then_inc(S["x_in"], 16)
                store_base(b)
            store_base(NB - 1)
            for name in ("rt_mm", "rt_exp", "wc_out", "ht_out"):
                sp.wait_ge(S[name], NB)
            sp.wait_ge(S["osq_out"], NB * NC)
            sp.dma_start(arena[:, 0:W1N], w1).then_inc(s_ew, 16)
            sp.dma_start(arena[:, W1N:W1N + W2N], w2).then_inc(s_ew, 16)
            sp.wait_ge(S["base_stored"], 16 * NB)
            sp.dma_start(xin, base[0:P, :]).then_inc(S["base_in"], 16)

            def store(b):
                sp.wait_ge(S["fin_out"], b + 1)
                sp.dma_start(out[bass.ts(b, P), :], row[:, 0, :]).then_inc(S["stored"], 16)

            with sp.Fori(0, NB - 1) as b:
                store(b)
                sp.dma_start(xin, base[bass.ts(b + 1, P), :]).then_inc(S["base_in"], 16)
            store(NB - 1)
            sp.wait_ge(S["stored"], 16 * NB)

        @block.gpsimd
        def _(pool):
            g = nc.gpsimd
            steps = [0]

            def build(ins):
                steps[0] += 1
                ins.then_inc(s_pool, 1)
                pool.wait_ge(s_pool, steps[0])

            def keep(ap, pattern, base, mult):
                build(g.affine_select(out=ap, in_=ap, pattern=pattern, compare_op=ALU.is_ge, fill=0.0,
                                      base=base, channel_multiplier=mult))

            build(g.memset(ident, 0.0))
            build(g.affine_select(out=ident, in_=ident, pattern=[[-1, P]], compare_op=ALU.not_equal,
                                  fill=1.0, base=0, channel_multiplier=1))
            build(g.memset(blk1, 1.0))
            keep(blk1, [[-C, 4], [0, C]], 0, 1)
            keep(blk1, [[C, 4], [0, C]], C - 1, -1)
            for m, base_, mult in ((gt, -1, 1), (le, 0, -1)):
                build(g.tensor_copy(m, blk1))
                keep(m, [[-mult, P]], base_, mult)
            build(g.memset(lvm, 0.0))
            for l in range(LV):
                b = 1 << l
                half = lvm[:, l, :].rearrange("p (n two b) -> p n two b", two=2, b=b)[:, :, 1, :]
                build(g.memset(half, 1.0))
                keep(half, [[-2 * b, P // (2 * b)], [0, b]], 0, 1)
                keep(half, [[2 * b, P // (2 * b)], [0, b]], b - 1, -1)
            build(g.memset(parind, 1.0))
            keep(parind, [[-DH, 2]], 0, 1)
            keep(parind, [[DH, 2]], DH - 1, -1)
            build(g.iota(iota, pattern=[[1, E]], base=0, channel_multiplier=0, allow_small_or_imprecise_dtypes=True))
            build(g.memset(mhalf, -0.5))
            build(g.memset(state, 0.0))
            g.memset(wc[:, :, E:EV], 0.5).then_inc(s_cst, 1)
            pool.wait_ge(S["pre_done"], 1)
            for z in (hist[:, :, 0:TAPS - 1], kbd, qbd):
                build(g.memset(z, 0.0))
            g.memset(vbd, 0.0).then_inc(s_cst, 1)

            def power(out_, in_, name):
                g.tensor_tensor(out_, in_, mhalf[:, 0:in_.shape[1]], ALU.pow).then_inc(S[name], 1)

            def mask(n, c, l):
                if l == 0:
                    pool.wait_ge(S["kq_out"], n + 1)
                    wait(pool, S["first_out"], n)
                elif not isinstance(n, int) or n > 0:
                    pool.wait_ge(S["p_mm"], (n - 1) * (LV - 1) + l)
                g.tensor_tensor(am[:, l, :, :].rearrange("p g (h i) -> p g h i", i=C),
                                kqc[:, c % 2, 1, :, :].unsqueeze(2).broadcast_to([P, G, 4, C]),
                                lvm[:, l, :].rearrange("p (h i) -> p h i", i=C).unsqueeze(1).broadcast_to([P, G, 4, C]),
                                ALU.mult).then_inc(S["mask_out"], 1)

            def prepare(n, c, stage):
                for l, when in enumerate(("keys", "p3", "p4", "first", "t4")):
                    if stage == when:
                        mask(n, c, l)
                if stage == "read":
                    wait(pool, S["au_mm"], n - 1)
                    g.tensor_tensor(aq[:, c % 2, :, :].rearrange("p g (h i) -> p g h i", i=C),
                                    kqc[:, c % 2, 0, :, :].unsqueeze(2).broadcast_to([P, G, 4, C]),
                                    le.rearrange("p (h i) -> p h i", i=C).unsqueeze(1).broadcast_to([P, G, 4, C]),
                                    ALU.mult).then_inc(S["qmask_out"], 1)

            inverse = nothing

            def step(b, n, c, stage):
                if stage == "query":
                    pool.wait_ge(S["cur_in"], n + 1)
                    pool.wait_ge(S["ks_mm"], n + 1)
                    pool.wait_ge(S["qs_mm"], n + 1)
                    wait(pool, S["s_out"], n)
                    s4 = state.rearrange("p g (r d) -> p g r d", r=2)
                    for r in range(2):
                        g.tensor_tensor(s4[:, :, r, :], s4[:, :, r, :],
                                        cur[:, c, (4 + r) * G:(5 + r) * G].unsqueeze(2).broadcast_to([P, G, DH]),
                                        ALU.mult).then_inc(S["sdec_out"], 1)
                if stage == "solve":
                    pool.wait_ge(S["u_out"], n + 1)
                    wait(pool, S["ku_mm"], n)
                    g.tensor_tensor(up, uu, cur[:, c, 3 * G:4 * G].unsqueeze(2).broadcast_to([P, G, P]),
                                    ALU.mult).then_inc(S["up_out"], 1)
                if stage == "grow":
                    pool.wait_ge(S["o_out"], n + 1)
                    wait(pool, S["osq_used"], n)
                    g.tensor_tensor(osq, oo[:, c % 2, :, :], oo[:, c % 2, :, :], ALU.mult).then_inc(S["osq_out"], 1)
                if stage == "t3":
                    pool.wait_ge(S["norm_in"], n + 1)
                    power(small[:, 11, 0:G], small[:, 10, 0:G], "norm_pow")

            def front(f, at):
                if at == (1, "t2"):
                    pool.wait_ge(S["qk_in"], f + 1)
                    power(small[:, 7, :], small[:, 6, :], "qk_pow")

            def tail(t, at):
                if at == (2, "query"):
                    pool.wait_ge(S["ln_in"], t + 1)
                    power(small[:, 18, 0:1], small[:, 19, 0:1], "ln_pow")
                if at == (2, "solve"):
                    pool.wait_ge(S["rms_in"], t + 1)
                    power(small[:, 20, 0:1], small[:, 21, 0:1], "rms_pow")

            run_all(pool, inverse, prepare, step, nothing, front, tail)

        @block.scalar
        def _(act):
            a = nc.scalar
            act.wait_ge(s_in, 64)
            a.activation(alg, alg, ACT.Exp).then_inc(S["alog_exp"], 1)
            act.wait_ge(S["xc_out"], 1)
            a.activation(xsq, xc.rearrange("p b d -> p (b d)"), ACT.Square).then_inc(S["xsq_out"], 1)
            for n in range(NB // 2):
                act.wait_ge(S["xt_t"], n + 1)
                a.activation(xt[:, :, 2 * P * n:2 * P * (n + 1)], banks[n].rearrange("p (k t) -> p k t", k=KD),
                             ACT.Copy).then_inc(S["xt_out"], 1)
            act.wait_ge(S["ab_mm"], 1)
            ab = BA.rearrange("p (b kh) -> p b kh", b=NB)
            a.activation(beta_tok[:, 1, :, :], ab[:, :, 0:NV], ACT.Tanh, scale=0.5).then_inc(S["beta_tanh"], 1)
            act.wait_ge(S["sp_in"], 1)
            a.activation(pt[:, 1, :, :], pt[:, 0, :, :], ACT.Exp).then_inc(S["sp_exp"], 1)
            act.wait_ge(S["sp_exp"], 1)
            a.activation(pt[:, 2, :, :], pt[:, 1, :, :], ACT.Ln, bias=1.0).then_inc(S["sp_ln"], 1)
            act.wait_ge(S["sum_mm"], 1)
            for k in range(4):
                a.activation(prm[:, :, 2 + k, :].rearrange("p b (c g) -> p c b g", c=NC),
                             banks[4 + k][:, 0:NBV].rearrange("p (c b g) -> p c b g", c=NC, b=NB),
                             ACT.Exp).then_inc(S["sum_exp"], 1)
            act.wait_ge(s_cst, 2)

            def prepare(n, c, stage):
                if stage == "first":
                    act.wait_ge(S["first_t"], n + 1)
                    wait(act, S["p_mm"], n * (LV - 1))
                    a.activation(tn, tiles(BT), ACT.Copy).then_inc(S["first_in"], 1)
                    act.wait_ge(S["kh_t"], n + 1)
                    wait(act, S["ku_mm"], n - 1)
                    a.activation(kh[:, c % 2, :, :], tiles(BO), ACT.Copy).then_inc(S["kh_out"], 1)

            def inverse(n, c, stage):
                if stage in ("p1", "p2", "p3", "p4"):
                    m = n * (LV - 1) + int(stage[1])
                    act.wait_ge(S["p_mm"], m)
                    wait(act, S["tt_mm"], m - 1)
                    a.activation(pp, tiles(BP), ACT.Copy).then_inc(S["p_out"], 1)

            def step(b, n, c, stage):
                if stage == "solve":
                    act.wait_ge(S["u_mm"], n + 1)
                    wait(act, S["au_mm"], n)
                    wait(act, S["up_out"], n)
                    a.activation(uu, tiles(BS), ACT.Copy).then_inc(S["u_out"], 1)
                if stage == "out":
                    act.wait_ge(S["y_mm"], n + 1)
                    if c == 0:
                        wait(act, S["yt_out"], 2 * b)
                    a.activation(yraw[:, :, C * c:C * (c + 1)], BQ[:, 0:2 * P].rearrange("p (u i) -> p u i", u=UT),
                                 ACT.Copy).then_inc(S["y_out"], 1)

            def spread(blk, c, what):
                n = blk * NC + c
                if what == "commit":
                    act.wait_ge(S["params_out"], blk + 1)
                    wait(act, S["osel_out"], n - 3)
                    wait(act, S["up_out"], n - 3)
                    wait(act, S["kq_out"], n - 3)
                    a.activation(cur[:, c, :], nxt[:, c, :], ACT.Copy).then_inc(S["cur_in"], 1)
                    return
                act.wait_ge(S["silu_out"], blk * 4 + 4)
                for name in ("kq_mm", "ks_mm", "qs_mm", "kh_t", "vx_t"):
                    wait(act, S[name], n - 3)
                cs = slice(C * c, C * (c + 1))
                for kind, dst in ((1, kbd), (0, qbd)):
                    for par in range(2):
                        rows = slice(DH * par, DH * par + DH)
                        a.activation(dst[rows, :, c, :].rearrange("p g (h i) -> p g h i", i=C)[:, :, 2 * par:2 * par + 2, :],
                                     qk[rows, kind, :, cs].unsqueeze(2).broadcast_to([DH, G, 2, C]), ACT.Copy)
                a.activation(qks[:, c, :, :, :], qk[:, :, :, cs], ACT.Copy)
                for r in range(2):
                    rows = slice(DH * r, DH * r + DH)
                    ins = a.activation(vbd[rows, :, c, :].rearrange("p g (par r i) -> p g par r i", r=2, i=C)[:, :, :, r, :],
                                       vt[rows, :, cs].rearrange("p (g par) i -> p g par i", par=2), ACT.Copy)
                ins.then_inc(S["spread_in"], 1)

            def front(f, at):
                for n in range(4):
                    if at == PROJECT_AT[n]:
                        act.wait_ge(S["proj_mm"], f * 4 + n + 1)
                        if n == 0:
                            wait(act, S["conv_out"], f * 4)
                            wait(act, S["hist_moved"], f)
                        a.activation(hist[:, 4 * n:4 * n + 4, TAPS - 1:TAPS - 1 + P], tiles((BA, BB)[n % 2]),
                                     ACT.Copy).then_inc(S["hist_in"], 1)
                    if at == TANH_AT[n]:
                        act.wait_ge(S["conv_out"], f * 4 + n + 1)
                        wait(act, S["silu_out"], f * 4 + n - 1)
                        a.activation(ctmp[:, n % 2, :, :], conv[:, n % 2, :, :], ACT.Tanh, scale=0.5).then_inc(S["tanh_out"], 1)
                if at == (1, "query"):
                    act.wait_ge(S["silu_out"], f * 4 + 2)
                    wait(act, S["ss_mm"], f)
                    a.activation(sqb, qk.rearrange("p k g t -> p (k g) t"), ACT.Square).then_inc(S["sq_out"], 1)
                if at == (1, "grow"):
                    act.wait_ge(S["conv_out"], f * 4 + 4)
                    act.wait_ge(S["hist_in"], f * 4 + 4)
                    a.activation(hist[:, :, 0:TAPS - 1], hist[:, :, P:P + TAPS - 1], ACT.Copy).then_inc(S["hist_moved"], 1)
                if at == (1, "t2"):
                    act.wait_ge(S["decay_mm"], f + 1)
                    wait(act, S["cur_in"], f * NC)
                    a.activation(nxt[:, :, F_D:F_DC], BA.rearrange("p (c x) -> p c x", c=NC), ACT.Exp).then_inc(S["decay_exp"], 1)

            def tail(t, at):
                for n, when in enumerate(((0, "t2"), (0, "grow"))):
                    if at == when:
                        act.wait_ge(S["z_mm"], t * 2 + n + 1)
                        wait(act, S["yt_out"], t * 2)
                        a.activation(zg[:, 4 * n:4 * n + 4, :], tiles((BA, BB)[n]), ACT.Tanh, scale=0.5).then_inc(S["z_tanh"], 1)
                if at == (2, "t2"):
                    act.wait_ge(S["h_t"], t + 1)
                    a.activation(htb, BA[:, 0:DIM].rearrange("p (k t) -> p k t", k=KD), ACT.Copy).then_inc(S["htb_in"], 1)
                if at == (2, "keys"):
                    act.wait_ge(S["htb_in"], t + 1)
                    a.activation(small[:, 23, 2:3], iota[:, 0:1], ACT.Copy)
                    a.activation(xt[:, :, bass.ts(t, P)], htb, ACT.Copy).then_inc(S["ht_out"], 1)
                if at == (2, "t3"):
                    act.wait_ge(S["rt_in"], t + 1)
                    a.activation(rt[:, 1, :], rt[:, 0, :], ACT.Exp, bias=small[:, 14, 0:1],
                                 accum_out=small[:, 15, 0:1]).then_inc(S["rt_exp"], 1)

            run_all(act, inverse, prepare, step, spread, front, tail)

            def gate(n, p, later):
                act.wait_ge(S["h1_mm"], n + 1)
                if later or p > 1:
                    act.wait_ge(S["act_out"], n if p == 0 else n - 1)
                a.activation(th[:, p % 2, 0:2, :], (BA, BB)[p % 2].rearrange("p (e k i) -> p e k i", e=2, k=2)[:, :, 0, :],
                             ACT.Tanh, scale=0.5).then_inc(S["h1_tanh"], 1)

            def turned(n, p, later):
                act.wait_ge(S["act_t"], n + 1)
                if later or p > 1:
                    act.wait_ge(S["moe_mm"], n if p == 0 else n - 1)
                a.activation(eat[:, p % 2, 0:2, :], (BQ, BP)[p % 2][:, 0:2 * P].rearrange("p (e t) -> p e t", e=2),
                             ACT.Copy).then_inc(S["act_in"], 1)

            def experts(b, later):
                if later:
                    act.wait_ge(S["h1_mm"], b * PAIRS)
                act.wait_ge(s_cst, 2)
                a.activation(htb, xt[:, :, bass.ts(b, P)], ACT.Copy).then_inc(S["hb_in"], 1)
                gate(b * PAIRS, 0, later)
                for p in range(PAIRS):
                    if p + 1 < PAIRS:
                        gate(b * PAIRS + p + 1, p + 1, later)
                    turned(b * PAIRS + p, p, later)

            act.wait_ge(S["rt_mm"], NB)
            act.wait_ge(S["wc_out"], NB)
            experts(0, False)
            with act.Fori(1, NB) as b:
                experts(b, True)

        @block.vector
        def _(dve):
            v = nc.vector
            ch = Chain(dve, s_vch)
            done = ch.done

            def hold():
                v.tensor_copy(small[:, 23, 0:1], iota[:, 0:1])

            def rsqrt(y, value, tmp, half):
                done(v.tensor_scalar(tmp.bitcast(I32), value.bitcast(I32), 1, None, ALU.logical_shift_right))
                done(v.tensor_scalar(y.bitcast(I32), tmp.bitcast(I32), -1.0, float(MAGIC), ALU.mult, ALU.add))
                done(v.tensor_scalar(half, value, -0.5, None, ALU.mult))
                for _ in range(3):
                    done(v.tensor_tensor(tmp, y, y, ALU.mult))
                    done(v.tensor_tensor(tmp, tmp, half, ALU.mult))
                    done(v.scalar_tensor_tensor(out=y, in0=tmp, scalar=1.5, in1=y, op0=ALU.add, op1=ALU.mult))

            dve.wait_ge(s_cst, 1)
            v.tensor_reduce(eq32, ident.rearrange("p (h i) -> p i h", i=C), X, ALU.add)
            v.tensor_reduce(le32, le.rearrange("p (h i) -> p i h", i=C), X, ALU.add)
            idv = ident.rearrange("p (a r i) -> p a r i", a=2, r=2)
            v.tensor_tensor(sel, idv[:, :, 0, :], idv[:, :, 1, :], ALU.add)
            done(v.tensor_reduce(ind4, blk1.rearrange("p (h i) -> p h i", i=C), X, ALU.add))
            done(v.tensor_scalar(ind4, ind4, 1.0 / C, None, ALU.mult))
            v.tensor_tensor(rmask, ind4[:, 0:2], ind4[:, 2:4], ALU.add)
            for r in range(2):
                done(v.tensor_copy(rsel[:, r, :, :], ind4.rearrange("p (a r) -> p a r", r=2)[:, :, r].unsqueeze(2).broadcast_to([P, 2, DH])))
            dve.wait_ge(s_in, 64)
            mean, var, rstd, t0, t1 = (small[:, k, 0:NB] for k in range(5))
            done(v.tensor_reduce(mean, xall, X, ALU.add))
            done(v.tensor_scalar(mean, mean, 1.0 / DIM, None, ALU.mult))
            v.tensor_tensor(xc, xall, mean.unsqueeze(2).broadcast_to([P, NB, DIM]), ALU.subtract).then_inc(S["xc_out"], 1)
            dve.wait_ge(S["xsq_out"], 1)
            done(v.tensor_reduce(var, xsq.rearrange("p (b d) -> p b d", b=NB), X, ALU.add))
            done(v.tensor_scalar(var, var, 1.0 / DIM, LN_EPS, ALU.mult, ALU.add))
            rsqrt(rstd, var, t0, t1)
            v.tensor_tensor(xc, xc, rstd.unsqueeze(2).broadcast_to([P, NB, DIM]), ALU.mult).then_inc(S["xn_out"], 1)
            dve.wait_ge(S["ab_mm"], 1)
            dve.wait_ge(S["beta_tanh"], 1)
            ab = BA.rearrange("p (b kh) -> p b kh", b=NB)
            za, zn = pt[:, 3, :, :], pt[:, 0, :, :]
            done(v.tensor_tensor(za, ab[:, :, NV:2 * NV], dtb.unsqueeze(1).broadcast_to([P, NB, NV]), ALU.add))
            done(v.tensor_scalar(zn, za, -1.0, None, ALU.mult))
            v.tensor_tensor(zn, zn, za, ALU.min).then_inc(S["sp_in"], 1)
            done(v.tensor_scalar(beta_tok[:, 1, :, :], beta_tok[:, 1, :, :], 0.5, 0.5, ALU.mult, ALU.add))
            dve.wait_ge(S["sp_ln"], 1)
            done(v.scalar_tensor_tensor(out=za, in0=za, scalar=0.0, in1=pt[:, 2, :, :], op0=ALU.max, op1=ALU.add))
            dve.wait_ge(S["alog_exp"], 1)
            done(v.tensor_scalar(alg, alg, -1.0, None, ALU.mult))
            v.tensor_tensor(beta_tok[:, 0, :, :], za, alg.unsqueeze(1).broadcast_to([P, NB, NV]), ALU.mult).then_inc(S["gate_out"], 1)
            dve.wait_ge(S["ghi_mm"], 1)
            for k in range(2):
                v.tensor_copy(prm[:, :, k, :].rearrange("p b (c g) -> p c b g", c=NC),
                              BB.rearrange("p (c k b g) -> p c k b g", c=NC, k=2, b=NB)[:, :, k, :, :]).then_inc(S["ghi_out"], 1)
            dve.wait_ge(s_w, 96)
            done(v.tensor_scalar(hw, hw, 0.5, None, ALU.mult))
            done(v.tensor_scalar(wo, wo, hw, None, ALU.mult))
            dve.wait_ge(S["sum_exp"], 4)
            dve.wait_ge(S["ghi_out"], 2)
            v.tensor_scalar(alg, alg, 1.0, None, ALU.mult).then_inc(S["pre_done"], 1)
            dve.wait_ge(s_cst, 2)

            def conv_taps(f, n, tap):
                if tap == TAPS - 1:
                    dve.wait_ge(S["hist_in"], f * 4 + n + 1)
                    wait(dve, S["silu_out"], f * 4 + n - 1)
                for k in range(4):
                    t = 4 * n + k
                    src, w, acc = hist[:, t, tap:tap + P], cw[:, t, tap:tap + 1], conv[:, n % 2, k, :]
                    if tap == TAPS - 1:
                        ins = v.tensor_scalar(acc, src, w, None, ALU.mult)
                    else:
                        ins = v.scalar_tensor_tensor(out=acc, in0=src, scalar=w, in1=acc, op0=ALU.mult, op1=ALU.add)
                if tap:
                    done(ins)
                else:
                    ins.then_inc(S["conv_out"], 1)

            def front(f, at):
                for n in range(4):
                    for k in range(TAPS):
                        if at == TAP_AT[n][k]:
                            conv_taps(f, n, TAPS - 1 - k)
                    if at == SILU_AT[n]:
                        dve.wait_ge(S["conv_out"], f * 4 + n + 1)
                        dve.wait_ge(S["tanh_out"], f * 4 + n + 1)
                        wait(dve, S["spread_in"], f * NC)
                        if n < 2:
                            wait(dve, S["sq_out"], f)
                        dst = qk[:, n, :, :] if n < 2 else vt[:, 4 * (n - 2):4 * (n - 1), :]
                        v.scalar_tensor_tensor(out=dst, in0=ctmp[:, n % 2, :, :], scalar=1.0, in1=conv[:, n % 2, :, :],
                                               op0=ALU.add, op1=ALU.mult).then_inc(S["silu_out"], 1)
                cg = "p (c g) -> p c g"
                if at == (1, "t1"):
                    wait(dve, S["cur_in"], f * NC)
                    wait(dve, S["beta_mm"], f)
                    hold()
                    done(v.tensor_copy(nxt[:, :, 0:F_HP].rearrange("p c (k g) -> p k c g", g=G),
                                       prm[:, f, :, :].rearrange("p k (c g) -> p k c g", c=NC)))
                    v.tensor_tensor(gm.rearrange("p (c g) i -> p c g i", c=NC),
                                    le32.unsqueeze(1).unsqueeze(1).broadcast_to([P, NC, G, C]),
                                    nxt[:, :, 0:G].unsqueeze(3).broadcast_to([P, NC, G, C]), ALU.mult).then_inc(S["decay_rhs"], 1)
                if at == (1, "solve"):
                    dve.wait_ge(S["ss_mm"], f + 1)
                    v.tensor_copy(small[:, 5, 0:16], BB[:, 0:16]).then_inc(S["ss_out"], 1)
                if at == (1, "write"):
                    dve.wait_ge(S["hi_mm"], f + 1)
                    v.tensor_scalar(small[:, 6, :], BB[:, 0:32], 4 * EPS, None, ALU.add).then_inc(S["qk_in"], 1)
                rq, rk, ck = small[:, 7, 0:16], small[:, 7, 16:32], small[:, 9, 0:16]
                if at == (1, "grow"):
                    dve.wait_ge(S["qk_pow"], f + 1)
                    v.tensor_scalar(nxt[:, :, F_RQ:F_RQ + G], rq.rearrange(cg, c=NC), DH ** -0.5, None, ALU.mult)
                    v.tensor_tensor(nxt[:, :, F_RQ2:F_RQ2 + G], rq.rearrange(cg, c=NC), rq.rearrange(cg, c=NC), ALU.mult)
                    done(v.tensor_tensor(nxt[:, :, F_SV:F_SV + G], nxt[:, :, G:2 * G], rk.rearrange(cg, c=NC), ALU.mult))
                    done(v.tensor_tensor(ck.rearrange(cg, c=NC), nxt[:, :, F_SV:F_SV + G], rk.rearrange(cg, c=NC), ALU.mult))
                    v.tensor_scalar(nxt[:, :, F_SV:F_SV + G], nxt[:, :, F_SV:F_SV + G], 0.5, None, ALU.mult)
                    dve.wait_ge(S["decay_mm"], f + 1)
                    v.tensor_tensor(gm, eq32.unsqueeze(1).broadcast_to([P, NC * G, C]),
                                         ck.unsqueeze(2).broadcast_to([P, NC * G, C]), ALU.mult).then_inc(S["beta_rhs"], 1)
                if at == (1, "first"):
                    v.tensor_scalar(nxt[:, :, F_RQ2:F_RQ2 + G], nxt[:, :, F_RQ2:F_RQ2 + G], 1.0 / DH / DH, None, ALU.mult)
                    for r in range(2):
                        eg = nxt[:, :, 2 * G:3 * G]
                        hp = nxt[:, :, F_HP:F_SV].rearrange("p c (k g r) -> p c k g r", k=2, g=G)
                        v.tensor_scalar(hp[:, :, 1, :, r], eg, rmask[:, r:r + 1], None, ALU.mult)
                        done(v.tensor_scalar(hp[:, :, 0, :, r], eg, rmask[:, r:r + 1], -1.0, ALU.mult, ALU.mult))
                        done(v.tensor_tensor(hp[:, :, 0, :, r], hp[:, :, 0, :, r], ck.rearrange(cg, c=NC), ALU.mult))
                if at == (2, "p1"):
                    dve.wait_ge(S["beta_mm"], f + 1)
                    dve.wait_ge(S["decay_exp"], f + 1)
                    v.tensor_tensor(nxt[:, :, F_DC:F_END], nxt[:, :, F_D:F_DC], BB.rearrange("p (c x) -> p c x", c=NC),
                                    ALU.mult).then_inc(S["params_out"], 1)

            def prepare(n, c, stage):
                if stage == "keys":
                    kq = BQ[:, 0:2 * G * C].rearrange("p (g k i) -> p g k i", g=G, k=2)
                    dve.wait_ge(S["cur_in"], n + 1)
                    dve.wait_ge(S["kq_mm"], n + 1)
                    wait(dve, S["qmask_out"], n - 1)
                    wait(dve, S["mask_out"], (n - 1) * LV)
                    v.tensor_tensor(kqc[:, c % 2, 1, :, :], kq[:, :, 1, :], cur[:, c, F_DC:F_END].rearrange("p (g i) -> p g i", g=G), ALU.mult)
                    v.tensor_tensor(kqc[:, c % 2, 0, :, :], kq[:, :, 0, :], cur[:, c, F_D:F_DC].rearrange("p (g i) -> p g i", g=G),
                                    ALU.mult).then_inc(S["kq_out"], 1)
                if stage == "turn":
                    dve.wait_ge(S["vx_t"], n + 1)
                    wait(dve, S["rhs_out"], n - 1)
                    v.tensor_tensor(vx[:, c % 2, :, :], tiles(BQ), cur[:, c, F_SV:F_SV + G].unsqueeze(2).broadcast_to([P, G, P]),
                                    ALU.mult).then_inc(S["vx_out"], 1)
                if stage == "t3":
                    dve.wait_ge(S["mask_out"], n * LV + 1)
                    wait(dve, S["u_mm"], n - 1)
                    v.tensor_tensor(tt[:, c % 2, :, :], ident.unsqueeze(1).broadcast_to([P, G, P]), am[:, 0, :, :],
                                    ALU.subtract).then_inc(S["first_out"], 1)

            def heads(t):
                return t.rearrange("p g (r d) -> p g r d", r=2)

            def scale(c, k):
                return cur[:, c, F_HP + 2 * G * k:F_HP + 2 * G * (k + 1)].rearrange("p (g r) -> p g r", r=2) \
                    .unsqueeze(3).broadcast_to([P, G, 2, DH])

            def inverse(n, c, stage):
                if stage == "read":
                    dve.wait_ge(S["ks_mm"], n + 1)
                    wait(dve, S["u_mm"], n)
                    done(v.tensor_tensor(heads(rhs), heads(tiles(BS)), scale(c, 0), ALU.mult))
                    dve.wait_ge(S["vx_out"], n + 1)
                    v.tensor_tensor(rhs, rhs, vx[:, c % 2, :, :], ALU.add).then_inc(S["rhs_out"], 1)
                if stage in ("t1", "t2", "t3", "t4"):
                    l = int(stage[1])
                    if l < LV - 1:
                        dve.wait_ge(S["t_mm"], n * (LV - 2) + l)
                        dve.wait_ge(S["first_in"], n + 1)
                        if l > 1:
                            dve.wait_ge(S["t_out"], n * (LV - 2) + l - 1)
                        v.tensor_tensor(tn, tn, tiles(BT), ALU.subtract).then_inc(S["t_out"], 1)
                    dve.wait_ge(S["tt_mm"], n * (LV - 1) + l)
                    if l == 1:
                        dve.wait_ge(S["first_out"], n + 1)
                    else:
                        dve.wait_ge(S["tt_out"], n * (LV - 1) + l - 1)
                    v.tensor_tensor(tt[:, c % 2, :, :], tt[:, c % 2, :, :], tiles(BTT), ALU.subtract).then_inc(S["tt_out"], 1)

            def step(b, n, c, stage):
                o = oo[:, c % 2, :, :]
                nin, nout = small[:, 10, 0:G], small[:, 11, 0:G]
                if stage == "query":
                    dve.wait_ge(S["qs_mm"], n + 1)
                    wait(dve, S["y_mm"], n - 1)
                    wait(dve, S["osq_out"], n - 1)
                    v.tensor_tensor(heads(o), heads(tiles(BO)), scale(c, 1), ALU.mult).then_inc(S["qs_used"], 1)
                if stage == "write":
                    dve.wait_ge(S["au_mm"], n + 1)
                    dve.wait_ge(S["qs_used"], n + 1)
                    v.tensor_tensor(o, o, tiles(BO), ALU.add).then_inc(S["o_out"], 1)
                if stage == "grow":
                    dve.wait_ge(S["ku_mm"], n + 1)
                    dve.wait_ge(S["sdec_out"], 2 * n + 2)
                    v.tensor_tensor(state, state, tiles(BS), ALU.add).then_inc(S["s_out"], 1)
                if stage == "turn":
                    dve.wait_ge(S["osq_out"], n + 1)
                    wait(dve, S["norm_pow"], n)
                    v.tensor_reduce(nin, osq, X, ALU.add).then_inc(S["osq_used"], 1)
                    dve.wait_ge(S["osq_used"], n + 1)
                    done(v.tensor_tensor(nin, nin, cur[:, c, F_RQ2:F_RQ2 + G], ALU.mult))
                    v.tensor_scalar(nin, nin, EPS, None, ALU.add).then_inc(S["norm_in"], 1)
                if stage == "t4":
                    dve.wait_ge(S["norm_pow"], n + 1)
                    done(v.tensor_tensor(nout, nout, cur[:, c, F_RQ:F_RQ + G], ALU.mult))
                    wait(dve, S["y_mm"], n)
                    v.tensor_tensor(osel, sel.rearrange("p a i -> p (a i)").unsqueeze(1).broadcast_to([P, G, 2 * C]),
                                    nout.unsqueeze(2).broadcast_to([P, G, 2 * C]), ALU.mult).then_inc(S["osel_out"], 1)

            x2, xn, hh, bs = (row[:, k, :] for k in range(4))
            mean_, var_ = small[:, 17, 0:1], small[:, 17, 1:2]
            r1, v1, r2, v2 = (small[:, k, 0:1] for k in (18, 19, 20, 21))
            lg, pr, sc, acc, one = (rt[:, k, :] for k in range(5))
            mx, top, val, idf = small[:, 14, 0:1], small[:, 22, 0:8], small[:, 22, 8:16], small[:, 22, 16:24]
            psum_, pinv, wsum, winv = (small[:, 15, k:k + 1] for k in range(4))

            def tail(t, at):
                for n, when in enumerate(((0, "keys"), (0, "turn"))):
                    if at == when:
                        dve.wait_ge(S["z_tanh"], t * 2 + n + 1)
                        zz = zg[:, 4 * n:4 * n + 4, :]
                        v.scalar_tensor_tensor(out=zz, in0=zz, scalar=1.0, in1=tiles((BA, BB)[n]), op0=ALU.add,
                                               op1=ALU.mult).then_inc(S["z_out"], 1)
                for n, when in enumerate(((1, "query"), (1, "t1"))):
                    if at == when:
                        dve.wait_ge(S["z_out"], t * 2 + n + 1)
                        dve.wait_ge(S["y_out"], (t + 1) * NC)
                        wait(dve, S["op_mm"], t)
                        half = slice(4 * n, 4 * n + 4)
                        v.tensor_tensor(yt[:, half, :], zg[:, half, :], yraw[:, half, :], ALU.mult).then_inc(S["yt_out"], 1)
                if at == (1, "out"):
                    dve.wait_ge(S["op_mm"], t + 1)
                    dve.wait_ge(S["x_in"], 16 * (t + 1))
                    v.tensor_tensor(x2, xin, BA[:, 0:DIM], ALU.add).then_inc(S["x2_out"], 1)
                    dve.wait_ge(S["x2_out"], t + 1)
                    done(v.bn_stats(small[:, 16, 0:6], x2))
                    hold()
                    done(v.bn_aggr(small[:, 17, 0:2], small[:, 16, 0:6]))
                    v.tensor_scalar(v1, var_, LN_EPS, None, ALU.add).then_inc(S["ln_in"], 1)
                if at == (2, "t1"):
                    dve.wait_ge(S["ln_pow"], t + 1)
                    v.tensor_scalar(xn, x2, mean_, r1, ALU.subtract, ALU.mult)
                    done(v.tensor_tensor(v2, r1, r1, ALU.mult))
                    v.tensor_scalar(v2, v2, var_, EPS, ALU.mult, ALU.add).then_inc(S["rms_in"], 1)
                if at == (2, "write"):
                    dve.wait_ge(S["rms_pow"], t + 1)
                    v.scalar_tensor_tensor(out=hh, in0=xn, scalar=r2, in1=fw, op0=ALU.mult, op1=ALU.mult).then_inc(S["h_out"], 1)
                    wait(dve, S["base_stored"], 16 * t)
                    v.tensor_tensor(bs, x2, xn, ALU.add).then_inc(S["base_out"], 1)
                if at == (2, "grow"):
                    dve.wait_ge(S["rt_mm"], t + 1)
                    done(v.tensor_copy(lg, BB[:, 0:E]))
                    done(v.tensor_reduce(mx, lg, X, ALU.max))
                    v.tensor_scalar(mx, mx, -1.0, None, ALU.mult).then_inc(S["rt_in"], 1)
                if at == (2, "first"):
                    dve.wait_ge(S["rt_exp"], t + 1)
                    done(v.reciprocal(pinv, psum_))
                    done(v.tensor_scalar(sc, pr, pinv, None, ALU.mult))
                if at == (3, "p1"):
                    hold()
                    done(v.max(top, sc))
                    hold()
                    done(v.max_index(idx, top, sc))
                if at == (3, "t1"):
                    v.tensor_copy(idf, idx)
                    done(v.tensor_reduce(wsum, top[:, 0:TOPK], X, ALU.add))
                    done(v.reciprocal(winv, wsum))
                if at == (3, "solve"):
                    done(v.tensor_scalar(val, top, winv, 0.5, ALU.mult, ALU.mult))
                    done(v.tensor_scalar(acc, iota, idf[:, 0:1], val[:, 0:1], ALU.is_equal, ALU.mult))
                for k, when in enumerate(((3, "write"), (3, "t2"), (3, "grow")), 1):
                    if at == when:
                        done(v.tensor_scalar(one, iota, idf[:, k:k + 1], val[:, k:k + 1], ALU.is_equal, ALU.mult))
                        if k < TOPK - 1:
                            done(v.tensor_tensor(acc, acc, one, ALU.add))
                        else:
                            v.tensor_tensor(wc[:, t, 0:E], acc, one, ALU.add).then_inc(S["wc_out"], 1)

            for c in range(NC):
                for stage in STAGES:
                    front(0, (c, stage))
            for stage in STAGES:
                prepare(0, 0, stage)
            parts = (inverse, prepare, step, nothing, front, tail)
            run(0, *parts, first=True)
            run(1, *parts)
            with dve.Fori(2, NB - 1) as b:
                ch.enter(b - 2, DVE_STEPS)
                run(b, *parts)
            ch.leave(NB - 3, DVE_STEPS)
            run(NB - 1, *parts, last=True)
            run(NB, *parts, end=True)

            def experts(b, later):
                che = Chain(dve, s_ech)
                che.base = b * (PAIRS + 1)
                if later:
                    hold()
                che.done(v.tensor_copy(wcb, wc[:, b, :]))
                for p in range(PAIRS):
                    n = b * PAIRS + p
                    h1 = (BA, BB)[p % 2].rearrange("p (e k i) -> p e k i", e=2, k=2)
                    act_ = ea[:, p % 2, :, :]
                    dve.wait_ge(S["h1_tanh"], n + 1)
                    if later or p > 1:
                        dve.wait_ge(S["act_t"], n if p == 0 else n - 1)
                    che.done(v.scalar_tensor_tensor(out=act_[:, 2:4, :], in0=th[:, p % 2, 0:2, :], scalar=1.0, in1=h1[:, :, 0, :],
                                                    op0=ALU.add, op1=ALU.mult))
                    for k in range(2):
                        ins = v.scalar_tensor_tensor(out=act_[:, k, :], in0=act_[:, 2 + k, :], scalar=wcb[:, 2 * p + k:2 * p + k + 1],
                                                     in1=h1[:, k, 1, :], op0=ALU.mult, op1=ALU.mult)
                    ins.then_inc(S["act_out"], 1)
                dve.wait_ge(S["moe_mm"], (b + 1) * PAIRS)
                dve.wait_ge(S["base_in"], (b + 1) * 16)
                if later:
                    dve.wait_ge(S["stored"], b * 16)
                v.tensor_tensor(row[:, 0, :], xin, BT[:, 0:DIM], ALU.add).then_inc(S["fin_out"], 1)

            experts(0, False)
            with dve.Fori(1, NB) as b:
                experts(b, True)

        @block.tensor
        def _(pe):
            mm, tr = nc.tensor.matmul, nc.tensor.transpose

            pe.wait_ge(s_cst, 1)
            pe.wait_ge(S["xn_out"], 1)
            for n in range(NB // 2):
                for k in range(KD):
                    for j in range(2):
                        ins = tr(banks[n][:, (2 * k + j) * P:(2 * k + j + 1) * P], xc[:, 2 * n + j, k * P:(k + 1) * P], ident)
                ins.then_inc(S["xt_t"], 1)
            pe.wait_ge(S["xt_out"], NB // 2)
            for b in range(NB):
                for k in range(KD):
                    ins = mm(BA[:, 2 * NV * b:2 * NV * (b + 1)], xt[:, k, b * P:(b + 1) * P], wab[:, k, :],
                             start=k == 0, stop=k == KD - 1)
            ins.then_inc(S["ab_mm"], 1)
            pe.wait_ge(S["gate_out"], 1)
            gb = beta_tok.rearrange("p k b (g h) -> p k b g h", h=4)
            for c in range(NC):
                for h in range(4):
                    ins = mm(BB[C * h:C * (h + 1), c * P:(c + 1) * P].rearrange("p (k b g) -> p (k b) g", k=2, b=NB),
                             ident[:, C * c:C * (c + 1)], gb[:, :, :, :, h].rearrange("p k b g -> p (k b) g"), start=True, stop=True)
            ins.then_inc(S["ghi_mm"], 1)
            pe.wait_ge(S["ghi_out"], 2)
            gsrc = prm[:, :, 0, :].rearrange("p b (c g) -> p c b g", c=NC)
            for k, w in enumerate((le, gt, rsel[:, 0, :, :].rearrange("p a d -> p (a d)"), rsel[:, 1, :, :].rearrange("p a d -> p (a d)"))):
                for c in range(NC):
                    ins = mm(banks[4 + k][:, c * NB * G:(c + 1) * NB * G].rearrange("p (b g) -> p b g", b=NB), w, gsrc[:, c, :, :],
                             start=True, stop=True)
            ins.then_inc(S["sum_mm"], 1)
            pe.wait_ge(s_w, 96)
            pe.wait_ge(S["sum_exp"], 4)

            def project(bank, first_tile, t):
                for j in range(4):
                    for k in range(KD):
                        m = (first_tile + j) * P
                        ins = mm(bank[:, j * P:(j + 1) * P], wqz[:, k, m:m + P], xt[:, k, bass.ts(t, P)],
                                 start=k == 0, stop=k == KD - 1)
                return ins

            def front(f, at):
                for n in range(4):
                    if at == PROJECT_AT[n]:
                        if n < 2:
                            wait(pe, S["decay_exp"], f)
                            wait(pe, S["params_out"], f)
                            wait(pe, S["htb_in"], f - 2)
                            wait(pe, S["rt_in"], f - 2)
                        else:
                            pe.wait_ge(S["hist_in"], f * 4 + n - 1)
                            if not isinstance(f, int) or f > 1:
                                pe.wait_ge(S["z_out"], (f - 1) * 2 + n - 3)
                        project((BA, BB)[n % 2], 4 * n, f).then_inc(S["proj_mm"], 1)
                if at == (1, "t2"):
                    pe.wait_ge(S["decay_rhs"], f + 1)
                    pe.wait_ge(S["hist_in"], f * 4 + 3)
                    mm(BA, gt, gm.rearrange("p n i -> p (n i)"), start=True, stop=True).then_inc(S["decay_mm"], 1)
                if at == (1, "solve"):
                    pe.wait_ge(S["sq_out"], f + 1)
                    pe.wait_ge(S["hist_in"], f * 4 + 4)
                    for k in range(2 * G):
                        ins = mm(BB[:, 2 * k:2 * k + 2], sqb[:, k, :], parind, start=True, stop=True)
                    ins.then_inc(S["ss_mm"], 1)
                if at == (1, "write"):
                    pe.wait_ge(S["ss_out"], f + 1)
                    sst = small[:, 5, 0:16].rearrange("p (k g a) -> p k g a", k=2, g=G)
                    for c in range(NC):
                        for h in range(4):
                            ins = mm(BB[C * h:C * (h + 1), 0:32].rearrange("p (k c g) -> p k c g", k=2, c=NC)[:, :, c, :],
                                     ident[:, C * c:C * (c + 1)], sst[:, :, :, h // 2], start=True, stop=True)
                    ins.then_inc(S["hi_mm"], 1)
                if at == (1, "first"):
                    pe.wait_ge(S["qk_in"], f + 1)
                    pe.wait_ge(S["beta_rhs"], f + 1)
                    mm(BB, blk1, gm.rearrange("p n i -> p (n i)"), start=True, stop=True).then_inc(S["beta_mm"], 1)

            def prepare(n, c, stage):
                if stage == "keys":
                    pe.wait_ge(S["spread_in"], n + 1)
                    wait(pe, S["y_out"], n - 2)
                    for g_ in range(G):
                        ins = mm(BQ[:, g_ * 2 * C:(g_ + 1) * 2 * C].rearrange("p (k i) -> p k i", k=2), kbd[:, g_, c, :],
                                 qks[:, c, :, g_, :], start=True, stop=True)
                    ins.then_inc(S["kq_mm"], 1)
                if stage == "turn":
                    pe.wait_ge(S["kq_out"], n + 1)
                    for g_ in range(G):
                        ins = tr(tiles(BQ)[:, g_, :], vbd[:, g_, c, :], ident)
                    ins.then_inc(S["vx_t"], 1)
                if stage == "first":
                    pe.wait_ge(S["first_out"], n + 1)
                    wait(pe, S["t_out"], n * (LV - 2))
                    for g_ in range(G):
                        ins = tr(tiles(BT)[:, g_, :], tt[:, c % 2, g_, :], ident)
                    ins.then_inc(S["first_t"], 1)
                    wait(pe, S["o_out"], n - 1)
                    for g_ in range(G):
                        ins = tr(tiles(BO)[:, g_, :], kbd[:, g_, c, :], ident)
                    ins.then_inc(S["kh_t"], 1)

            def inverse(n, c, stage):
                if stage == "read":
                    wait(pe, S["s_out"], n)
                    for g_ in range(G):
                        ins = mm(tiles(BS)[:, g_, :], kbd[:, g_, c, :], state[:, g_, :], start=True, stop=True)
                    ins.then_inc(S["ks_mm"], 1)
                if stage in ("p1", "p2", "p3", "p4"):
                    l = int(stage[1])
                    pe.wait_ge(S["mask_out"], n * LV + l + 1)
                    if l == 1:
                        pe.wait_ge(S["first_in"], n + 1)
                        wait(pe, S["p_out"], n * (LV - 1))
                    else:
                        pe.wait_ge(S["t_out"], n * (LV - 2) + l - 1)
                        pe.wait_ge(S["p_out"], n * (LV - 1) + l - 1)
                    for g_ in range(G):
                        ins = mm(tiles(BP)[:, g_, :], am[:, l, g_, :], tn[:, g_, :], start=True, stop=True)
                    ins.then_inc(S["p_mm"], 1)
                if stage in ("t1", "t2", "t3", "t4"):
                    l = int(stage[1])
                    pe.wait_ge(S["p_out"], n * (LV - 1) + l)
                    if l == 1:
                        wait(pe, S["tt_out"], n * (LV - 1))
                    else:
                        pe.wait_ge(S["tt_out"], n * (LV - 1) + l - 1)
                    if l < LV - 1:
                        for g_ in range(G):
                            ins = mm(tiles(BT)[:, g_, :], tt[:, c % 2, g_, :], pp[:, g_, :], start=True, stop=True)
                        ins.then_inc(S["t_mm"], 1)
                    for g_ in range(G):
                        ins = mm(tiles(BTT)[:, g_, :], pp[:, g_, :], tt[:, c % 2, g_, :], start=True, stop=True)
                    ins.then_inc(S["tt_mm"], 1)

            def step(b, n, c, stage):
                if stage == "query":
                    pe.wait_ge(S["kh_out"], n + 2 if not isinstance(n, int) or n + 2 <= NB * NC else NB * NC)
                    wait(pe, S["o_out"], n)
                    for g_ in range(G):
                        ins = mm(tiles(BO)[:, g_, :], qbd[:, g_, c, :], state[:, g_, :], start=True, stop=True)
                    ins.then_inc(S["qs_mm"], 1)
                if stage == "solve":
                    pe.wait_ge(S["rhs_out"], n + 1)
                    pe.wait_ge(S["tt_out"], (n + 1) * (LV - 1))
                    for g_ in range(G):
                        ins = mm(tiles(BS)[:, g_, :], tt[:, c % 2, g_, :], rhs[:, g_, :], start=True, stop=True)
                    ins.then_inc(S["u_mm"], 1)
                if stage == "write":
                    pe.wait_ge(S["u_out"], n + 1)
                    pe.wait_ge(S["qmask_out"], n + 1)
                    pe.wait_ge(S["qs_used"], n + 1)
                    for g_ in range(G):
                        ins = mm(tiles(BO)[:, g_, :], aq[:, c % 2, g_, :], uu[:, g_, :], start=True, stop=True)
                    ins.then_inc(S["au_mm"], 1)
                if stage == "grow":
                    pe.wait_ge(S["up_out"], n + 1)
                    pe.wait_ge(S["kh_out"], n + 1)
                    for g_ in range(G):
                        ins = mm(tiles(BS)[:, g_, :], kh[:, c % 2, g_, :], up[:, g_, :], start=True, stop=True)
                    ins.then_inc(S["ku_mm"], 1)
                if stage == "out":
                    pe.wait_ge(S["osel_out"], n + 1)
                    pe.wait_ge(S["vx_out"], n + 3 if not isinstance(n, int) or n + 3 <= NC * NB else NC * NB)
                    for g_ in range(G):
                        ins = mm(BQ[:, 2 * C * g_:2 * C * (g_ + 1)], oo[:, c % 2, g_, :], osel[:, g_, :], start=True, stop=True)
                    ins.then_inc(S["y_mm"], 1)

            def tail(t, at):
                for n, when in enumerate(((0, "t2"), (0, "grow"))):
                    if at == when:
                        if not isinstance(t, int) or t < NB - 1:
                            pe.wait_ge(S["hist_in"], (t + 2) * 4 + 1 + n if not isinstance(t, int) or t < NB - 2 else NB * 4)
                        built = NB if isinstance(t, int) and t == NB - 1 else t + 2
                        pe.wait_ge(S["decay_exp"], built)
                        pe.wait_ge(S["params_out"], built)
                        wait(pe, S["htb_in"], t)
                        wait(pe, S["rt_in"], t)
                        project((BA, BB)[n], CT + 4 * n, t).then_inc(S["z_mm"], 1)
                if at == (1, "t3"):
                    pe.wait_ge(S["yt_out"], 2 * t + 2)
                    pe.wait_ge(S["z_out"], 2 * t + 1)
                    if not isinstance(t, int) or t < NB - 2:
                        pe.wait_ge(S["decay_exp"], t + 3)
                    for u in range(UT):
                        ins = mm(BA[:, 0:DIM], yt[:, u, :], wo[:, u, :], start=u == 0, stop=u == UT - 1)
                    ins.then_inc(S["op_mm"], 1)
                if at == (2, "t2"):
                    pe.wait_ge(S["h_out"], t + 1)
                    pe.wait_ge(S["x2_out"], t + 1)
                    for k in range(KD):
                        ins = tr(BA[:, k * P:(k + 1) * P], row[:, 2, k * P:(k + 1) * P], ident)
                    ins.then_inc(S["h_t"], 1)
                if at == (2, "grow"):
                    pe.wait_ge(S["htb_in"], t + 1)
                    pe.wait_ge(S["z_out"], 2 * t + 2)
                    if not isinstance(t, int) or t < NB - 2:
                        pe.wait_ge(S["params_out"], t + 3)
                    for k in range(KD):
                        ins = mm(BB[:, 0:E], htb[:, k, :], wr[:, k, :], start=k == 0, stop=k == KD - 1)
                    ins.then_inc(S["rt_mm"], 1)

            run_all(pe, inverse, prepare, step, nothing, front, tail)

            w1v = arena[:, 0:W1N].rearrange("p (k e j) -> p k e j", k=KD, e=EV)
            w2v = arena[:, W1N:W1N + W2N].rearrange("p (e d) -> p e d", e=EV)
            pe.wait_ge(s_ew, 32)
            pe.wait_ge(S["wc_out"], NB)

            def up_products(b, p, later):
                n = b * PAIRS + p
                if later or p > 1:
                    pe.wait_ge(S["act_out"], n if p == 0 else n - 1)
                for k in range(2):
                    for d in range(KD):
                        ins = mm((BA, BB)[p % 2][:, k * 2 * I:(k + 1) * 2 * I], htb[:, d, :], w1v[:, d, 2 * p + k, :],
                                 start=d == 0, stop=d == KD - 1)
                ins.then_inc(S["h1_mm"], 1)

            def down_products(b, p, later):
                n = b * PAIRS + p
                pe.wait_ge(S["act_out"], n + 1)
                if later or p > 1:
                    pe.wait_ge(S["act_in"], n if p == 0 else n - 1)
                for k in range(2):
                    ins = tr((BQ, BP)[p % 2][:, k * P:(k + 1) * P], ea[:, p % 2, k, :], ident)
                ins.then_inc(S["act_t"], 1)

            def sum_products(b, p, later):
                n = b * PAIRS + p
                pe.wait_ge(S["act_in"], n + 1)
                if later and p == 0:
                    pe.wait_ge(S["fin_out"], b)
                for k in range(2):
                    ins = mm(BT[:, 0:DIM], eat[:, p % 2, k, :], w2v[:, 2 * p + k, :], start=p == 0 and k == 0,
                             stop=p == PAIRS - 1 and k == 1)
                ins.then_inc(S["moe_mm"], 1)

            def experts(b, later):
                pe.wait_ge(S["hb_in"], b + 1)
                up_products(b, 0, later)
                for p in range(PAIRS):
                    if p + 1 < PAIRS:
                        up_products(b, p + 1, later)
                    down_products(b, p, later)
                    if p > 0:
                        sum_products(b, p - 1, later)
                sum_products(b, PAIRS - 1, later)

            experts(0, False)
            with pe.Fori(1, NB) as b:
                experts(b, True)

def kernel(L0_attn_x, L0_attn_W_qkv, L0_attn_W_z, L0_attn_W_b, L0_attn_W_a, L0_attn_W_out, L0_attn_conv_w, L0_attn_dt_bias,
           L0_attn_A_log, L0_attn_norm_weight, L0_ffn_norm_w, L0_ffn_router_w, L0_ffn_w1, L0_ffn_w2, L0_ffn_sg, L0_ffn_su, L0_ffn_sd):
    import numpy as np
    import concourse.bacc as bacc
    from concourse.bass_utils import run_bass_kernel_spmd

    def ktiles(w):
        w = np.asarray(w)
        return np.ascontiguousarray(w.reshape(w.shape[0] // P, P, w.shape[1]).transpose(1, 0, 2))

    def rows(w):
        w = np.asarray(w).reshape(-1)
        return np.ascontiguousarray(np.broadcast_to(w, (P, w.shape[0])))

    sg, su, sd = (np.asarray(w) for w in (L0_ffn_sg, L0_ffn_su, L0_ffn_sd))
    shared_in = np.stack([np.concatenate([sg[:, j * I:(j + 1) * I], su[:, j * I:(j + 1) * I]], 1) for j in range(EV - E)])
    w1 = np.concatenate([np.asarray(L0_ffn_w1), shared_in])
    w2 = np.concatenate([np.asarray(L0_ffn_w2), sd.reshape(EV - E, I, DIM)])
    arrays = {
        "x": np.asarray(L0_attn_x).reshape(T, DIM),
        "w_qkvz": ktiles(np.concatenate([np.asarray(L0_attn_W_qkv), np.asarray(L0_attn_W_z)]).T),
        "w_ab": ktiles(np.concatenate([np.asarray(L0_attn_W_b), np.asarray(L0_attn_W_a)]).T),
        "w_out": ktiles(np.asarray(L0_attn_W_out).T),
        "conv_w": ktiles(np.asarray(L0_attn_conv_w).reshape(CT * P, TAPS)),
        "dt_bias": rows(L0_attn_dt_bias),
        "a_log": rows(L0_attn_A_log),
        "head_w": np.ascontiguousarray(np.tile(np.asarray(L0_attn_norm_weight), 2).reshape(P, 1)),
        "ffn_w": rows(L0_ffn_norm_w),
        "w_router": ktiles(np.asarray(L0_ffn_router_w).T),
        "w1": np.ascontiguousarray(w1.reshape(EV, KD, P, 2 * I).transpose(2, 1, 0, 3).reshape(P, -1)),
        "w2": np.ascontiguousarray(w2.transpose(1, 0, 2).reshape(P, -1)),
    }
    nc = bacc.Bacc("TRN2", target_bir_lowering=False, num_devices=1)
    aps = [nc.dram_tensor(f"in_{n}", a.shape, F32, kind="ExternalInput").ap() for n, a in arrays.items()]
    out = nc.dram_tensor("out", (T, DIM), F32, kind="ExternalOutput").ap()
    gated_delta_moe(nc, *aps, out)
    r = run_bass_kernel_spmd(nc, [{f"in_{n}": a for n, a in arrays.items()}], core_ids=[0])
    return r.results[0]["out"].reshape(1, T, DIM)
```

```python
from contextlib import ExitStack

import concourse.bass as bass
from concourse import mybir

F32 = mybir.dt.float32
I32 = mybir.dt.int32
U32 = mybir.dt.uint32
ACT = mybir.ActivationFunctionType
ALU = mybir.AluOpType
X = mybir.AxisListType.X

P = 128
T, DIM = 2048, 256
KD = DIM // P
NB = T // P
NK, NV, DH = 8, 16, 64
C = 32
NC = P // C
G = NV // 4
UT = NV // 2
TAPS = 4
CT = (2 * NK * DH + NV * DH) // P
CH = 2 * NK * DH + 2 * NV * DH
LV = 5
LI = LV - 1
E, I, TOPK = 32, 128, 4
EV = E + 2
PAIRS = EV // 2
LN_EPS, EPS = 1e-5, 1e-6
MAGIC = 0x5F3759DF
DVE_STEPS = 49
STAGES = ("p1", "query", "t1", "solve", "p2", "keys", "t2", "weigh", "p3", "settle", "t3", "turn", "write", "grow",
          "first", "lay", "read", "out")
TAP_AT = [[(0, "t1"), (0, "solve"), (0, "p2"), (0, "keys")],
          [(0, "t2"), (0, "weigh"), (0, "p3"), (0, "settle")],
          [(1, "p1"), (1, "query"), (1, "t1"), (1, "solve")],
          [(1, "p2"), (1, "t2"), (1, "weigh"), (1, "p3")]]
PROJECT_AT = [(0, "p1"), (0, "t1"), (0, "t3"), (1, "p1")]
TANH_AT = [(0, "t2"), (0, "t3"), (1, "p2"), (1, "settle")]
SILU_AT = [(0, "t3"), (0, "write"), (1, "t2"), (1, "turn")]
SPREAD_AT = {(2, "query"): [(1, 0, "queries")], (2, "t1"): [(1, 0, "keys")], (2, "p2"): [(1, 0, "values")],
             (2, "t2"): [(1, 0, "commit")],
             (3, "query"): [(1, 1, "queries")], (3, "t1"): [(1, 1, "keys")], (3, "p2"): [(1, 1, "values")],
             (3, "t2"): [(1, 1, "commit")],
             (0, "query"): [(0, 2, "queries")], (0, "t1"): [(0, 2, "keys")], (0, "p2"): [(0, 2, "values")],
             (0, "t2"): [(0, 2, "commit"), (0, 3, "queries")], (0, "settle"): [(0, 3, "keys")], (1, "query"): [(0, 3, "values")],
             (1, "p1"): [(0, 3, "commit")]}


class Chain:

    def __init__(self, engine, sem):
        self.engine, self.sem, self.base, self.count, self.pre = engine, sem, 0, 0, 0

    def enter(self, iteration, per):
        self.pre = self.base + self.count
        self.base, self.count = self.pre + iteration * per, 0

    def leave(self, iterations, per):
        assert self.count == per, self.count
        self.base, self.count = self.pre + iterations * per, 0

    def done(self, instruction):
        self.count += 1
        instruction.then_inc(self.sem, 1)
        self.engine.wait_ge(self.sem, self.base + self.count)


def wait(engine, sem, value):
    if not (isinstance(value, int) and value <= 0):
        engine.wait_ge(sem, value)


def gated_delta_moe(nc, x, w_qkvz, w_ab, w_out, conv_w, dt_bias, a_log, head_w, ffn_w, w_router, w12, out):
    ctx = ExitStack()
    with ctx:
        def sem(name):
            return ctx.enter_context(nc.semaphore(name))

        def sb(name, *dims, dt=F32):
            t = ctx.enter_context(nc.sbuf_tensor(name, [P] + list(dims), dt))
            return t[(slice(None),) * (len(dims) + 1)]

        base = nc.dram_tensor("base", (T, DIM), F32).ap()

        xt = sb("xt", KD, T)
        wc = sb("wc", NB, EV)
        ident = sb("ident", P)
        small = sb("small", 24, 32)

        UP, PAIR = KD * 2 * 2 * I, KD * 2 * 2 * I + 2 * DIM
        arena = sb("arena", PAIRS * PAIR)
        used = [0]

        def carve(*dims):
            n = 1
            for d in dims:
                n *= d
            a = arena[:, used[0]:used[0] + n]
            used[0] += n
            assert used[0] <= PAIRS * PAIR
            names = "abcd"[:len(dims)]
            return a.rearrange(f"p ({' '.join(names)}) -> p {' '.join(names)}", **dict(zip(names, dims))) if len(dims) > 1 else a

        hist = carve(CT, TAPS - 1 + P)
        conv = carve(2, 4, P)
        ctmp = carve(2, 4, P)
        qk = carve(2, G, P)
        vt = carve(UT, P)
        vbd = carve(G, NC, P)
        early = used[0] // PAIR
        am = carve(LV, G, P)
        kbd = carve(G, NC, P)
        qbd = carve(G, NC, P)
        tt = carve(2, G, P)
        stepped = used[0] // PAIR
        zg = carve(UT, P)
        scratch_end = used[0]
        wqz = carve(KD, CH)
        wo = carve(UT, DIM)
        parts = ((0, early), (early, stepped), (stepped, PAIRS))

        tn = sb("tn", G, P)
        pp = sb("pp", G, P)
        aq = sb("aq", 2, G, P)
        kh = sb("kh", 2, G, P)
        vx = sb("vx", 2, G, P)
        state = sb("state", G, P)
        rhs = sb("rhs", G, P)
        uu = sb("uu", G, P)
        up = sb("up", G, P)
        oo = sb("oo", 2, G, P)
        osq = sb("osq", G, P)
        osel = sb("osel", G, 2 * C)
        yraw = sb("yraw", UT, P)
        yt = sb("yt", UT, P)
        sqb = sb("sqb", 2 * G, P)
        gm = sb("gm", NC * G, C)
        kqc = sb("kqc", 2, 2, G, C)
        qks = sb("qks", NC, 2, G, C)
        prm = sb("prm", NB, 6, NC * G)
        F_HP, F_SV, F_RQ, F_RQ2, F_D, F_DC, F_END = 24, 40, 44, 48, 52, 180, 308
        nxt = sb("nxt", NC, F_END)
        cur = sb("cur", NC, F_END)
        wab = sb("wab", KD, 2 * NV)
        cw = sb("cw", CT, TAPS)
        fw = sb("fw", DIM)
        wr = sb("wr", KD, E)
        hw = sb("hw", 1)
        dtb = sb("dtb", NV)
        alg = sb("alg", NV)
        xin = sb("xin", DIM)
        row = sb("row", 4, DIM)
        htb = sb("htb", KD, P)
        rt = sb("rt", 5, E)
        idx = sb("idx", 8, dt=U32)
        iota = sb("iota", E)
        wcb = sb("wcb", EV)

        blk1 = sb("blk1", P)
        gt = sb("gt", P)
        le = sb("le", P)
        lvm = sb("lvm", LV, P)
        ind4 = sb("ind4", 4)
        rsel = sb("rsel", 2, 2, DH)
        parind = sb("parind", 2)
        le32 = sb("le32", C)
        eq32 = sb("eq32", C)
        sel = sb("sel", 2, C)
        rmask = sb("rmask", 2)
        mhalf = sb("mhalf", 32)

        th, ea, eat = aq, kh, vx

        NBV = NB * NV
        place = [0]

        def scratch(n):
            place[0] += n
            assert place[0] <= scratch_end
            return arena[:, place[0] - n:place[0]]

        xc = scratch(NB * DIM).rearrange("p (b d) -> p b d", b=NB)
        beta_tok = scratch(2 * NBV).rearrange("p (k b h) -> p k b h", k=2, b=NB)
        pt = scratch(4 * NBV).rearrange("p (k b h) -> p k b h", k=4, b=NB)
        xsq = scratch(NB * DIM)
        xall = scratch(NB * DIM).rearrange("p (b d) -> p b d", b=NB)

        ps = [ctx.enter_context(nc.psum_tensor(f"ps{n}", [P, 512], F32)) for n in range(8)]
        BA, BB, BQ, BP, BT, BTT, BS, BO = (t[:, :] for t in ps)
        banks = [BA, BB, BQ, BP, BT, BTT, BS, BO]

        def tiles(bank):
            return bank.rearrange("p (g j) -> p g j", g=4)

        s_in, s_w, s_cst, s_pool, s_vch, s_ech = (sem(n) for n in (
            "inputs_loaded", "weights_loaded", "constants_ready", "pool_steps", "vector_steps", "expert_steps"))
        s_ew = [sem(f"experts_loaded_{k}") for k in range(3)]
        S = {n: sem(n) for n in (
            "xc_out", "xsq_out", "xn_out", "xt_t", "xt_out", "ab_mm", "beta_tanh", "sp_in", "sp_exp", "sp_ln", "alog_exp",
            "gate_out", "ghi_mm", "ghi_out", "sum_mm", "sum_exp",
            "proj_mm", "hist_in", "conv_out", "tanh_out", "silu_out", "hist_moved", "queries_in", "keys_in", "values_in", "cur_in",
            "sq_out", "ss_mm", "ss_out", "hi_mm", "qk_in", "qk_pow", "decay_rhs", "decay_mm", "decay_exp",
            "beta_rhs", "beta_mm", "params_out",
            "kh_t", "kh_out", "vx_t", "vx_out", "kq_mm", "kq_out", "mask_out", "last_mask_out", "qmask_out",
            "first_out", "first_t", "first_in", "p_mm", "p_out", "t_mm", "t_out", "tt_mm", "tt_out",
            "ks_mm", "qs_mm", "qs_used", "rhs_out", "sdec_out", "v_mm", "v_out", "w_mm", "w_out", "u_mm", "u_out", "up_out", "au_mm", "o_out",
            "osq_out", "osq_used", "ku_mm", "s_out", "norm_in", "norm_pow", "osel_out", "y_mm", "y_out",
            "z_mm", "z_tanh", "z_out", "yt_out", "op_mm", "x_in", "x2_out", "ln_in", "ln_pow", "rms_in", "rms_pow",
            "h_out", "base_out", "base_stored", "h_t", "htb_in", "ht_out", "rt_mm", "rt_in", "rt_exp", "wc_out",
            "base_in", "hb_in", "h1_mm", "h1_tanh", "act_out", "act_t", "act_in", "moe_mm", "fin_out", "stored")}

        def run(b, inverse, prepare, step, late, spread, front, tail, first=False, last=False, end=False):
            for c in range(NC):
                n = b * NC + c
                for stage in STAGES:
                    if not end:
                        inverse(n, c, stage)
                    if not end and not (last and c == NC - 1):
                        prepare(n + 1, (c + 1) % NC, stage)
                    if not (first and c == 0) and not (end and c > 0):
                        step(b, n - 1, (c - 1) % NC, stage)
                    if not (first and c < 2) and not (end and c > 1):
                        late(b, n - 2, (c - 2) % NC, stage)
                    for ahead, k, what in SPREAD_AT.get((c, stage), ()):
                        if (ahead == 0 and not end) or (ahead == 1 and not last and not end):
                            spread(b + ahead, k, what)
                    if not last and not end:
                        front(b + 1, (c, stage))
                    if not first:
                        tail(b - 1, (c, stage))

        def run_all(engine, *parts):
            prepare, spread, front = parts[1], parts[4], parts[5]
            for c in range(NC):
                for stage in STAGES:
                    front(0, (c, stage))
            for k in range(2):
                for what in ("queries", "keys", "values", "commit"):
                    spread(0, k, what)
            for stage in STAGES:
                prepare(0, 0, stage)
            run(0, *parts, first=True)
            run(1, *parts)
            with engine.Fori(2, NB - 1) as b:
                run(b, *parts)
            run(NB - 1, *parts, last=True)
            run(NB, *parts, end=True)

        def nothing(*_):
            pass

        block = ctx.enter_context(nc.Block())

        @block.sync
        def _(sp):
            sp.dma_start(xall, x.rearrange("(b p) d -> p b d", p=P)).then_inc(s_in, 16)
            for dst, src in ((wab, w_ab), (dtb, dt_bias), (alg, a_log)):
                sp.dma_start(dst, src).then_inc(s_in, 16)
            for dst, src in ((wqz, w_qkvz), (cw, conv_w), (wo, w_out), (hw, head_w), (fw, ffn_w), (wr, w_router)):
                sp.dma_start(dst, src).then_inc(s_w, 16)
            sp.dma_start(xin, x[0:P, :]).then_inc(S["x_in"], 16)

            def store_base(b):
                sp.wait_ge(S["base_out"], b + 1)
                sp.dma_start(base[bass.ts(b, P), :], row[:, 3, :]).then_inc(S["base_stored"], 16)

            with sp.Fori(0, NB - 1) as b:
                sp.wait_ge(S["x2_out"], b + 1)
                sp.dma_start(xin, x[bass.ts(b + 1, P), :]).then_inc(S["x_in"], 16)
                store_base(b)
            def load_experts(k):
                lo, hi = parts[k][0] * PAIR, parts[k][1] * PAIR
                sp.dma_start(arena[:, lo:hi], w12[:, lo:hi]).then_inc(s_ew[k], 16)

            for name in ("queries_in", "keys_in", "vx_t"):
                sp.wait_ge(S[name], NB * NC)
            sp.wait_ge(S["hist_moved"], NB)
            load_experts(0)
            for name in ("u_mm", "qs_mm", "kh_t"):
                sp.wait_ge(S[name], NB * NC)
            load_experts(1)
            sp.wait_ge(S["yt_out"], 2 * NB)
            sp.wait_ge(S["op_mm"], NB)
            load_experts(2)
            store_base(NB - 1)
            sp.wait_ge(S["base_stored"], 16 * NB)
            sp.dma_start(xin, base[0:P, :]).then_inc(S["base_in"], 16)

            def store(b):
                sp.wait_ge(S["fin_out"], b + 1)
                sp.dma_start(out[bass.ts(b, P), :], row[:, 0, :]).then_inc(S["stored"], 16)

            with sp.Fori(0, NB - 1) as b:
                store(b)
                sp.dma_start(xin, base[bass.ts(b + 1, P), :]).then_inc(S["base_in"], 16)
            store(NB - 1)
            sp.wait_ge(S["stored"], 16 * NB)

        @block.gpsimd
        def _(pool):
            g = nc.gpsimd
            steps = [0]

            def build(ins):
                steps[0] += 1
                ins.then_inc(s_pool, 1)
                pool.wait_ge(s_pool, steps[0])

            def keep(ap, pattern, base, mult):
                build(g.affine_select(out=ap, in_=ap, pattern=pattern, compare_op=ALU.is_ge, fill=0.0,
                                      base=base, channel_multiplier=mult))

            build(g.memset(ident, 0.0))
            build(g.affine_select(out=ident, in_=ident, pattern=[[-1, P]], compare_op=ALU.not_equal,
                                  fill=1.0, base=0, channel_multiplier=1))
            build(g.memset(blk1, 1.0))
            keep(blk1, [[-C, 4], [0, C]], 0, 1)
            keep(blk1, [[C, 4], [0, C]], C - 1, -1)
            for m, base_, mult in ((gt, -1, 1), (le, 0, -1)):
                build(g.tensor_copy(m, blk1))
                keep(m, [[-mult, P]], base_, mult)
            build(g.memset(lvm, 0.0))
            for l in range(LV):
                b = 1 << l
                half = lvm[:, l, :].rearrange("p (n two b) -> p n two b", two=2, b=b)[:, :, 1, :]
                build(g.memset(half, 1.0))
                keep(half, [[-2 * b, P // (2 * b)], [0, b]], 0, 1)
                keep(half, [[2 * b, P // (2 * b)], [0, b]], b - 1, -1)
            build(g.memset(parind, 1.0))
            keep(parind, [[-DH, 2]], 0, 1)
            keep(parind, [[DH, 2]], DH - 1, -1)
            build(g.iota(iota, pattern=[[1, E]], base=0, channel_multiplier=0, allow_small_or_imprecise_dtypes=True))
            build(g.memset(mhalf, -0.5))
            build(g.memset(state, 0.0))
            g.memset(wc[:, :, E:EV], 0.5).then_inc(s_cst, 1)
            pool.wait_ge(S["xn_out"], 1)
            for z in (kbd, qbd, vbd):
                build(g.memset(z, 0.0))
            pool.wait_ge(S["xt_t"], NB // 2)
            g.memset(hist[:, :, 0:TAPS - 1], 0.0).then_inc(s_cst, 1)

            def power(out_, in_, name):
                g.tensor_tensor(out_, in_, mhalf[:, 0:in_.shape[1]], ALU.pow).then_inc(S[name], 1)

            def mask(n, c, l):
                if l == 0:
                    pool.wait_ge(S["kq_out"], n + 1)
                    wait(pool, S["first_out"], n)
                elif l == LI:
                    wait(pool, S["w_mm"], n)
                elif not isinstance(n, int) or n > 0:
                    pool.wait_ge(S["p_mm"], (n - 1) * (LI - 1) + l)
                g.tensor_tensor(am[:, l, :, :].rearrange("p g (h i) -> p g h i", i=C),
                                kqc[:, c % 2, 1, :, :].unsqueeze(2).broadcast_to([P, G, 4, C]),
                                lvm[:, l, :].rearrange("p (h i) -> p h i", i=C).unsqueeze(1).broadcast_to([P, G, 4, C]),
                                ALU.mult).then_inc(S["last_mask_out" if l == LI else "mask_out"], 1)

            def prepare(n, c, stage):
                for l, when in enumerate(("t2", "turn", "grow", "first")):
                    if stage == when:
                        mask(n, c, l)
                if stage == "out":
                    wait(pool, S["au_mm"], n - 1)
                    g.tensor_tensor(aq[:, c % 2, :, :].rearrange("p g (h i) -> p g h i", i=C),
                                    kqc[:, c % 2, 0, :, :].unsqueeze(2).broadcast_to([P, G, 4, C]),
                                    le.rearrange("p (h i) -> p h i", i=C).unsqueeze(1).broadcast_to([P, G, 4, C]),
                                    ALU.mult).then_inc(S["qmask_out"], 1)

            def inverse(n, c, stage):
                if stage == "weigh":
                    mask(n, c, LI)

            def step(b, n, c, stage):
                if stage == "query":
                    pool.wait_ge(S["cur_in"], n + 1)
                    pool.wait_ge(S["ks_mm"], n + 1)
                    pool.wait_ge(S["qs_mm"], n + 1)
                    wait(pool, S["s_out"], n)
                    s4 = state.rearrange("p g (r d) -> p g r d", r=2)
                    for r in range(2):
                        g.tensor_tensor(s4[:, :, r, :], s4[:, :, r, :],
                                        cur[:, c, (4 + r) * G:(5 + r) * G].unsqueeze(2).broadcast_to([P, G, DH]),
                                        ALU.mult).then_inc(S["sdec_out"], 1)
                if stage == "settle":
                    pool.wait_ge(S["u_out"], n + 1)
                    wait(pool, S["ku_mm"], n)
                    g.tensor_tensor(up, uu, cur[:, c, 3 * G:4 * G].unsqueeze(2).broadcast_to([P, G, P]),
                                    ALU.mult).then_inc(S["up_out"], 1)
                if stage == "write":
                    pool.wait_ge(S["o_out"], n + 1)
                    wait(pool, S["osq_used"], n)
                    g.tensor_tensor(osq, oo[:, c % 2, :, :], oo[:, c % 2, :, :], ALU.mult).then_inc(S["osq_out"], 1)
                if stage == "read":
                    pool.wait_ge(S["norm_in"], n + 1)
                    power(small[:, 11, 0:G], small[:, 10, 0:G], "norm_pow")

            def front(f, at):
                if at == (1, "t2"):
                    pool.wait_ge(S["qk_in"], f + 1)
                    power(small[:, 7, :], small[:, 6, :], "qk_pow")

            def tail(t, at):
                if at == (2, "query"):
                    pool.wait_ge(S["ln_in"], t + 1)
                    power(small[:, 18, 0:1], small[:, 19, 0:1], "ln_pow")
                if at == (2, "solve"):
                    pool.wait_ge(S["rms_in"], t + 1)
                    power(small[:, 20, 0:1], small[:, 21, 0:1], "rms_pow")

            run_all(pool, inverse, prepare, step, nothing, nothing, front, tail)

        @block.scalar
        def _(act):
            a = nc.scalar
            act.wait_ge(s_in, 64)
            a.activation(alg, alg, ACT.Exp).then_inc(S["alog_exp"], 1)
            act.wait_ge(S["xc_out"], 1)
            a.activation(xsq, xc.rearrange("p b d -> p (b d)"), ACT.Square).then_inc(S["xsq_out"], 1)
            for n in range(NB // 2):
                act.wait_ge(S["xt_t"], n + 1)
                a.activation(xt[:, :, 2 * P * n:2 * P * (n + 1)], banks[n].rearrange("p (k t) -> p k t", k=KD),
                             ACT.Copy).then_inc(S["xt_out"], 1)
            act.wait_ge(S["ab_mm"], 1)
            ab = BA.rearrange("p (b kh) -> p b kh", b=NB)
            a.activation(beta_tok[:, 1, :, :], ab[:, :, 0:NV], ACT.Tanh, scale=0.5).then_inc(S["beta_tanh"], 1)
            act.wait_ge(S["sp_in"], 1)
            a.activation(pt[:, 1, :, :], pt[:, 0, :, :], ACT.Exp).then_inc(S["sp_exp"], 1)
            act.wait_ge(S["sp_exp"], 1)
            a.activation(pt[:, 2, :, :], pt[:, 1, :, :], ACT.Ln, bias=1.0).then_inc(S["sp_ln"], 1)
            act.wait_ge(S["sum_mm"], 1)
            for k in range(4):
                a.activation(prm[:, :, 2 + k, :].rearrange("p b (c g) -> p c b g", c=NC),
                             banks[4 + k][:, 0:NBV].rearrange("p (c b g) -> p c b g", c=NC, b=NB),
                             ACT.Exp).then_inc(S["sum_exp"], 1)
            act.wait_ge(s_cst, 2)

            def prepare(n, c, stage):
                if stage == "first":
                    act.wait_ge(S["first_t"], n + 1)
                    wait(act, S["p_mm"], n * (LI - 1))
                    a.activation(tn, tiles(BT), ACT.Copy).then_inc(S["first_in"], 1)
                if stage == "lay":
                    act.wait_ge(S["kh_t"], n + 1)
                    wait(act, S["ku_mm"], n - 1)
                    a.activation(kh[:, c % 2, :, :], tiles(BO), ACT.Copy).then_inc(S["kh_out"], 1)

            def inverse(n, c, stage):
                if stage in ("p1", "p2", "p3"):
                    m = n * (LI - 1) + int(stage[1])
                    act.wait_ge(S["p_mm"], m)
                    wait(act, S["tt_mm"], m - 1)
                    a.activation(pp, tiles(BP), ACT.Copy).then_inc(S["p_out"], 1)

            def step(b, n, c, stage):
                if stage == "solve":
                    act.wait_ge(S["v_mm"], n + 1)
                    wait(act, S["au_mm"], n)
                    wait(act, S["up_out"], n)
                    a.activation(uu, tiles(BS), ACT.Copy).then_inc(S["v_out"], 1)
                if stage == "weigh":
                    act.wait_ge(S["w_mm"], n + 1)
                    a.activation(rhs, tiles(BT), ACT.Copy).then_inc(S["w_out"], 1)

            def late(b, n, c, stage):
                if stage == "t1":
                    act.wait_ge(S["y_mm"], n + 1)
                    if c == 0:
                        wait(act, S["yt_out"], 2 * b)
                    a.activation(yraw[:, :, C * c:C * (c + 1)], BQ[:, 0:2 * P].rearrange("p (u i) -> p u i", u=UT),
                                 ACT.Copy).then_inc(S["y_out"], 1)

            def spread(blk, c, what):
                n = blk * NC + c
                if what == "commit":
                    act.wait_ge(S["params_out"], blk + 1)
                    wait(act, S["osel_out"], n - 3)
                    wait(act, S["up_out"], n - 3)
                    wait(act, S["kq_out"], n - 3)
                    a.activation(cur[:, c, :], nxt[:, c, :], ACT.Copy).then_inc(S["cur_in"], 1)
                    return
                act.wait_ge(S["silu_out"], blk * 4 + 4)
                cs = slice(C * c, C * (c + 1))
                if what == "values":
                    wait(act, S["vx_t"], n - 3)
                    for r in range(2):
                        rows = slice(DH * r, DH * r + DH)
                        ins = a.activation(vbd[rows, :, c, :].rearrange("p g (par r i) -> p g par r i", r=2, i=C)[:, :, :, r, :],
                                           vt[rows, :, cs].rearrange("p (g par) i -> p g par i", par=2), ACT.Copy)
                    ins.then_inc(S["values_in"], 1)
                    return
                for name in ("kq_mm", "ks_mm", "kh_t") if what == "keys" else ("qs_mm",):
                    wait(act, S[name], n - 3)
                kind, dst = (1, kbd) if what == "keys" else (0, qbd)
                if what == "keys":
                    a.activation(qks[:, c, :, :, :], qk[:, :, :, cs], ACT.Copy)
                for par in range(2):
                    rows = slice(DH * par, DH * par + DH)
                    ins = a.activation(dst[rows, :, c, :].rearrange("p g (h i) -> p g h i", i=C)[:, :, 2 * par:2 * par + 2, :],
                                       qk[rows, kind, :, cs].unsqueeze(2).broadcast_to([DH, G, 2, C]), ACT.Copy)
                ins.then_inc(S[what + "_in"], 1)

            def front(f, at):
                for n in range(4):
                    if at == PROJECT_AT[n]:
                        act.wait_ge(S["proj_mm"], f * 4 + n + 1)
                        if n == 0:
                            wait(act, S["conv_out"], f * 4)
                            wait(act, S["hist_moved"], f)
                        a.activation(hist[:, 4 * n:4 * n + 4, TAPS - 1:TAPS - 1 + P], tiles((BA, BB)[n % 2]),
                                     ACT.Copy).then_inc(S["hist_in"], 1)
                    if at == TANH_AT[n]:
                        act.wait_ge(S["conv_out"], f * 4 + n + 1)
                        wait(act, S["silu_out"], f * 4 + n - 1)
                        a.activation(ctmp[:, n % 2, :, :], conv[:, n % 2, :, :], ACT.Tanh, scale=0.5).then_inc(S["tanh_out"], 1)
                if at == (1, "query"):
                    act.wait_ge(S["silu_out"], f * 4 + 2)
                    wait(act, S["ss_mm"], f)
                    a.activation(sqb, qk.rearrange("p k g t -> p (k g) t"), ACT.Square).then_inc(S["sq_out"], 1)
                if at == (1, "t3"):
                    act.wait_ge(S["conv_out"], f * 4 + 4)
                    act.wait_ge(S["hist_in"], f * 4 + 4)
                    a.activation(hist[:, :, 0:TAPS - 1], hist[:, :, P:P + TAPS - 1], ACT.Copy).then_inc(S["hist_moved"], 1)
                if at == (1, "t2"):
                    act.wait_ge(S["decay_mm"], f + 1)
                    wait(act, S["cur_in"], f * NC)
                    a.activation(nxt[:, :, F_D:F_DC], BA.rearrange("p (c x) -> p c x", c=NC), ACT.Exp).then_inc(S["decay_exp"], 1)

            def tail(t, at):
                for n, when in enumerate(((0, "t2"), (0, "p3"))):
                    if at == when:
                        act.wait_ge(S["z_mm"], t * 2 + n + 1)
                        wait(act, S["yt_out"], t * 2)
                        a.activation(zg[:, 4 * n:4 * n + 4, :], tiles((BA, BB)[n]), ACT.Tanh, scale=0.5).then_inc(S["z_tanh"], 1)
                if at == (2, "t2"):
                    act.wait_ge(S["h_t"], t + 1)
                    a.activation(htb, BA[:, 0:DIM].rearrange("p (k t) -> p k t", k=KD), ACT.Copy).then_inc(S["htb_in"], 1)
                if at == (2, "weigh"):
                    act.wait_ge(S["htb_in"], t + 1)
                    a.activation(small[:, 23, 2:3], iota[:, 0:1], ACT.Copy)
                    a.activation(xt[:, :, bass.ts(t, P)], htb, ACT.Copy).then_inc(S["ht_out"], 1)
                if at == (2, "t3"):
                    act.wait_ge(S["rt_in"], t + 1)
                    a.activation(rt[:, 1, :], rt[:, 0, :], ACT.Exp, bias=small[:, 14, 0:1],
                                 accum_out=small[:, 15, 0:1]).then_inc(S["rt_exp"], 1)

            run_all(act, inverse, prepare, step, late, spread, front, tail)

            def gate(n, p, later):
                act.wait_ge(S["h1_mm"], n + 1)
                if later or p > 1:
                    act.wait_ge(S["act_out"], n if p == 0 else n - 1)
                a.activation(th[:, p % 2, 0:2, :], (BA, BB)[p % 2].rearrange("p (e k i) -> p e k i", e=2, k=2)[:, :, 0, :],
                             ACT.Tanh, scale=0.5).then_inc(S["h1_tanh"], 1)

            def turned(n, p, later):
                act.wait_ge(S["act_t"], n + 1)
                if later or p > 1:
                    act.wait_ge(S["moe_mm"], n if p == 0 else n - 1)
                a.activation(eat[:, p % 2, 0:2, :], (BQ, BP)[p % 2][:, 0:2 * P].rearrange("p (e t) -> p e t", e=2),
                             ACT.Copy).then_inc(S["act_in"], 1)

            def experts(b, later):
                if later:
                    act.wait_ge(S["h1_mm"], b * PAIRS)
                act.wait_ge(s_cst, 2)
                a.activation(htb, xt[:, :, bass.ts(b, P)], ACT.Copy).then_inc(S["hb_in"], 1)
                gate(b * PAIRS, 0, later)
                for p in range(PAIRS):
                    if p + 1 < PAIRS:
                        gate(b * PAIRS + p + 1, p + 1, later)
                    turned(b * PAIRS + p, p, later)

            act.wait_ge(S["rt_mm"], NB)
            act.wait_ge(S["wc_out"], NB)
            act.wait_ge(S["ht_out"], NB)
            experts(0, False)
            with act.Fori(1, NB) as b:
                experts(b, True)

        @block.vector
        def _(dve):
            v = nc.vector
            ch = Chain(dve, s_vch)
            done = ch.done

            def hold():
                v.tensor_copy(small[:, 23, 0:1], iota[:, 0:1])

            def rsqrt(y, value, tmp, half):
                done(v.tensor_scalar(tmp.bitcast(I32), value.bitcast(I32), 1, None, ALU.logical_shift_right))
                done(v.tensor_scalar(y.bitcast(I32), tmp.bitcast(I32), -1.0, float(MAGIC), ALU.mult, ALU.add))
                done(v.tensor_scalar(half, value, -0.5, None, ALU.mult))
                for _ in range(3):
                    done(v.tensor_tensor(tmp, y, y, ALU.mult))
                    done(v.tensor_tensor(tmp, tmp, half, ALU.mult))
                    done(v.scalar_tensor_tensor(out=y, in0=tmp, scalar=1.5, in1=y, op0=ALU.add, op1=ALU.mult))

            dve.wait_ge(s_cst, 1)
            v.tensor_reduce(eq32, ident.rearrange("p (h i) -> p i h", i=C), X, ALU.add)
            v.tensor_reduce(le32, le.rearrange("p (h i) -> p i h", i=C), X, ALU.add)
            idv = ident.rearrange("p (a r i) -> p a r i", a=2, r=2)
            v.tensor_tensor(sel, idv[:, :, 0, :], idv[:, :, 1, :], ALU.add)
            done(v.tensor_reduce(ind4, blk1.rearrange("p (h i) -> p h i", i=C), X, ALU.add))
            done(v.tensor_scalar(ind4, ind4, 1.0 / C, None, ALU.mult))
            v.tensor_tensor(rmask, ind4[:, 0:2], ind4[:, 2:4], ALU.add)
            for r in range(2):
                done(v.tensor_copy(rsel[:, r, :, :], ind4.rearrange("p (a r) -> p a r", r=2)[:, :, r].unsqueeze(2).broadcast_to([P, 2, DH])))
            dve.wait_ge(s_in, 64)
            mean, var, rstd, t0, t1 = (small[:, k, 0:NB] for k in range(5))
            done(v.tensor_reduce(mean, xall, X, ALU.add))
            done(v.tensor_scalar(mean, mean, 1.0 / DIM, None, ALU.mult))
            v.tensor_tensor(xc, xall, mean.unsqueeze(2).broadcast_to([P, NB, DIM]), ALU.subtract).then_inc(S["xc_out"], 1)
            dve.wait_ge(S["xsq_out"], 1)
            done(v.tensor_reduce(var, xsq.rearrange("p (b d) -> p b d", b=NB), X, ALU.add))
            done(v.tensor_scalar(var, var, 1.0 / DIM, LN_EPS, ALU.mult, ALU.add))
            rsqrt(rstd, var, t0, t1)
            v.tensor_tensor(xc, xc, rstd.unsqueeze(2).broadcast_to([P, NB, DIM]), ALU.mult).then_inc(S["xn_out"], 1)
            dve.wait_ge(S["ab_mm"], 1)
            dve.wait_ge(S["beta_tanh"], 1)
            ab = BA.rearrange("p (b kh) -> p b kh", b=NB)
            za, zn = pt[:, 3, :, :], pt[:, 0, :, :]
            done(v.tensor_tensor(za, ab[:, :, NV:2 * NV], dtb.unsqueeze(1).broadcast_to([P, NB, NV]), ALU.add))
            done(v.tensor_scalar(zn, za, -1.0, None, ALU.mult))
            v.tensor_tensor(zn, zn, za, ALU.min).then_inc(S["sp_in"], 1)
            done(v.tensor_scalar(beta_tok[:, 1, :, :], beta_tok[:, 1, :, :], 0.5, 0.5, ALU.mult, ALU.add))
            dve.wait_ge(S["sp_ln"], 1)
            done(v.scalar_tensor_tensor(out=za, in0=za, scalar=0.0, in1=pt[:, 2, :, :], op0=ALU.max, op1=ALU.add))
            dve.wait_ge(S["alog_exp"], 1)
            done(v.tensor_scalar(alg, alg, -1.0, None, ALU.mult))
            v.tensor_tensor(beta_tok[:, 0, :, :], za, alg.unsqueeze(1).broadcast_to([P, NB, NV]), ALU.mult).then_inc(S["gate_out"], 1)
            dve.wait_ge(S["ghi_mm"], 1)
            for k in range(2):
                v.tensor_copy(prm[:, :, k, :].rearrange("p b (c g) -> p c b g", c=NC),
                              BB.rearrange("p (c k b g) -> p c k b g", c=NC, k=2, b=NB)[:, :, k, :, :]).then_inc(S["ghi_out"], 1)
            dve.wait_ge(s_w, 96)
            done(v.tensor_scalar(hw, hw, 0.5, None, ALU.mult))
            done(v.tensor_scalar(wo, wo, hw, None, ALU.mult))
            dve.wait_ge(S["sum_exp"], 4)
            dve.wait_ge(S["ghi_out"], 2)
            dve.wait_ge(s_cst, 2)

            def conv_taps(f, n, tap):
                if tap == TAPS - 1:
                    dve.wait_ge(S["hist_in"], f * 4 + n + 1)
                    wait(dve, S["silu_out"], f * 4 + n - 1)
                for k in range(4):
                    t = 4 * n + k
                    src, w, acc = hist[:, t, tap:tap + P], cw[:, t, tap:tap + 1], conv[:, n % 2, k, :]
                    if tap == TAPS - 1:
                        ins = v.tensor_scalar(acc, src, w, None, ALU.mult)
                    else:
                        ins = v.scalar_tensor_tensor(out=acc, in0=src, scalar=w, in1=acc, op0=ALU.mult, op1=ALU.add)
                if tap:
                    done(ins)
                else:
                    ins.then_inc(S["conv_out"], 1)

            def front(f, at):
                for n in range(4):
                    for k in range(TAPS):
                        if at == TAP_AT[n][k]:
                            conv_taps(f, n, TAPS - 1 - k)
                    if at == SILU_AT[n]:
                        dve.wait_ge(S["conv_out"], f * 4 + n + 1)
                        dve.wait_ge(S["tanh_out"], f * 4 + n + 1)
                        for name in ("queries_in", "keys_in") if n < 2 else ("values_in",):
                            wait(dve, S[name], f * NC)
                        if n < 2:
                            wait(dve, S["sq_out"], f)
                        dst = qk[:, n, :, :] if n < 2 else vt[:, 4 * (n - 2):4 * (n - 1), :]
                        v.scalar_tensor_tensor(out=dst, in0=ctmp[:, n % 2, :, :], scalar=1.0, in1=conv[:, n % 2, :, :],
                                               op0=ALU.add, op1=ALU.mult).then_inc(S["silu_out"], 1)
                cg = "p (c g) -> p c g"
                if at == (1, "t1"):
                    wait(dve, S["cur_in"], f * NC)
                    wait(dve, S["beta_mm"], f)
                    hold()
                    done(v.tensor_copy(nxt[:, :, 0:F_HP].rearrange("p c (k g) -> p k c g", g=G),
                                       prm[:, f, :, :].rearrange("p k (c g) -> p k c g", c=NC)))
                    v.tensor_tensor(gm.rearrange("p (c g) i -> p c g i", c=NC),
                                    le32.unsqueeze(1).unsqueeze(1).broadcast_to([P, NC, G, C]),
                                    nxt[:, :, 0:G].unsqueeze(3).broadcast_to([P, NC, G, C]), ALU.mult).then_inc(S["decay_rhs"], 1)
                if at == (1, "solve"):
                    dve.wait_ge(S["ss_mm"], f + 1)
                    v.tensor_copy(small[:, 5, 0:16], BB[:, 0:16]).then_inc(S["ss_out"], 1)
                if at == (1, "keys"):
                    dve.wait_ge(S["hi_mm"], f + 1)
                    v.tensor_scalar(small[:, 6, :], BB[:, 0:32], 4 * EPS, None, ALU.add).then_inc(S["qk_in"], 1)
                rq, rk, ck = small[:, 7, 0:16], small[:, 7, 16:32], small[:, 9, 0:16]
                if at == (1, "p3"):
                    dve.wait_ge(S["qk_pow"], f + 1)
                    v.tensor_scalar(nxt[:, :, F_RQ:F_RQ + G], rq.rearrange(cg, c=NC), DH ** -0.5, None, ALU.mult)
                    v.tensor_tensor(nxt[:, :, F_RQ2:F_RQ2 + G], rq.rearrange(cg, c=NC), rq.rearrange(cg, c=NC), ALU.mult)
                    done(v.tensor_tensor(nxt[:, :, F_SV:F_SV + G], nxt[:, :, G:2 * G], rk.rearrange(cg, c=NC), ALU.mult))
                    done(v.tensor_tensor(ck.rearrange(cg, c=NC), nxt[:, :, F_SV:F_SV + G], rk.rearrange(cg, c=NC), ALU.mult))
                    v.tensor_scalar(nxt[:, :, F_SV:F_SV + G], nxt[:, :, F_SV:F_SV + G], 0.5, None, ALU.mult)
                    dve.wait_ge(S["decay_mm"], f + 1)
                    v.tensor_tensor(gm, eq32.unsqueeze(1).broadcast_to([P, NC * G, C]),
                                         ck.unsqueeze(2).broadcast_to([P, NC * G, C]), ALU.mult).then_inc(S["beta_rhs"], 1)
                if at == (1, "write"):
                    v.tensor_scalar(nxt[:, :, F_RQ2:F_RQ2 + G], nxt[:, :, F_RQ2:F_RQ2 + G], 1.0 / DH / DH, None, ALU.mult)
                    for r in range(2):
                        eg = nxt[:, :, 2 * G:3 * G]
                        hp = nxt[:, :, F_HP:F_SV].rearrange("p c (k g r) -> p c k g r", k=2, g=G)
                        v.tensor_scalar(hp[:, :, 1, :, r], eg, rmask[:, r:r + 1], None, ALU.mult)
                        done(v.tensor_scalar(hp[:, :, 0, :, r], eg, rmask[:, r:r + 1], -1.0, ALU.mult, ALU.mult))
                        done(v.tensor_tensor(hp[:, :, 0, :, r], hp[:, :, 0, :, r], ck.rearrange(cg, c=NC), ALU.mult))
                if at == (2, "p1"):
                    dve.wait_ge(S["beta_mm"], f + 1)
                    dve.wait_ge(S["decay_exp"], f + 1)
                    v.tensor_tensor(nxt[:, :, F_DC:F_END], nxt[:, :, F_D:F_DC], BB.rearrange("p (c x) -> p c x", c=NC),
                                    ALU.mult).then_inc(S["params_out"], 1)

            def prepare(n, c, stage):
                if stage == "keys":
                    kq = BQ[:, 0:2 * G * C].rearrange("p (g k i) -> p g k i", g=G, k=2)
                    dve.wait_ge(S["cur_in"], n + 1)
                    dve.wait_ge(S["kq_mm"], n + 1)
                    wait(dve, S["qmask_out"], n - 1)
                    wait(dve, S["mask_out"], (n - 1) * LI)
                    wait(dve, S["last_mask_out"], n - 1)
                    v.tensor_tensor(kqc[:, c % 2, 1, :, :], kq[:, :, 1, :], cur[:, c, F_DC:F_END].rearrange("p (g i) -> p g i", g=G), ALU.mult)
                    v.tensor_tensor(kqc[:, c % 2, 0, :, :], kq[:, :, 0, :], cur[:, c, F_D:F_DC].rearrange("p (g i) -> p g i", g=G),
                                    ALU.mult).then_inc(S["kq_out"], 1)
                if stage == "turn":
                    dve.wait_ge(S["vx_t"], n + 1)
                    wait(dve, S["rhs_out"], n - 1)
                    v.tensor_tensor(vx[:, c % 2, :, :], tiles(BQ), cur[:, c, F_SV:F_SV + G].unsqueeze(2).broadcast_to([P, G, P]),
                                    ALU.mult).then_inc(S["vx_out"], 1)
                if stage == "turn":
                    dve.wait_ge(S["mask_out"], n * LI + 1)
                    wait(dve, S["u_mm"], n - 1)
                    v.tensor_tensor(tt[:, c % 2, :, :], ident.unsqueeze(1).broadcast_to([P, G, P]), am[:, 0, :, :],
                                    ALU.subtract).then_inc(S["first_out"], 1)

            def heads(t):
                return t.rearrange("p g (r d) -> p g r d", r=2)

            def scale(c, k):
                return cur[:, c, F_HP + 2 * G * k:F_HP + 2 * G * (k + 1)].rearrange("p (g r) -> p g r", r=2) \
                    .unsqueeze(3).broadcast_to([P, G, 2, DH])

            def inverse(n, c, stage):
                if stage == "read":
                    dve.wait_ge(S["ks_mm"], n + 1)
                    wait(dve, S["u_mm"], n)
                    done(v.tensor_tensor(heads(rhs), heads(tiles(BS)), scale(c, 0), ALU.mult))
                    dve.wait_ge(S["vx_out"], n + 1)
                    v.tensor_tensor(rhs, rhs, vx[:, c % 2, :, :], ALU.add).then_inc(S["rhs_out"], 1)
                if stage in ("t1", "t2", "t3"):
                    l = int(stage[1])
                    if l < LI - 1:
                        dve.wait_ge(S["t_mm"], n * (LI - 2) + l)
                        dve.wait_ge(S["first_in"], n + 1)
                        if l > 1:
                            dve.wait_ge(S["t_out"], n * (LI - 2) + l - 1)
                        v.tensor_tensor(tn, tn, tiles(BT), ALU.subtract).then_inc(S["t_out"], 1)
                    dve.wait_ge(S["tt_mm"], n * (LI - 1) + l)
                    if l == 1:
                        dve.wait_ge(S["first_out"], n + 1)
                    else:
                        dve.wait_ge(S["tt_out"], n * (LI - 1) + l - 1)
                    v.tensor_tensor(tt[:, c % 2, :, :], tt[:, c % 2, :, :], tiles(BTT), ALU.subtract).then_inc(S["tt_out"], 1)

            def step(b, n, c, stage):
                o = oo[:, c % 2, :, :]
                nin, nout = small[:, 10, 0:G], small[:, 11, 0:G]
                if stage == "query":
                    dve.wait_ge(S["qs_mm"], n + 1)
                    wait(dve, S["y_mm"], n - 1)
                    wait(dve, S["osq_out"], n - 1)
                    v.tensor_tensor(heads(o), heads(tiles(BO)), scale(c, 1), ALU.mult).then_inc(S["qs_used"], 1)
                if stage == "settle":
                    dve.wait_ge(S["u_mm"], n + 1)
                    dve.wait_ge(S["w_mm"], n + 1)
                    dve.wait_ge(S["v_out"], n + 1)
                    v.tensor_tensor(uu, uu, tiles(BS), ALU.subtract).then_inc(S["u_out"], 1)
                if stage == "write":
                    dve.wait_ge(S["au_mm"], n + 1)
                    dve.wait_ge(S["qs_used"], n + 1)
                    v.tensor_tensor(o, o, tiles(BO), ALU.add).then_inc(S["o_out"], 1)
                if stage == "grow":
                    dve.wait_ge(S["ku_mm"], n + 1)
                    dve.wait_ge(S["sdec_out"], 2 * n + 2)
                    v.tensor_tensor(state, state, tiles(BS), ALU.add).then_inc(S["s_out"], 1)
                if stage == "lay":
                    dve.wait_ge(S["osq_out"], n + 1)
                    wait(dve, S["norm_pow"], n)
                    v.tensor_reduce(nin, osq, X, ALU.add).then_inc(S["osq_used"], 1)
                    dve.wait_ge(S["osq_used"], n + 1)
                    done(v.tensor_tensor(nin, nin, cur[:, c, F_RQ2:F_RQ2 + G], ALU.mult))
                    v.tensor_scalar(nin, nin, EPS, None, ALU.add).then_inc(S["norm_in"], 1)
                if stage == "out":
                    dve.wait_ge(S["norm_pow"], n + 1)
                    done(v.tensor_tensor(nout, nout, cur[:, c, F_RQ:F_RQ + G], ALU.mult))
                    wait(dve, S["y_mm"], n)
                    v.tensor_tensor(osel, sel.rearrange("p a i -> p (a i)").unsqueeze(1).broadcast_to([P, G, 2 * C]),
                                    nout.unsqueeze(2).broadcast_to([P, G, 2 * C]), ALU.mult).then_inc(S["osel_out"], 1)

            x2, xn, hh, bs = (row[:, k, :] for k in range(4))
            mean_, var_ = small[:, 17, 0:1], small[:, 17, 1:2]
            r1, v1, r2, v2 = (small[:, k, 0:1] for k in (18, 19, 20, 21))
            lg, pr, sc, acc, one = (rt[:, k, :] for k in range(5))
            mx, top, val, idf = small[:, 14, 0:1], small[:, 22, 0:8], small[:, 22, 8:16], small[:, 22, 16:24]
            psum_, pinv, wsum, winv = (small[:, 15, k:k + 1] for k in range(4))

            def tail(t, at):
                for n, when in enumerate(((0, "weigh"), (0, "settle"))):
                    if at == when:
                        dve.wait_ge(S["z_tanh"], t * 2 + n + 1)
                        zz = zg[:, 4 * n:4 * n + 4, :]
                        v.scalar_tensor_tensor(out=zz, in0=zz, scalar=1.0, in1=tiles((BA, BB)[n]), op0=ALU.add,
                                               op1=ALU.mult).then_inc(S["z_out"], 1)
                for n, when in enumerate(((1, "solve"), (1, "p2"))):
                    if at == when:
                        dve.wait_ge(S["z_out"], t * 2 + n + 1)
                        dve.wait_ge(S["y_out"], (t + 1) * NC)
                        wait(dve, S["op_mm"], t)
                        half = slice(4 * n, 4 * n + 4)
                        v.tensor_tensor(yt[:, half, :], zg[:, half, :], yraw[:, half, :], ALU.mult).then_inc(S["yt_out"], 1)
                if at == (1, "out"):
                    dve.wait_ge(S["op_mm"], t + 1)
                    dve.wait_ge(S["x_in"], 16 * (t + 1))
                    v.tensor_tensor(x2, xin, BA[:, 0:DIM], ALU.add).then_inc(S["x2_out"], 1)
                    dve.wait_ge(S["x2_out"], t + 1)
                    done(v.bn_stats(small[:, 16, 0:6], x2))
                    hold()
                    done(v.bn_aggr(small[:, 17, 0:2], small[:, 16, 0:6]))
                    v.tensor_scalar(v1, var_, LN_EPS, None, ALU.add).then_inc(S["ln_in"], 1)
                if at == (2, "t1"):
                    dve.wait_ge(S["ln_pow"], t + 1)
                    v.tensor_scalar(xn, x2, mean_, r1, ALU.subtract, ALU.mult)
                    done(v.tensor_tensor(v2, r1, r1, ALU.mult))
                    v.tensor_scalar(v2, v2, var_, EPS, ALU.mult, ALU.add).then_inc(S["rms_in"], 1)
                if at == (2, "keys"):
                    dve.wait_ge(S["rms_pow"], t + 1)
                    v.scalar_tensor_tensor(out=hh, in0=xn, scalar=r2, in1=fw, op0=ALU.mult, op1=ALU.mult).then_inc(S["h_out"], 1)
                    wait(dve, S["base_stored"], 16 * t)
                    v.tensor_tensor(bs, x2, xn, ALU.add).then_inc(S["base_out"], 1)
                if at == (2, "p3"):
                    dve.wait_ge(S["rt_mm"], t + 1)
                    done(v.tensor_copy(lg, BB[:, 0:E]))
                    done(v.tensor_reduce(mx, lg, X, ALU.max))
                    v.tensor_scalar(mx, mx, -1.0, None, ALU.mult).then_inc(S["rt_in"], 1)
                if at == (2, "write"):
                    dve.wait_ge(S["rt_exp"], t + 1)
                    done(v.reciprocal(pinv, psum_))
                    done(v.tensor_scalar(sc, pr, pinv, None, ALU.mult))
                if at == (3, "p1"):
                    hold()
                    done(v.max(top, sc))
                    hold()
                    done(v.max_index(idx, top, sc))
                if at == (3, "t1"):
                    v.tensor_copy(idf, idx)
                    done(v.tensor_reduce(wsum, top[:, 0:TOPK], X, ALU.add))
                    done(v.reciprocal(winv, wsum))
                if at == (3, "solve"):
                    done(v.tensor_scalar(val, top, winv, 0.5, ALU.mult, ALU.mult))
                    done(v.tensor_scalar(acc, iota, idf[:, 0:1], val[:, 0:1], ALU.is_equal, ALU.mult))
                for k, when in enumerate(((3, "keys"), (3, "t2"), (3, "p3")), 1):
                    if at == when:
                        done(v.tensor_scalar(one, iota, idf[:, k:k + 1], val[:, k:k + 1], ALU.is_equal, ALU.mult))
                        if k < TOPK - 1:
                            done(v.tensor_tensor(acc, acc, one, ALU.add))
                        else:
                            v.tensor_tensor(wc[:, t, 0:E], acc, one, ALU.add).then_inc(S["wc_out"], 1)

            for c in range(NC):
                for stage in STAGES:
                    front(0, (c, stage))
            for stage in STAGES:
                prepare(0, 0, stage)
            parts = (inverse, prepare, step, nothing, nothing, front, tail)
            run(0, *parts, first=True)
            run(1, *parts)
            with dve.Fori(2, NB - 1) as b:
                ch.enter(b - 2, DVE_STEPS)
                run(b, *parts)
            ch.leave(NB - 3, DVE_STEPS)
            run(NB - 1, *parts, last=True)
            run(NB, *parts, end=True)

            def experts(b, later):
                che = Chain(dve, s_ech)
                che.base = b * (PAIRS + 1)
                if later:
                    hold()
                che.done(v.tensor_copy(wcb, wc[:, b, :]))
                for p in range(PAIRS):
                    n = b * PAIRS + p
                    h1 = (BA, BB)[p % 2].rearrange("p (e k i) -> p e k i", e=2, k=2)
                    act_ = ea[:, p % 2, :, :]
                    dve.wait_ge(S["h1_tanh"], n + 1)
                    if later or p > 1:
                        dve.wait_ge(S["act_t"], n if p == 0 else n - 1)
                    che.done(v.scalar_tensor_tensor(out=act_[:, 2:4, :], in0=th[:, p % 2, 0:2, :], scalar=1.0, in1=h1[:, :, 0, :],
                                                    op0=ALU.add, op1=ALU.mult))
                    for k in range(2):
                        ins = v.scalar_tensor_tensor(out=act_[:, k, :], in0=act_[:, 2 + k, :], scalar=wcb[:, 2 * p + k:2 * p + k + 1],
                                                     in1=h1[:, k, 1, :], op0=ALU.mult, op1=ALU.mult)
                    ins.then_inc(S["act_out"], 1)
                dve.wait_ge(S["moe_mm"], (b + 1) * PAIRS)
                dve.wait_ge(S["base_in"], (b + 1) * 16)
                if later:
                    dve.wait_ge(S["stored"], b * 16)
                v.tensor_tensor(row[:, 0, :], xin, BT[:, 0:DIM], ALU.add).then_inc(S["fin_out"], 1)

            experts(0, False)
            with dve.Fori(1, NB) as b:
                experts(b, True)

        @block.tensor
        def _(pe):
            mm, tr = nc.tensor.matmul, nc.tensor.transpose

            pe.wait_ge(s_cst, 1)
            pe.wait_ge(S["xn_out"], 1)
            for n in range(NB // 2):
                for k in range(KD):
                    for j in range(2):
                        ins = tr(banks[n][:, (2 * k + j) * P:(2 * k + j + 1) * P], xc[:, 2 * n + j, k * P:(k + 1) * P], ident)
                ins.then_inc(S["xt_t"], 1)
            pe.wait_ge(S["xt_out"], NB // 2)
            for b in range(NB):
                for k in range(KD):
                    ins = mm(BA[:, 2 * NV * b:2 * NV * (b + 1)], xt[:, k, b * P:(b + 1) * P], wab[:, k, :],
                             start=k == 0, stop=k == KD - 1)
            ins.then_inc(S["ab_mm"], 1)
            pe.wait_ge(S["gate_out"], 1)
            gb = beta_tok.rearrange("p k b (g h) -> p k b g h", h=4)
            for c in range(NC):
                for h in range(4):
                    ins = mm(BB[C * h:C * (h + 1), c * P:(c + 1) * P].rearrange("p (k b g) -> p (k b) g", k=2, b=NB),
                             ident[:, C * c:C * (c + 1)], gb[:, :, :, :, h].rearrange("p k b g -> p (k b) g"), start=True, stop=True)
            ins.then_inc(S["ghi_mm"], 1)
            pe.wait_ge(S["ghi_out"], 2)
            gsrc = prm[:, :, 0, :].rearrange("p b (c g) -> p c b g", c=NC)
            for k, w in enumerate((le, gt, rsel[:, 0, :, :].rearrange("p a d -> p (a d)"), rsel[:, 1, :, :].rearrange("p a d -> p (a d)"))):
                for c in range(NC):
                    ins = mm(banks[4 + k][:, c * NB * G:(c + 1) * NB * G].rearrange("p (b g) -> p b g", b=NB), w, gsrc[:, c, :, :],
                             start=True, stop=True)
            ins.then_inc(S["sum_mm"], 1)
            pe.wait_ge(s_w, 96)
            pe.wait_ge(S["sum_exp"], 4)

            def project(bank, first_tile, t):
                for j in range(4):
                    for k in range(KD):
                        m = (first_tile + j) * P
                        ins = mm(bank[:, j * P:(j + 1) * P], wqz[:, k, m:m + P], xt[:, k, bass.ts(t, P)],
                                 start=k == 0, stop=k == KD - 1)
                return ins

            def front(f, at):
                for n in range(4):
                    if at == PROJECT_AT[n]:
                        if n < 2:
                            wait(pe, S["decay_exp"], f)
                            wait(pe, S["params_out"], f)
                            wait(pe, S["htb_in"], f - 2)
                            wait(pe, S["rt_in"], f - 2)
                        else:
                            pe.wait_ge(S["hist_in"], f * 4 + n - 1)
                            if not isinstance(f, int) or f > 1:
                                pe.wait_ge(S["z_out"], (f - 1) * 2 + n - 3)
                        project((BA, BB)[n % 2], 4 * n, f).then_inc(S["proj_mm"], 1)
                if at == (1, "t2"):
                    pe.wait_ge(S["decay_rhs"], f + 1)
                    pe.wait_ge(S["hist_in"], f * 4 + 3)
                    mm(BA, gt, gm.rearrange("p n i -> p (n i)"), start=True, stop=True).then_inc(S["decay_mm"], 1)
                if at == (1, "solve"):
                    pe.wait_ge(S["sq_out"], f + 1)
                    pe.wait_ge(S["hist_in"], f * 4 + 4)
                    for k in range(2 * G):
                        ins = mm(BB[:, 2 * k:2 * k + 2], sqb[:, k, :], parind, start=True, stop=True)
                    ins.then_inc(S["ss_mm"], 1)
                if at == (1, "keys"):
                    pe.wait_ge(S["ss_out"], f + 1)
                    sst = small[:, 5, 0:16].rearrange("p (k g a) -> p k g a", k=2, g=G)
                    for c in range(NC):
                        for h in range(4):
                            ins = mm(BB[C * h:C * (h + 1), 0:32].rearrange("p (k c g) -> p k c g", k=2, c=NC)[:, :, c, :],
                                     ident[:, C * c:C * (c + 1)], sst[:, :, :, h // 2], start=True, stop=True)
                    ins.then_inc(S["hi_mm"], 1)
                if at == (1, "write"):
                    pe.wait_ge(S["qk_in"], f + 1)
                    pe.wait_ge(S["beta_rhs"], f + 1)
                    mm(BB, blk1, gm.rearrange("p n i -> p (n i)"), start=True, stop=True).then_inc(S["beta_mm"], 1)

            def prepare(n, c, stage):
                if stage == "keys":
                    pe.wait_ge(S["keys_in"], n + 1)
                    wait(pe, S["y_out"], n - 2)
                    for g_ in range(G):
                        ins = mm(BQ[:, g_ * 2 * C:(g_ + 1) * 2 * C].rearrange("p (k i) -> p k i", k=2), kbd[:, g_, c, :],
                                 qks[:, c, :, g_, :], start=True, stop=True)
                    ins.then_inc(S["kq_mm"], 1)
                if stage == "turn":
                    pe.wait_ge(S["kq_out"], n + 1)
                    pe.wait_ge(S["values_in"], n + 1)
                    for g_ in range(G):
                        ins = tr(tiles(BQ)[:, g_, :], vbd[:, g_, c, :], ident)
                    ins.then_inc(S["vx_t"], 1)
                if stage == "first":
                    pe.wait_ge(S["first_out"], n + 1)
                    wait(pe, S["t_out"], n * (LI - 2))
                    wait(pe, S["w_out"], n - 1)
                    for g_ in range(G):
                        ins = tr(tiles(BT)[:, g_, :], tt[:, c % 2, g_, :], ident)
                    ins.then_inc(S["first_t"], 1)
                if stage == "lay":
                    wait(pe, S["o_out"], n - 1)
                    for g_ in range(G):
                        ins = tr(tiles(BO)[:, g_, :], kbd[:, g_, c, :], ident)
                    ins.then_inc(S["kh_t"], 1)

            def inverse(n, c, stage):
                if stage == "read":
                    wait(pe, S["s_out"], n)
                    for g_ in range(G):
                        ins = mm(tiles(BS)[:, g_, :], kbd[:, g_, c, :], state[:, g_, :], start=True, stop=True)
                    ins.then_inc(S["ks_mm"], 1)
                if stage in ("p1", "p2", "p3"):
                    l = int(stage[1])
                    pe.wait_ge(S["mask_out"], n * LI + l + 1)
                    if l == 1:
                        pe.wait_ge(S["first_in"], n + 1)
                        wait(pe, S["p_out"], n * (LI - 1))
                    else:
                        pe.wait_ge(S["t_out"], n * (LI - 2) + l - 1)
                        pe.wait_ge(S["p_out"], n * (LI - 1) + l - 1)
                    for g_ in range(G):
                        ins = mm(tiles(BP)[:, g_, :], am[:, l, g_, :], tn[:, g_, :], start=True, stop=True)
                    ins.then_inc(S["p_mm"], 1)
                if stage in ("t1", "t2", "t3"):
                    l = int(stage[1])
                    pe.wait_ge(S["p_out"], n * (LI - 1) + l)
                    if l == 1:
                        wait(pe, S["tt_out"], n * (LI - 1))
                    else:
                        pe.wait_ge(S["tt_out"], n * (LI - 1) + l - 1)
                    if l < LI - 1:
                        for g_ in range(G):
                            ins = mm(tiles(BT)[:, g_, :], tt[:, c % 2, g_, :], pp[:, g_, :], start=True, stop=True)
                        ins.then_inc(S["t_mm"], 1)
                    for g_ in range(G):
                        ins = mm(tiles(BTT)[:, g_, :], pp[:, g_, :], tt[:, c % 2, g_, :], start=True, stop=True)
                    ins.then_inc(S["tt_mm"], 1)

            def step(b, n, c, stage):
                if stage == "query":
                    pe.wait_ge(S["queries_in"], n + 1)
                    pe.wait_ge(S["kh_out"], n + 2 if not isinstance(n, int) or n + 2 <= NB * NC else NB * NC)
                    wait(pe, S["o_out"], n)
                    for g_ in range(G):
                        ins = mm(tiles(BO)[:, g_, :], qbd[:, g_, c, :], state[:, g_, :], start=True, stop=True)
                    ins.then_inc(S["qs_mm"], 1)
                if stage == "solve":
                    pe.wait_ge(S["rhs_out"], n + 1)
                    pe.wait_ge(S["tt_out"], (n + 1) * (LI - 1))
                    for g_ in range(G):
                        ins = mm(tiles(BS)[:, g_, :], tt[:, c % 2, g_, :], rhs[:, g_, :], start=True, stop=True)
                    ins.then_inc(S["v_mm"], 1)
                if stage == "weigh":
                    pe.wait_ge(S["v_out"], n + 1)
                    pe.wait_ge(S["last_mask_out"], n + 1)
                    pe.wait_ge(S["t_out"], (n + 2) * (LI - 2) if not isinstance(n, int) or n + 2 <= NB * NC else NB * NC * (LI - 2))
                    for g_ in range(G):
                        ins = mm(tiles(BT)[:, g_, :], am[:, LI, g_, :], uu[:, g_, :], start=True, stop=True)
                    ins.then_inc(S["w_mm"], 1)
                if stage == "settle":
                    pe.wait_ge(S["w_out"], n + 1)
                    for g_ in range(G):
                        ins = mm(tiles(BS)[:, g_, :], tt[:, c % 2, g_, :], rhs[:, g_, :], start=True, stop=True)
                    ins.then_inc(S["u_mm"], 1)
                if stage == "write":
                    pe.wait_ge(S["u_out"], n + 1)
                    pe.wait_ge(S["qmask_out"], n + 1)
                    pe.wait_ge(S["qs_used"], n + 1)
                    for g_ in range(G):
                        ins = mm(tiles(BO)[:, g_, :], aq[:, c % 2, g_, :], uu[:, g_, :], start=True, stop=True)
                    ins.then_inc(S["au_mm"], 1)
                if stage == "grow":
                    pe.wait_ge(S["up_out"], n + 1)
                    pe.wait_ge(S["kh_out"], n + 1)
                    for g_ in range(G):
                        ins = mm(tiles(BS)[:, g_, :], kh[:, c % 2, g_, :], up[:, g_, :], start=True, stop=True)
                    ins.then_inc(S["ku_mm"], 1)
            def late(b, n, c, stage):
                if stage == "t1":
                    pe.wait_ge(S["osel_out"], n + 1)
                    pe.wait_ge(S["vx_out"], n + 3 if not isinstance(n, int) or n + 3 <= NC * NB else NC * NB)
                    for g_ in range(G):
                        ins = mm(BQ[:, 2 * C * g_:2 * C * (g_ + 1)], oo[:, c % 2, g_, :], osel[:, g_, :], start=True, stop=True)
                    ins.then_inc(S["y_mm"], 1)

            def tail(t, at):
                for n, when in enumerate(((0, "t2"), (0, "p3"))):
                    if at == when:
                        if not isinstance(t, int) or t < NB - 1:
                            pe.wait_ge(S["hist_in"], (t + 2) * 4 + 1 + n if not isinstance(t, int) or t < NB - 2 else NB * 4)
                        built = NB if isinstance(t, int) and t == NB - 1 else t + 2
                        pe.wait_ge(S["decay_exp"], built)
                        pe.wait_ge(S["params_out"], built)
                        wait(pe, S["htb_in"], t)
                        wait(pe, S["rt_in"], t)
                        project((BA, BB)[n], CT + 4 * n, t).then_inc(S["z_mm"], 1)
                if at == (1, "t3"):
                    pe.wait_ge(S["yt_out"], 2 * t + 2)
                    pe.wait_ge(S["z_out"], 2 * t + 1)
                    if not isinstance(t, int) or t < NB - 2:
                        pe.wait_ge(S["decay_exp"], t + 3)
                    for u in range(UT):
                        ins = mm(BA[:, 0:DIM], yt[:, u, :], wo[:, u, :], start=u == 0, stop=u == UT - 1)
                    ins.then_inc(S["op_mm"], 1)
                if at == (2, "t2"):
                    pe.wait_ge(S["h_out"], t + 1)
                    pe.wait_ge(S["x2_out"], t + 1)
                    for k in range(KD):
                        ins = tr(BA[:, k * P:(k + 1) * P], row[:, 2, k * P:(k + 1) * P], ident)
                    ins.then_inc(S["h_t"], 1)
                if at == (2, "p3"):
                    pe.wait_ge(S["htb_in"], t + 1)
                    pe.wait_ge(S["z_out"], 2 * t + 2)
                    if not isinstance(t, int) or t < NB - 2:
                        pe.wait_ge(S["params_out"], t + 3)
                    for k in range(KD):
                        ins = mm(BB[:, 0:E], htb[:, k, :], wr[:, k, :], start=k == 0, stop=k == KD - 1)
                    ins.then_inc(S["rt_mm"], 1)

            run_all(pe, inverse, prepare, step, late, nothing, front, tail)

            pairs = arena.rearrange("p (n w) -> p n w", n=PAIRS)
            w1v = pairs[:, :, 0:UP].rearrange("p n (k e j) -> p k n e j", k=KD, e=2)
            w2v = pairs[:, :, UP:PAIR].rearrange("p n (e d) -> p n e d", e=2)
            pe.wait_ge(S["wc_out"], NB)

            def up_products(b, p, later):
                n = b * PAIRS + p
                for j in range(3):
                    if not later and p == parts[j][0]:
                        pe.wait_ge(s_ew[j], 16)
                if later or p > 1:
                    pe.wait_ge(S["act_out"], n if p == 0 else n - 1)
                for k in range(2):
                    for d in range(KD):
                        ins = mm((BA, BB)[p % 2][:, k * 2 * I:(k + 1) * 2 * I], htb[:, d, :], w1v[:, d, p, k, :],
                                 start=d == 0, stop=d == KD - 1)
                ins.then_inc(S["h1_mm"], 1)

            def down_products(b, p, later):
                n = b * PAIRS + p
                pe.wait_ge(S["act_out"], n + 1)
                if later or p > 1:
                    pe.wait_ge(S["act_in"], n if p == 0 else n - 1)
                for k in range(2):
                    ins = tr((BQ, BP)[p % 2][:, k * P:(k + 1) * P], ea[:, p % 2, k, :], ident)
                ins.then_inc(S["act_t"], 1)

            def sum_products(b, p, later):
                n = b * PAIRS + p
                pe.wait_ge(S["act_in"], n + 1)
                if later and p == 0:
                    pe.wait_ge(S["fin_out"], b)
                for k in range(2):
                    ins = mm(BT[:, 0:DIM], eat[:, p % 2, k, :], w2v[:, p, k, :], start=p == 0 and k == 0,
                             stop=p == PAIRS - 1 and k == 1)
                ins.then_inc(S["moe_mm"], 1)

            def experts(b, later):
                pe.wait_ge(S["hb_in"], b + 1)
                up_products(b, 0, later)
                for p in range(PAIRS):
                    if p + 1 < PAIRS:
                        up_products(b, p + 1, later)
                    down_products(b, p, later)
                    if p > 0:
                        sum_products(b, p - 1, later)
                sum_products(b, PAIRS - 1, later)

            experts(0, False)
            with pe.Fori(1, NB) as b:
                experts(b, True)

def kernel(L0_attn_x, L0_attn_W_qkv, L0_attn_W_z, L0_attn_W_b, L0_attn_W_a, L0_attn_W_out, L0_attn_conv_w, L0_attn_dt_bias,
           L0_attn_A_log, L0_attn_norm_weight, L0_ffn_norm_w, L0_ffn_router_w, L0_ffn_w1, L0_ffn_w2, L0_ffn_sg, L0_ffn_su, L0_ffn_sd):
    import numpy as np
    import concourse.bacc as bacc
    from concourse.bass_utils import run_bass_kernel_spmd

    def ktiles(w):
        w = np.asarray(w)
        return np.ascontiguousarray(w.reshape(w.shape[0] // P, P, w.shape[1]).transpose(1, 0, 2))

    def rows(w):
        w = np.asarray(w).reshape(-1)
        return np.ascontiguousarray(np.broadcast_to(w, (P, w.shape[0])))

    sg, su, sd = (np.asarray(w) for w in (L0_ffn_sg, L0_ffn_su, L0_ffn_sd))
    shared_in = np.stack([np.concatenate([sg[:, j * I:(j + 1) * I], su[:, j * I:(j + 1) * I]], 1) for j in range(EV - E)])
    w1 = np.concatenate([np.asarray(L0_ffn_w1), shared_in])
    w2 = np.concatenate([np.asarray(L0_ffn_w2), sd.reshape(EV - E, I, DIM)])
    arrays = {
        "x": np.asarray(L0_attn_x).reshape(T, DIM),
        "w_qkvz": ktiles(np.concatenate([np.asarray(L0_attn_W_qkv), np.asarray(L0_attn_W_z)]).T),
        "w_ab": ktiles(np.concatenate([np.asarray(L0_attn_W_b), np.asarray(L0_attn_W_a)]).T),
        "w_out": ktiles(np.asarray(L0_attn_W_out).T),
        "conv_w": ktiles(np.asarray(L0_attn_conv_w).reshape(CT * P, TAPS)),
        "dt_bias": rows(L0_attn_dt_bias),
        "a_log": rows(L0_attn_A_log),
        "head_w": np.ascontiguousarray(np.tile(np.asarray(L0_attn_norm_weight), 2).reshape(P, 1)),
        "ffn_w": rows(L0_ffn_norm_w),
        "w_router": ktiles(np.asarray(L0_ffn_router_w).T),
        "w12": np.ascontiguousarray(np.concatenate([
            w1.reshape(PAIRS, 2, KD, P, 2 * I).transpose(3, 0, 2, 1, 4).reshape(P, PAIRS, -1),
            w2.reshape(PAIRS, 2, I, DIM).transpose(2, 0, 1, 3).reshape(P, PAIRS, -1)], 2).reshape(P, -1)),
    }
    nc = bacc.Bacc("TRN2", target_bir_lowering=False, num_devices=1)
    aps = [nc.dram_tensor(f"in_{n}", a.shape, F32, kind="ExternalInput").ap() for n, a in arrays.items()]
    out = nc.dram_tensor("out", (T, DIM), F32, kind="ExternalOutput").ap()
    gated_delta_moe(nc, *aps, out)
    r = run_bass_kernel_spmd(nc, [{f"in_{n}": a for n, a in arrays.items()}], core_ids=[0])
    return r.results[0]["out"].reshape(1, T, DIM)
```
